# Optimizing a Trainium2 kernel written in Bass

```python
import numpy as np
import jax
import jax.numpy as jnp

def _softmax(x, axis=-1):
    return jax.nn.softmax(x, axis=axis)

def _gelu(x):
    return jax.nn.gelu(x, approximate=True)

def _silu(x):
    return jax.nn.silu(x)

def _sigmoid(x):
    return jax.nn.sigmoid(x)

def _layernorm(x, axis=-1, eps=1e-05):
    m = jnp.mean(x, axis=axis, keepdims=True)
    v = jnp.var(x, axis=axis, keepdims=True)
    return (x - m) / jnp.sqrt(v + eps)

def _scatter_add(tgt, idx, src, axis=0):
    return tgt.at[idx].add(src)

def _segment_sum(src, seg, n):
    return jax.ops.segment_sum(src, seg, n)
kernel_name = 'mk_hybrid_d2_jaxref_r8_8c9f8e'

def setup_inputs(seed: int=0):
    np.random.seed(seed)
    _w = jnp.asarray

    def _L0_attn_a_setup():
        import jax, jax.numpy as jnp
        import numpy as np
        D_MODEL = 256
        N_HEADS = 16
        HEAD_DIM = D_MODEL // N_HEADS
        B, T = (2, 256)
        key = jax.random.key(seed)
        ks = jax.random.split(key, 9)
        s = 0.02
        x = jax.random.normal(ks[0], (B, T, D_MODEL), dtype=jnp.float32)
        Wq = jax.random.normal(ks[1], (N_HEADS, D_MODEL, HEAD_DIM), dtype=jnp.float32) * s
        bq = jax.random.normal(ks[2], (N_HEADS, HEAD_DIM), dtype=jnp.float32) * s
        Wk = jax.random.normal(ks[3], (N_HEADS, D_MODEL, HEAD_DIM), dtype=jnp.float32) * s
        bk = jax.random.normal(ks[4], (N_HEADS, HEAD_DIM), dtype=jnp.float32) * s
        Wv = jax.random.normal(ks[5], (N_HEADS, D_MODEL, HEAD_DIM), dtype=jnp.float32) * s
        bv = jax.random.normal(ks[6], (N_HEADS, HEAD_DIM), dtype=jnp.float32) * s
        Wo = jax.random.normal(ks[7], (D_MODEL, D_MODEL), dtype=jnp.float32) * s
        bo = jax.random.normal(ks[8], (D_MODEL,), dtype=jnp.float32) * s
        return {'x': x, 'Wq': Wq, 'bq': bq, 'Wk': Wk, 'bk': bk, 'Wv': Wv, 'bv': bv, 'Wo': Wo, 'bo': bo}
    _L0_attn_a_in = _L0_attn_a_setup()

    def _L0_attn_b_setup():
        import math
        import jax, jax.numpy as jnp
        import numpy as np
        H, D = (16, 128)
        INNER = H * D
        QUERY_DIM = 256
        EPS = 1e-06
        NUM_SEQ_SHIFTS = 16
        MAX_SEQ_LEN = 256
        CHANNEL_SHIFTS = [1, 2, 4, 8]

        def compute_seq_shifts(num_shifts, max_len=256):
            if num_shifts <= 1:
                return [0]
            half = (num_shifts - 1 + 1) // 2
            max_s = max(max_len // 2, 2)
            if half <= 1:
                positive = [1]
            else:
                positive = sorted(set((max(1, round(math.exp(math.log(max_s) * i / (half - 1)))) for i in range(half))))
                while len(positive) < half:
                    new_vals = []
                    for i in range(len(positive) - 1):
                        mid = (positive[i] + positive[i + 1]) // 2
                        if mid not in positive and mid not in new_vals:
                            new_vals.append(mid)
                        if len(positive) + len(new_vals) >= half:
                            break
                    if not new_vals:
                        v = positive[-1] + 1
                        while len(positive) + len(new_vals) < half and v <= max_s:
                            new_vals.append(v)
                            v += 1
                    positive = sorted(set(positive + new_vals))[:half]
            shifts = [0]
            for s in positive:
                shifts.append(s)
                shifts.append(-s)
            return shifts[:num_shifts]
        SEQ_SHIFTS = compute_seq_shifts(NUM_SEQ_SHIFTS, MAX_SEQ_LEN)

        def _rmsnorm(x, g, eps=EPS):
            return x * jax.lax.rsqrt(jnp.mean(x * x, axis=-1, keepdims=True) + eps) * g
        key = jax.random.key(seed)
        ks = jax.random.split(key, 12)
        s = 0.02
        return {'x': jax.random.normal(ks[0], (2, 256, QUERY_DIM), dtype=jnp.float32), 'wq': jax.random.normal(ks[1], (INNER, QUERY_DIM), dtype=jnp.float32) * s, 'bq': jnp.zeros((INNER,), jnp.float32), 'wk': jax.random.normal(ks[2], (INNER, QUERY_DIM), dtype=jnp.float32) * s, 'bk': jnp.zeros((INNER,), jnp.float32), 'wv': jax.random.normal(ks[3], (INNER, QUERY_DIM), dtype=jnp.float32) * s, 'bv': jnp.zeros((INNER,), jnp.float32), 'gq': jnp.ones((INNER,), jnp.float32), 'gk': jnp.ones((INNER,), jnp.float32), 'w_mix': jax.random.normal(ks[4], (1, 1 + len(CHANNEL_SHIFTS)), dtype=jnp.float32) * 0.4, 'wo': jax.random.normal(ks[5], (QUERY_DIM, INNER), dtype=jnp.float32) * s, 'bo': jnp.zeros((QUERY_DIM,), jnp.float32)}
    _L0_attn_b_in = _L0_attn_b_setup()

    def _L0_ffn_setup():
        import jax, jax.numpy as jnp
        import numpy as np
        TOP_K = 6
        CAP_FACTOR = 2

        def _moe_block(x2d, wg_router, w_gate, w_up, w_down, ws_gate, ws_up, ws_down):
            T, D = x2d.shape
            E = wg_router.shape[0]
            scores = jax.nn.softmax(x2d @ wg_router.T, axis=-1)
            topk_w, topk_idx = jax.lax.top_k(scores, TOP_K)
            topk_w = topk_w / (jnp.sum(topk_w, axis=-1, keepdims=True) + 1e-20)
            flat_idx = topk_idx.reshape(-1)
            oh = jax.nn.one_hot(flat_idx, E, dtype=jnp.int32)
            pos = jnp.cumsum(oh, axis=0) - 1
            pos_in_e = jnp.take_along_axis(pos, flat_idx[:, None], axis=1)[:, 0]
            C = CAP_FACTOR * (T * TOP_K // E)
            valid = pos_in_e < C
            safe_pos = jnp.where(valid, pos_in_e, 0)
            tok_id = jnp.repeat(jnp.arange(T), TOP_K)
            vmask = valid[:, None].astype(x2d.dtype)
            x_rep = x2d[tok_id] * vmask
            xe = jnp.zeros((E, C, D), x2d.dtype).at[flat_idx, safe_pos].add(x_rep)
            g = jnp.einsum('ecd,edf->ecf', xe, w_gate)
            u = jnp.einsum('ecd,edf->ecf', xe, w_up)
            ye = jnp.einsum('ecf,efd->ecd', jax.nn.silu(g) * u, w_down)
            y_tok = ye[flat_idx, safe_pos] * vmask
            y = jnp.sum(y_tok.reshape(T, TOP_K, D) * topk_w[..., None], axis=1)
            sh = jax.nn.silu(x2d @ ws_gate) * (x2d @ ws_up) @ ws_down
            return y + sh
        key = jax.random.key(seed)
        ks = jax.random.split(key, 9)
        B, S, D, F, E = (1, 256, 256, 176, 32)
        FS = F * 2
        s = 0.02
        return {'hidden_states': jax.random.normal(ks[0], (B, S, D), jnp.float32), 'wg_router': jax.random.normal(ks[1], (E, D), jnp.float32) * s, 'w_gate': jax.random.normal(ks[2], (E, D, F), jnp.float32) * s, 'w_up': jax.random.normal(ks[3], (E, D, F), jnp.float32) * s, 'w_down': jax.random.normal(ks[4], (E, F, D), jnp.float32) * s, 'ws_gate': jax.random.normal(ks[5], (D, FS), jnp.float32) * s, 'ws_up': jax.random.normal(ks[6], (D, FS), jnp.float32) * s, 'ws_down': jax.random.normal(ks[7], (FS, D), jnp.float32) * s}
    _L0_ffn_in = _L0_ffn_setup()

    def _L1_attn_a_setup():
        import jax, jax.numpy as jnp
        import numpy as np
        E = 256
        H = 16
        D = E // H
        B = 4
        N = 256
        key = jax.random.key(seed)
        ks = jax.random.split(key, 5)
        scale_qkv = 1.0 / np.sqrt(E)
        scale_fc = 1.0 / np.sqrt(E)
        return {'x': jax.random.normal(ks[0], (B, N, E), dtype=jnp.float32), 'w_qkv': jax.random.uniform(ks[1], (E, E + 2 * D), jnp.float32, -scale_qkv, scale_qkv), 'b_qkv': jax.random.uniform(ks[2], (E + 2 * D,), jnp.float32, -scale_qkv, scale_qkv), 'w_fc': jax.random.uniform(ks[3], (E, E), jnp.float32, -scale_fc, scale_fc), 'b_fc': jax.random.uniform(ks[4], (E,), jnp.float32, -scale_fc, scale_fc)}
    _L1_attn_a_in = _L1_attn_a_setup()

    def _L1_attn_b_setup():
        import jax, jax.numpy as jnp
        import numpy as np
        import math
        H = 16
        KV = 8
        D = 128
        HID = 256
        LAYER_IDX = 1
        LAMBDA_INIT = 0.8 - 0.6 * math.exp(-0.3 * LAYER_IDX)
        EPS = 1e-05
        key = jax.random.key(seed)
        ks = jax.random.split(key, 8)
        B, S = (2, 256)
        op_size = H * D + 2 * KV * D
        return {'hidden_states': jax.random.normal(ks[0], (B, S, HID), jnp.float32), 'Wqkv_w': jax.random.normal(ks[1], (op_size, HID), jnp.float32) * 0.02, 'Wqkv_b': jnp.zeros((op_size,), jnp.float32), 'lambda_q1': jax.random.normal(ks[2], (D,), jnp.float32) * 0.1, 'lambda_k1': jax.random.normal(ks[3], (D,), jnp.float32) * 0.1, 'lambda_q2': jax.random.normal(ks[4], (D,), jnp.float32) * 0.1, 'lambda_k2': jax.random.normal(ks[5], (D,), jnp.float32) * 0.1, 'subln_w': jnp.ones((2 * D,), jnp.float32), 'out_w': jax.random.normal(ks[6], (HID, H * D), jnp.float32) * 0.02, 'out_b': jnp.zeros((HID,), jnp.float32)}
    _L1_attn_b_in = _L1_attn_b_setup()

    def _L1_ffn_setup():
        import jax, jax.numpy as jnp
        import numpy as np
        B, S, H = (4, 128, 256)
        NH = 16
        HD = H // NH
        RD = HD // 2
        LAT = H // 4
        I = 128
        NE = 8
        NSH = 1
        NR = NE - NSH
        TOPK = 2
        EPS = 1e-05
        SCALING = 8.0

        def _w(key, shape, fan_in):
            return jax.random.normal(key, shape, dtype=jnp.float32) / np.sqrt(fan_in)

        def rmsnorm(x, w):
            rms = jax.lax.rsqrt(jnp.mean(x * x, axis=-1, keepdims=True) + EPS)
            return w * rms * x

        def rope_cos_sin(seq_len):
            inv_freq = 1.0 / 10000.0 ** (jnp.arange(0, RD, 2, dtype=jnp.float32) / RD)
            t = jnp.arange(seq_len, dtype=jnp.float32)
            ang = jnp.outer(t, inv_freq)
            emb = jnp.concatenate([ang, ang], axis=-1)
            return (jnp.cos(emb), jnp.sin(emb))

        def apply_rope(x, cos, sin):
            c = cos[None, :, None, :]
            s = sin[None, :, None, :]
            x1, x2 = jnp.split(x, 2, axis=-1)
            rot = jnp.concatenate([-x2, x1], axis=-1)
            return x * c + rot * s

        def expert_ffn(x, wg, wu, wd):
            h = jax.nn.silu(x @ wg) * (x @ wu) / SCALING
            return h @ wd

        def attention(x, kv_d_w, q_d_w, k_u_w, v_u_w, q_u_w, rope_k_w, rope_q_w, o_w):
            b, s, _ = x.shape
            kv_d = x @ kv_d_w
            q_d = x @ q_d_w
            k_p = (kv_d @ k_u_w).reshape(b, s, NH, RD)
            q_p = (q_d @ q_u_w).reshape(b, s, NH, RD)
            v = (kv_d @ v_u_w).reshape(b, s, NH, HD)
            k_r = (x @ rope_k_w).reshape(b, s, NH, RD)
            q_r = (q_d @ rope_q_w).reshape(b, s, NH, RD)
            cos, sin = rope_cos_sin(s)
            k_r = apply_rope(k_r, cos, sin)
            q_r = apply_rope(q_r, cos, sin)
            k = jnp.concatenate([k_p, k_r], axis=-1)
            q = jnp.concatenate([q_p, q_r], axis=-1)
            scale = 1.0 / np.sqrt(HD)
            scores = jnp.einsum('bqhd,bkhd->bhqk', q, k) * scale
            causal = jnp.tril(jnp.ones((s, s), dtype=bool))
            scores = jnp.where(causal[None, None], scores, jnp.finfo(scores.dtype).min)
            probs = jax.nn.softmax(scores, axis=-1)
            out = jnp.einsum('bhqk,bkhd->bqhd', probs, v).reshape(b, s, H)
            return out @ o_w

        def moe(x, sh_gate, sh_up, sh_down, r_gate, r_up, r_down, router_w, router_b):
            shared = expert_ffn(x, sh_gate, sh_up, sh_down)
            logits = x @ router_w + router_b
            probs = jax.nn.sigmoid(logits)
            scores, idx = jax.lax.top_k(probs, TOPK)
            scores = scores / jnp.sum(scores, axis=-1, keepdims=True)
            w = jnp.sum(jax.nn.one_hot(idx, NR, dtype=x.dtype) * scores[..., None], axis=-2)
            combined = jnp.zeros_like(x)
            for e in range(NR):
                combined = combined + w[..., e:e + 1] * expert_ffn(x, r_gate[e], r_up[e], r_down[e])
            return shared + combined
        key = jax.random.key(seed)
        ks = jax.random.split(key, 24)
        return {'x': jax.random.normal(ks[0], (B, S, H), dtype=jnp.float32), 'ln1_w': jnp.ones((H,), jnp.float32), 'ln2_w': jnp.ones((H,), jnp.float32), 'kv_d_w': _w(ks[1], (H, LAT), H), 'q_d_w': _w(ks[2], (H, LAT), H), 'k_u_w': _w(ks[3], (LAT, H // 2), LAT), 'v_u_w': _w(ks[4], (LAT, H), LAT), 'q_u_w': _w(ks[5], (LAT, H // 2), LAT), 'rope_k_w': _w(ks[6], (H, H // 2), H), 'rope_q_w': _w(ks[7], (LAT, H // 2), LAT), 'o_w': _w(ks[8], (H, H), H), 'sh_gate': _w(ks[9], (H, I), H), 'sh_up': _w(ks[10], (H, I), H), 'sh_down': _w(ks[11], (I, H), I), 'r_gate': _w(ks[12], (NR, H, I), H), 'r_up': _w(ks[13], (NR, H, I), H), 'r_down': _w(ks[14], (NR, I, H), I), 'router_w': _w(ks[15], (H, NR), H), 'router_b': jnp.zeros((NR,), jnp.float32)}
    _L1_ffn_in = _L1_ffn_setup()
    _d = {'L0_attn_a_x': _L0_attn_a_in['x'], 'L0_attn_a_Wq': _L0_attn_a_in['Wq'], 'L0_attn_a_bq': _L0_attn_a_in['bq'], 'L0_attn_a_Wk': _L0_attn_a_in['Wk'], 'L0_attn_a_bk': _L0_attn_a_in['bk'], 'L0_attn_a_Wv': _L0_attn_a_in['Wv'], 'L0_attn_a_bv': _L0_attn_a_in['bv'], 'L0_attn_a_Wo': _L0_attn_a_in['Wo'], 'L0_attn_a_bo': _L0_attn_a_in['bo'], 'L0_attn_b_wq': _L0_attn_b_in['wq'], 'L0_attn_b_bq': _L0_attn_b_in['bq'], 'L0_attn_b_wk': _L0_attn_b_in['wk'], 'L0_attn_b_bk': _L0_attn_b_in['bk'], 'L0_attn_b_wv': _L0_attn_b_in['wv'], 'L0_attn_b_bv': _L0_attn_b_in['bv'], 'L0_attn_b_gq': _L0_attn_b_in['gq'], 'L0_attn_b_gk': _L0_attn_b_in['gk'], 'L0_attn_b_w_mix': _L0_attn_b_in['w_mix'], 'L0_attn_b_wo': _L0_attn_b_in['wo'], 'L0_attn_b_bo': _L0_attn_b_in['bo'], 'L0_ffn_wg_router': _L0_ffn_in['wg_router'], 'L0_ffn_w_gate': _L0_ffn_in['w_gate'], 'L0_ffn_w_up': _L0_ffn_in['w_up'], 'L0_ffn_w_down': _L0_ffn_in['w_down'], 'L0_ffn_ws_gate': _L0_ffn_in['ws_gate'], 'L0_ffn_ws_up': _L0_ffn_in['ws_up'], 'L0_ffn_ws_down': _L0_ffn_in['ws_down'], 'L1_attn_a_w_qkv': _L1_attn_a_in['w_qkv'], 'L1_attn_a_b_qkv': _L1_attn_a_in['b_qkv'], 'L1_attn_a_w_fc': _L1_attn_a_in['w_fc'], 'L1_attn_a_b_fc': _L1_attn_a_in['b_fc'], 'L1_attn_b_Wqkv_w': _L1_attn_b_in['Wqkv_w'], 'L1_attn_b_Wqkv_b': _L1_attn_b_in['Wqkv_b'], 'L1_attn_b_lambda_q1': _L1_attn_b_in['lambda_q1'], 'L1_attn_b_lambda_k1': _L1_attn_b_in['lambda_k1'], 'L1_attn_b_lambda_q2': _L1_attn_b_in['lambda_q2'], 'L1_attn_b_lambda_k2': _L1_attn_b_in['lambda_k2'], 'L1_attn_b_subln_w': _L1_attn_b_in['subln_w'], 'L1_attn_b_out_w': _L1_attn_b_in['out_w'], 'L1_attn_b_out_b': _L1_attn_b_in['out_b'], 'L1_ffn_ln1_w': _L1_ffn_in['ln1_w'], 'L1_ffn_ln2_w': _L1_ffn_in['ln2_w'], 'L1_ffn_kv_d_w': _L1_ffn_in['kv_d_w'], 'L1_ffn_q_d_w': _L1_ffn_in['q_d_w'], 'L1_ffn_k_u_w': _L1_ffn_in['k_u_w'], 'L1_ffn_v_u_w': _L1_ffn_in['v_u_w'], 'L1_ffn_q_u_w': _L1_ffn_in['q_u_w'], 'L1_ffn_rope_k_w': _L1_ffn_in['rope_k_w'], 'L1_ffn_rope_q_w': _L1_ffn_in['rope_q_w'], 'L1_ffn_o_w': _L1_ffn_in['o_w'], 'L1_ffn_sh_gate': _L1_ffn_in['sh_gate'], 'L1_ffn_sh_up': _L1_ffn_in['sh_up'], 'L1_ffn_sh_down': _L1_ffn_in['sh_down'], 'L1_ffn_r_gate': _L1_ffn_in['r_gate'], 'L1_ffn_r_up': _L1_ffn_in['r_up'], 'L1_ffn_r_down': _L1_ffn_in['r_down'], 'L1_ffn_router_w': _L1_ffn_in['router_w'], 'L1_ffn_router_b': _L1_ffn_in['router_b']}
    _x0 = _d['L0_attn_a_x']
    _d['L0_attn_a_x'] = jax.random.normal(jax.random.fold_in(jax.random.key(seed), 1), (1, 1024, 256), dtype=_x0.dtype)
    del _x0
    return _d

def reference(L0_attn_a_x, L0_attn_a_Wq, L0_attn_a_bq, L0_attn_a_Wk, L0_attn_a_bk, L0_attn_a_Wv, L0_attn_a_bv, L0_attn_a_Wo, L0_attn_a_bo, L0_attn_b_wq, L0_attn_b_bq, L0_attn_b_wk, L0_attn_b_bk, L0_attn_b_wv, L0_attn_b_bv, L0_attn_b_gq, L0_attn_b_gk, L0_attn_b_w_mix, L0_attn_b_wo, L0_attn_b_bo, L0_ffn_wg_router, L0_ffn_w_gate, L0_ffn_w_up, L0_ffn_w_down, L0_ffn_ws_gate, L0_ffn_ws_up, L0_ffn_ws_down, L1_attn_a_w_qkv, L1_attn_a_b_qkv, L1_attn_a_w_fc, L1_attn_a_b_fc, L1_attn_b_Wqkv_w, L1_attn_b_Wqkv_b, L1_attn_b_lambda_q1, L1_attn_b_lambda_k1, L1_attn_b_lambda_q2, L1_attn_b_lambda_k2, L1_attn_b_subln_w, L1_attn_b_out_w, L1_attn_b_out_b, L1_ffn_ln1_w, L1_ffn_ln2_w, L1_ffn_kv_d_w, L1_ffn_q_d_w, L1_ffn_k_u_w, L1_ffn_v_u_w, L1_ffn_q_u_w, L1_ffn_rope_k_w, L1_ffn_rope_q_w, L1_ffn_o_w, L1_ffn_sh_gate, L1_ffn_sh_up, L1_ffn_sh_down, L1_ffn_r_gate, L1_ffn_r_up, L1_ffn_r_down, L1_ffn_router_w, L1_ffn_router_b):

    def _L0_attn_a_ref(x, Wq, bq, Wk, bk, Wv, bv, Wo, bo):
        import jax, jax.numpy as jnp
        import numpy as np
        D_MODEL = 256
        N_HEADS = 16
        HEAD_DIM = D_MODEL // N_HEADS
        B, T = (2, 256)
        Bn, Tn, C = x.shape
        H, _, D = Wq.shape
        scale = D ** (-0.5)
        q = jnp.einsum('btc,hcd->bhtd', x, Wq) + bq[None, :, None, :]
        k = jnp.einsum('btc,hcd->bhtd', x, Wk) + bk[None, :, None, :]
        v = jnp.einsum('btc,hcd->bhtd', x, Wv) + bv[None, :, None, :]
        scores = jnp.einsum('bhtd,bhsd->bhts', q, k) * scale
        neg = jnp.finfo(scores.dtype).min
        causal = jnp.triu(jnp.full((Tn, Tn), neg, dtype=scores.dtype), k=1)
        probs = jax.nn.softmax(scores + causal, axis=-1)
        y = jnp.einsum('bhts,bhsd->bhtd', probs, v)
        y = y.transpose(0, 2, 1, 3).reshape(Bn, Tn, H * D)
        return y @ Wo + bo

    def _L0_attn_b_ref(x, wq, bq, wk, bk, wv, bv, gq, gk, w_mix, wo, bo):
        import math
        import jax, jax.numpy as jnp
        import numpy as np
        H, D = (16, 128)
        INNER = H * D
        QUERY_DIM = 256
        EPS = 1e-06
        NUM_SEQ_SHIFTS = 16
        MAX_SEQ_LEN = 256
        CHANNEL_SHIFTS = [1, 2, 4, 8]

        def compute_seq_shifts(num_shifts, max_len=256):
            if num_shifts <= 1:
                return [0]
            half = (num_shifts - 1 + 1) // 2
            max_s = max(max_len // 2, 2)
            if half <= 1:
                positive = [1]
            else:
                positive = sorted(set((max(1, round(math.exp(math.log(max_s) * i / (half - 1)))) for i in range(half))))
                while len(positive) < half:
                    new_vals = []
                    for i in range(len(positive) - 1):
                        mid = (positive[i] + positive[i + 1]) // 2
                        if mid not in positive and mid not in new_vals:
                            new_vals.append(mid)
                        if len(positive) + len(new_vals) >= half:
                            break
                    if not new_vals:
                        v = positive[-1] + 1
                        while len(positive) + len(new_vals) < half and v <= max_s:
                            new_vals.append(v)
                            v += 1
                    positive = sorted(set(positive + new_vals))[:half]
            shifts = [0]
            for s in positive:
                shifts.append(s)
                shifts.append(-s)
            return shifts[:num_shifts]
        SEQ_SHIFTS = compute_seq_shifts(NUM_SEQ_SHIFTS, MAX_SEQ_LEN)

        def _rmsnorm(x, g, eps=EPS):
            return x * jax.lax.rsqrt(jnp.mean(x * x, axis=-1, keepdims=True) + eps) * g
        B, L, _ = x.shape
        scale = D ** (-0.5)
        q = _rmsnorm(x @ wq.T + bq, gq).reshape(B, L, H, D)
        k = _rmsnorm(x @ wk.T + bk, gk).reshape(B, L, H, D)
        v = (x @ wv.T + bv).reshape(B, L, H, D)
        shifts = np.asarray(SEQ_SHIFTS)
        idx = (np.arange(L)[None, :] - shifts[:, None]) % L
        k_sh = k[:, idx]
        v_sh = v[:, idx]
        q_all = jnp.stack([q] + [jnp.roll(q, c, axis=-1) for c in CHANNEL_SHIFTS], axis=0)
        scores = jnp.einsum('cblhd,bslhd->blhsc', q_all, k_sh) * scale
        mixed = jnp.einsum('blhsc,c->blhs', scores, w_mix[0])
        attn = jax.nn.softmax(mixed, axis=-1)
        out = jnp.einsum('blhs,bslhd->blhd', attn, v_sh).reshape(B, L, H * D)
        return out @ wo.T + bo

    def _L0_ffn_ref(hidden_states, wg_router, w_gate, w_up, w_down, ws_gate, ws_up, ws_down):
        import jax, jax.numpy as jnp
        import numpy as np
        TOP_K = 6
        CAP_FACTOR = 2

        def _moe_block(x2d, wg_router, w_gate, w_up, w_down, ws_gate, ws_up, ws_down):
            T, D = x2d.shape
            E = wg_router.shape[0]
            scores = jax.nn.softmax(x2d @ wg_router.T, axis=-1)
            topk_w, topk_idx = jax.lax.top_k(scores, TOP_K)
            topk_w = topk_w / (jnp.sum(topk_w, axis=-1, keepdims=True) + 1e-20)
            flat_idx = topk_idx.reshape(-1)
            oh = jax.nn.one_hot(flat_idx, E, dtype=jnp.int32)
            pos = jnp.cumsum(oh, axis=0) - 1
            pos_in_e = jnp.take_along_axis(pos, flat_idx[:, None], axis=1)[:, 0]
            C = CAP_FACTOR * (T * TOP_K // E)
            valid = pos_in_e < C
            safe_pos = jnp.where(valid, pos_in_e, 0)
            tok_id = jnp.repeat(jnp.arange(T), TOP_K)
            vmask = valid[:, None].astype(x2d.dtype)
            x_rep = x2d[tok_id] * vmask
            xe = jnp.zeros((E, C, D), x2d.dtype).at[flat_idx, safe_pos].add(x_rep)
            g = jnp.einsum('ecd,edf->ecf', xe, w_gate)
            u = jnp.einsum('ecd,edf->ecf', xe, w_up)
            ye = jnp.einsum('ecf,efd->ecd', jax.nn.silu(g) * u, w_down)
            y_tok = ye[flat_idx, safe_pos] * vmask
            y = jnp.sum(y_tok.reshape(T, TOP_K, D) * topk_w[..., None], axis=1)
            sh = jax.nn.silu(x2d @ ws_gate) * (x2d @ ws_up) @ ws_down
            return y + sh
        B, S, D = hidden_states.shape
        x2d = hidden_states.reshape(-1, D)
        out = _moe_block(x2d, wg_router, w_gate, w_up, w_down, ws_gate, ws_up, ws_down)
        return out.reshape(B, S, D)

    def _L1_attn_a_ref(x, w_qkv, b_qkv, w_fc, b_fc):
        import jax, jax.numpy as jnp
        import numpy as np
        E = 256
        H = 16
        D = E // H
        B = 4
        N = 256
        b, n, _ = x.shape
        qkv = x @ w_qkv + b_qkv
        q = qkv[..., :E].reshape(b, n, H, D)
        k = qkv[..., E:E + D]
        v = qkv[..., E + D:]
        scores = jnp.einsum('bnhd,bmd->bhnm', q, k) / jnp.sqrt(jnp.float32(D))
        causal = jnp.triu(jnp.ones((n, n), dtype=bool), k=1)
        scores = jnp.where(causal, -jnp.inf, scores)
        attn = jax.nn.softmax(scores, axis=-1)
        out = jnp.einsum('bhnm,bmd->bnhd', attn, v)
        out = out.reshape(b, n, E)
        return out @ w_fc + b_fc

    def _L1_attn_b_ref(hidden_states, Wqkv_w, Wqkv_b, lambda_q1, lambda_k1, lambda_q2, lambda_k2, subln_w, out_w, out_b):
        import jax, jax.numpy as jnp
        import numpy as np
        import math
        H = 16
        KV = 8
        D = 128
        HID = 256
        LAYER_IDX = 1
        LAMBDA_INIT = 0.8 - 0.6 * math.exp(-0.3 * LAYER_IDX)
        EPS = 1e-05
        B, S, _ = hidden_states.shape
        qkv = hidden_states @ Wqkv_w.T + Wqkv_b
        q, k, v = jnp.split(qkv, [H * D, H * D + KV * D], axis=-1)
        q = q.reshape(B, S, H // 2, 2, D)
        k = k.reshape(B, S, KV // 2, 2, D)
        v = v.reshape(B, S, KV // 2, 2 * D)
        rep = H // KV
        k = jnp.repeat(k, rep, axis=2)
        v = jnp.repeat(v, rep, axis=2)
        scale = D ** (-0.5)
        causal = jnp.tril(jnp.ones((S, S), bool))
        neg = jnp.finfo(jnp.float32).min

        def attn_map(qi, ki):
            s = jnp.einsum('bqhd,bkhd->bhqk', qi, ki) * scale
            s = jnp.where(causal, s, neg)
            return jax.nn.softmax(s, axis=-1)
        p1 = attn_map(q[:, :, :, 0], k[:, :, :, 0])
        p2 = attn_map(q[:, :, :, 1], k[:, :, :, 1])
        lam1 = jnp.exp(jnp.sum(lambda_q1 * lambda_k1))
        lam2 = jnp.exp(jnp.sum(lambda_q2 * lambda_k2))
        lam = lam1 - lam2 + LAMBDA_INIT
        p = p1 - lam * p2
        o = jnp.einsum('bhqk,bkhe->bqhe', p, v)
        rms = jax.lax.rsqrt(jnp.mean(o * o, axis=-1, keepdims=True) + EPS)
        o = o * rms * subln_w
        o = o * (1.0 - LAMBDA_INIT)
        o = o.reshape(B, S, H * D)
        return o @ out_w.T + out_b

    def _L1_ffn_ref(x, ln1_w, ln2_w, kv_d_w, q_d_w, k_u_w, v_u_w, q_u_w, rope_k_w, rope_q_w, o_w, sh_gate, sh_up, sh_down, r_gate, r_up, r_down, router_w, router_b):
        import jax, jax.numpy as jnp
        import numpy as np
        B, S, H = (4, 128, 256)
        NH = 16
        HD = H // NH
        RD = HD // 2
        LAT = H // 4
        I = 128
        NE = 8
        NSH = 1
        NR = NE - NSH
        TOPK = 2
        EPS = 1e-05
        SCALING = 8.0

        def _w(key, shape, fan_in):
            return jax.random.normal(key, shape, dtype=jnp.float32) / np.sqrt(fan_in)

        def rmsnorm(x, w):
            rms = jax.lax.rsqrt(jnp.mean(x * x, axis=-1, keepdims=True) + EPS)
            return w * rms * x

        def rope_cos_sin(seq_len):
            inv_freq = 1.0 / 10000.0 ** (jnp.arange(0, RD, 2, dtype=jnp.float32) / RD)
            t = jnp.arange(seq_len, dtype=jnp.float32)
            ang = jnp.outer(t, inv_freq)
            emb = jnp.concatenate([ang, ang], axis=-1)
            return (jnp.cos(emb), jnp.sin(emb))

        def apply_rope(x, cos, sin):
            c = cos[None, :, None, :]
            s = sin[None, :, None, :]
            x1, x2 = jnp.split(x, 2, axis=-1)
            rot = jnp.concatenate([-x2, x1], axis=-1)
            return x * c + rot * s

        def expert_ffn(x, wg, wu, wd):
            h = jax.nn.silu(x @ wg) * (x @ wu) / SCALING
            return h @ wd

        def attention(x, kv_d_w, q_d_w, k_u_w, v_u_w, q_u_w, rope_k_w, rope_q_w, o_w):
            b, s, _ = x.shape
            kv_d = x @ kv_d_w
            q_d = x @ q_d_w
            k_p = (kv_d @ k_u_w).reshape(b, s, NH, RD)
            q_p = (q_d @ q_u_w).reshape(b, s, NH, RD)
            v = (kv_d @ v_u_w).reshape(b, s, NH, HD)
            k_r = (x @ rope_k_w).reshape(b, s, NH, RD)
            q_r = (q_d @ rope_q_w).reshape(b, s, NH, RD)
            cos, sin = rope_cos_sin(s)
            k_r = apply_rope(k_r, cos, sin)
            q_r = apply_rope(q_r, cos, sin)
            k = jnp.concatenate([k_p, k_r], axis=-1)
            q = jnp.concatenate([q_p, q_r], axis=-1)
            scale = 1.0 / np.sqrt(HD)
            scores = jnp.einsum('bqhd,bkhd->bhqk', q, k) * scale
            causal = jnp.tril(jnp.ones((s, s), dtype=bool))
            scores = jnp.where(causal[None, None], scores, jnp.finfo(scores.dtype).min)
            probs = jax.nn.softmax(scores, axis=-1)
            out = jnp.einsum('bhqk,bkhd->bqhd', probs, v).reshape(b, s, H)
            return out @ o_w

        def moe(x, sh_gate, sh_up, sh_down, r_gate, r_up, r_down, router_w, router_b):
            shared = expert_ffn(x, sh_gate, sh_up, sh_down)
            logits = x @ router_w + router_b
            probs = jax.nn.sigmoid(logits)
            scores, idx = jax.lax.top_k(probs, TOPK)
            scores = scores / jnp.sum(scores, axis=-1, keepdims=True)
            w = jnp.sum(jax.nn.one_hot(idx, NR, dtype=x.dtype) * scores[..., None], axis=-2)
            combined = jnp.zeros_like(x)
            for e in range(NR):
                combined = combined + w[..., e:e + 1] * expert_ffn(x, r_gate[e], r_up[e], r_down[e])
            return shared + combined
        h = x + attention(rmsnorm(x, ln1_w), kv_d_w, q_d_w, k_u_w, v_u_w, q_u_w, rope_k_w, rope_q_w, o_w)
        out = h + moe(rmsnorm(h, ln2_w), sh_gate, sh_up, sh_down, r_gate, r_up, r_down, router_w, router_b)
        return out
    x = L0_attn_a_x
    x = x + _L0_attn_a_ref(_layernorm(x, axis=-1), L0_attn_a_Wq, L0_attn_a_bq, L0_attn_a_Wk, L0_attn_a_bk, L0_attn_a_Wv, L0_attn_a_bv, L0_attn_a_Wo, L0_attn_a_bo)
    x = x + _L0_ffn_ref(_layernorm(x, axis=-1), L0_ffn_wg_router, L0_ffn_w_gate, L0_ffn_w_up, L0_ffn_w_down, L0_ffn_ws_gate, L0_ffn_ws_up, L0_ffn_ws_down)
    x = x + _L0_attn_b_ref(_layernorm(x, axis=-1), L0_attn_b_wq, L0_attn_b_bq, L0_attn_b_wk, L0_attn_b_bk, L0_attn_b_wv, L0_attn_b_bv, L0_attn_b_gq, L0_attn_b_gk, L0_attn_b_w_mix, L0_attn_b_wo, L0_attn_b_bo)
    x = x + _L0_ffn_ref(_layernorm(x, axis=-1), L0_ffn_wg_router, L0_ffn_w_gate, L0_ffn_w_up, L0_ffn_w_down, L0_ffn_ws_gate, L0_ffn_ws_up, L0_ffn_ws_down)
    x = x + _L1_attn_a_ref(_layernorm(x, axis=-1), L1_attn_a_w_qkv, L1_attn_a_b_qkv, L1_attn_a_w_fc, L1_attn_a_b_fc)
    x = x + _L1_ffn_ref(_layernorm(x, axis=-1), L1_ffn_ln1_w, L1_ffn_ln2_w, L1_ffn_kv_d_w, L1_ffn_q_d_w, L1_ffn_k_u_w, L1_ffn_v_u_w, L1_ffn_q_u_w, L1_ffn_rope_k_w, L1_ffn_rope_q_w, L1_ffn_o_w, L1_ffn_sh_gate, L1_ffn_sh_up, L1_ffn_sh_down, L1_ffn_r_gate, L1_ffn_r_up, L1_ffn_r_down, L1_ffn_router_w, L1_ffn_router_b)
    x = x + _L1_attn_b_ref(_layernorm(x, axis=-1), L1_attn_b_Wqkv_w, L1_attn_b_Wqkv_b, L1_attn_b_lambda_q1, L1_attn_b_lambda_k1, L1_attn_b_lambda_q2, L1_attn_b_lambda_k2, L1_attn_b_subln_w, L1_attn_b_out_w, L1_attn_b_out_b)
    x = x + _L1_ffn_ref(_layernorm(x, axis=-1), L1_ffn_ln1_w, L1_ffn_ln2_w, L1_ffn_kv_d_w, L1_ffn_q_d_w, L1_ffn_k_u_w, L1_ffn_v_u_w, L1_ffn_q_u_w, L1_ffn_rope_k_w, L1_ffn_rope_q_w, L1_ffn_o_w, L1_ffn_sh_gate, L1_ffn_sh_up, L1_ffn_sh_down, L1_ffn_r_gate, L1_ffn_r_up, L1_ffn_r_down, L1_ffn_router_w, L1_ffn_router_b)
    return x

_drawn_inputs = setup_inputs


def setup_inputs(seed=0):
    import zlib

    import numpy as np

    out = dict(_drawn_inputs(seed))
    spreads = {'L0_attn_b_bq': (0.0, 0.337),
     'L0_attn_b_bk': (0.0, 0.8),
     'L0_attn_b_bv': (0.0, 0.1),
     'L0_attn_b_gq': (1.0, 0.6),
     'L0_attn_b_gk': (1.0, 0.6),
     'L0_attn_b_bo': (0.0, 0.1),
     'L1_attn_b_Wqkv_b': (0.0, 0.1),
     'L1_attn_b_subln_w': (1.0, 0.2),
     'L1_attn_b_out_b': (0.0, 0.1),
     'L1_ffn_ln1_w': (1.0, 0.2),
     'L1_ffn_ln2_w': (1.0, 0.6),
     'L1_ffn_router_b': (0.0, 0.765)}
    factors = {'L0_attn_a_Wq': 8.0,
     'L0_attn_a_bq': 8.0,
     'L0_attn_a_Wk': 8.0,
     'L0_attn_a_bk': 64.0,
     'L0_attn_a_Wv': 2.838,
     'L0_attn_a_bv': 5.028,
     'L0_ffn_wg_router': 5.269,
     'L0_ffn_w_gate': 4.682,
     'L0_ffn_w_up': 4.559,
     'L0_ffn_w_down': 4.528,
     'L1_attn_b_lambda_q1': 8.0,
     'L1_attn_b_lambda_k1': 64.0,
     'L1_attn_b_lambda_q2': 64.0,
     'L1_attn_b_lambda_k2': 7.167,
     'L1_attn_a_b_qkv': 3.374}
    for name, (base, spread) in spreads.items():
        noise = np.random.default_rng([zlib.crc32(name.encode()), seed]).standard_normal(out[name].shape)
        drawn = base * np.exp(spread * noise) if base else spread * noise
        out[name] = jnp.asarray(drawn.astype(out[name].dtype))
    for name, factor in factors.items():
        out[name] = (out[name] * factor).astype(out[name].dtype)
    return out
```

```python
from contextlib import ExitStack
import math

import numpy as np

import concourse.bass as bass
from concourse import mybir

F32 = mybir.dt.float32
BF16 = mybir.dt.bfloat16
U32 = mybir.dt.uint32
I32 = mybir.dt.int32
ALU = mybir.AluOpType
ACT = mybir.ActivationFunctionType
X_AXIS = mybir.AxisListType.X

P = 128
T = 1024
NT = T // P
D = 256
C = D // P
H = 16
HD = 16
BANK = 512
MASKED = -1.0e30
MAXIMA_PACE = 1.4

PAIRS = [(0, 0), (0, 1), (0, 2), (1, 0), (1, 1), (2, 0)]
ROWS = len(PAIRS) * HD
ROWS_M = ROWS + 3

E0, F0, K0 = 32, 176, 6
FH = F0 // 2
CAP = 2 * (T * K0 // E0)
CT = CAP // P
SLOTS = E0 * CAP
FS = 2 * F0
NS = FS // FH
DROPPED = 65536.0

D2 = 128
SHIFTS = [0, 1, -1, 2, -2, 4, -4, 8, -8, 16, -16, 32, -32, 64, -64, 128]
ROLLS = [0, 1, 2, 4, 8]
PAD_L, PAD_R = 128, 64
BAND = PAD_L + P + PAD_R
EPS = 1e-5
EPS_SHIFTED = 1e-6

E1, K1, I1 = 8, 2, 128
LAT = 64
LAMBDA_INIT = 0.8 - 0.6 * math.exp(-0.3)

CREDIT = 32


class Count:

    def __init__(self, sem, base=0):
        self.sem, self.base = sem, base

    def at(self, n):
        return n + self.base


class Kernel:

    def __init__(self, nc, ctx, dram):
        self.nc, self.ctx, self.dram, self.counts, self.serial = nc, ctx, dram, {}, 0
        self.credited = []

    def count(self, name):
        if name not in self.counts:
            self.counts[name] = Count(self.ctx.enter_context(self.nc.semaphore(name)))
        return self.counts[name]

    def freed(self, name):
        if name not in self.counts:
            c = self.count(name)
            c.base = CREDIT
            self.credited.append(c)
        return self.counts[name]


class Stage:

    def __init__(self, k):
        self.k, self.ctx = k, ExitStack()

    def __enter__(self):
        self.ctx.__enter__()
        self.k.serial += 1
        return self

    def __exit__(self, *a):
        return self.ctx.__exit__(*a)

    def sb(self, name, shape, dt=F32):
        return self.ctx.enter_context(self.k.nc.sbuf_tensor(f"{name}_{self.k.serial}", shape, dt))

    def block(self):
        return self.ctx.enter_context(self.k.nc.Block())


class Steps:

    def __init__(self, eng, count, offset=0):
        self.eng, self.count, self.offset, self.n = eng, count, offset, 0

    def mark(self, ins):
        ins.then_inc(self.count.sem, 1)
        self.n += 1
        return self.n

    def wait(self, n=None):
        self.eng.wait_ge(self.count.sem, self.count.at(self.offset + (self.n if n is None else n)))

    def link(self, ins):
        self.mark(ins)
        self.wait()


def bc(ap, shape):
    return ap.broadcast_to(shape)


def constants_stage(k):
    nc, d = k.nc, k.dram
    loaded = k.count("constants_loaded")
    with Stage(k) as st:
        raw = st.sb("raw", [P, 5 * P])
        raw_band = st.sb("raw_band", [P, BAND])
        block = st.block()

        @block.sync
        def _(sp):
            sp.dma_start(k.x[:], d["x"].rearrange("(i p) n -> p i n", p=P)).then_inc(loaded.sem, 16)
            sp.dma_start(raw[:], d["c_square"]).then_inc(loaded.sem, 16)
            sp.dma_start(raw_band[:], d["c_band"]).then_inc(loaded.sem, 16)
            sp.dma_start(k.iota[:], d["c_iota"]).then_inc(loaded.sem, 16)
            sp.dma_start(k.sel[:], d["c_sel"]).then_inc(loaded.sem, 16)
            sp.wait_ge(loaded.sem, 80)

        @block.gpsimd
        def _(pool):
            nc.gpsimd.memset(k.zero[:], 0.0)
            nc.gpsimd.memset(k.minus_half[:], -0.5)
            nc.gpsimd.memset(k.zero_bf[:], 0.0)
            for c in k.credited:
                pool.sem_inc(c.sem, CREDIT)

        @block.vector
        def _(dve):
            dve.wait_ge(loaded.sem, 80)
            nc.vector.tensor_copy(k.ident[:], raw[:, 0:P])
            nc.vector.tensor_copy(k.ident_bf[:], raw[:, 0:P])
            nc.vector.tensor_copy(k.mask_q[:], raw[:, P:2 * P])
            nc.vector.tensor_copy(k.mask_k[:], raw[:, 2 * P:3 * P])
            nc.vector.tensor_copy(k.ones[:], raw[:, 3 * P:4 * P])
            nc.vector.tensor_copy(k.ones_bf[:], raw[:, 3 * P:4 * P])
            nc.vector.tensor_copy(k.before_bf[:], raw[:, 4 * P:5 * P])
            nc.vector.tensor_copy(k.mask_band[:], raw_band[:])


def norm_stage(k, src, nat, rms_weight=None, layernorm=True):
    nc = k.nc
    stats, spread, rows = k.count("norm_stats"), k.count("norm_spread"), k.count("norm_rows")
    turned, weight = k.count("norm_turned"), k.count("norm_weight")
    steps = k.count("dve_steps")
    rms = rms_weight is not None
    roots = int(layernorm) + int(rms)
    with Stage(k) as st:
        bn = st.sb("bn", [P, NT, 6])
        mv = st.sb("mv", [P, NT, 2])
        base = st.sb("base", [P, 2, NT])
        scale = st.sb("scale", [P, 2, NT])
        second = st.sb("second", [P, NT])
        scaled = st.sb("scaled", [P, NT, D]) if rms else nat
        w = st.sb("w", [P, C]) if rms else None
        block = st.block()

        @block.sync
        def _(sp):
            if rms:
                sp.dma_start(w[:], rms_weight).then_inc(weight.sem, 16)

        @block.vector
        def _(dve):
            s = Steps(dve, steps)
            for i in range(NT):
                s.mark(nc.vector.bn_stats(bn[:, i, :], src[:, i, :]))
            s.wait()
            for i in range(NT):
                s.mark(nc.vector.bn_aggr(mv[:, i, :], bn[:, i, :]))
            s.wait()
            if layernorm:
                nc.vector.tensor_scalar(base[:, 0, :], mv[:, :, 1], EPS, None, ALU.add).then_inc(stats.sem, 1)
            if layernorm:
                dve.wait_ge(spread.sem, spread.at(1))
                for i in range(NT):
                    last = nc.vector.tensor_scalar(nat[:, i, :], src[:, i, :], mv[:, i, 0:1], scale[:, 0, i:i + 1],
                                                   ALU.subtract, ALU.mult)
                    if rms:
                        s.mark(last)
                    else:
                        last.then_inc(rows.sem, 1)
            if rms:
                if layernorm:
                    s.link(nc.vector.tensor_tensor(second[:], mv[:, :, 1], scale[:, 0, :], ALU.mult))
                    s.link(nc.vector.tensor_tensor(second[:], second[:], scale[:, 0, :], ALU.mult))
                else:
                    s.link(nc.vector.tensor_tensor(second[:], mv[:, :, 0], mv[:, :, 0], ALU.mult))
                    s.link(nc.vector.tensor_tensor(second[:], second[:], mv[:, :, 1], ALU.add))
                nc.vector.tensor_scalar(base[:, 1, :], second[:], EPS, None, ALU.add).then_inc(stats.sem, 1)
                dve.wait_ge(spread.sem, spread.at(roots))
                for i in range(NT):
                    nc.vector.tensor_scalar(scaled[:, i, :], (nat if layernorm else src)[:, i, :], scale[:, 1, i:i + 1],
                                            None, ALU.mult).then_inc(rows.sem, 1)
                dve.wait_ge(weight.sem, weight.at(16))
            for n in (1, 3):
                dve.wait_ge(turned.sem, turned.at(n + 1))
                out, bank = k.xt[:, n % 2, (n // 2) * BANK:(n // 2 + 1) * BANK], k.ps[:, n, :]
                if rms:
                    nc.vector.tensor_scalar(out, bank, w[:, 1:2], None, ALU.mult)
                else:
                    nc.vector.tensor_copy(out, bank)
            steps.base += s.n

        @block.scalar
        def _(act):
            if rms:
                act.wait_ge(weight.sem, weight.at(16))
            for n in (0, 2):
                act.wait_ge(turned.sem, turned.at(n + 1))
                out, bank = k.xt[:, n % 2, (n // 2) * BANK:(n // 2 + 1) * BANK], k.ps[:, n, :]
                if rms:
                    nc.scalar.activation(out, bank, ACT.Copy, scale=w[:, 0:1])
                else:
                    nc.scalar.copy(out, bank)

        @block.gpsimd
        def _(pool):
            for n in range(roots):
                pool.wait_ge(stats.sem, stats.at(n + 1))
                g = n if layernorm else 1
                nc.gpsimd.tensor_tensor(scale[:, g, :], base[:, g, :], k.minus_half[:, 0:NT], ALU.pow).then_inc(spread.sem, 1)

        @block.tensor
        def _(pe):
            for half in range(2):
                for c in range(C):
                    for j in range(4):
                        i = 4 * half + j
                        pe.wait_ge(rows.sem, rows.at(i + 1))
                        last = nc.tensor.transpose(k.ps[:, 2 * half + c, j * P:(j + 1) * P],
                                                   scaled[:, i, c * P:(c + 1) * P], k.ident[:])
                    last.then_inc(turned.sem, 1)

        stats.base += roots
        spread.base += roots
        rows.base += NT
        turned.base += 4
        weight.base += 16 * int(rms)


def stack_pair(k, kind, sp, pair, qs, ks, stacked):
    cols = bass.ds(pair * (2 * T), 2 * T)
    row = 0
    for part in range(3):
        again = (3 - part) * HD
        src = k.dram["q_parts"][part, :, bass.ds(pair * 2, 2), :].rearrange("d h t -> d (h t)")
        sp.dma_start(qs[row:row + again, cols], bc(src.unsqueeze(0), [3 - part, HD, 2 * T])).then_inc(stacked.sem, 16)
        if kind != "mqa":
            src = k.dram["k_parts"][0:3 - part, :, bass.ds(pair * 2, 2), :].rearrange("j d h t -> (j d) (h t)")
            sp.dma_start(ks[row:row + again, cols], src).then_inc(stacked.sem, 16)
        row += again


def stacked_per_pair(kind):
    return 16 * 3 * (1 if kind == "mqa" else 2)


def small_projections(k, kind, qf, kf, v, qs, ks):
    nc, d = k.nc, k.dram
    loaded, made, evac = k.count("small_weights"), k.count("small_products"), k.count("small_copied")
    rooms = k.count("small_turned")
    by_act, by_dve = k.count("operand_by_act"), k.count("operand_by_dve")
    first, second, third, rest = (k.count(n) for n in ("part_0", "part_1", "part_2", "part_rest"))
    stored, stacked, shared_stacked = k.count("parts_stored"), k.count("parts_stacked"), k.count("shared_stacked")
    k_rows = HD if kind == "mqa" else P
    if kind == "mla":
        units = [("k", 0, by_act), ("q", 0, by_act), ("k", 1, by_dve), ("q", 1, by_dve)]
    else:
        units = [("q", 0, by_dve), ("k", 0, by_act), ("q", 1, by_dve), ("k", 1, by_act)][:3 if kind == "mqa" else 4]
    U = len(units)
    nth = [sum(by is w for _, _, w in units[:n + 1]) for n, (_, _, by) in enumerate(units)]
    scale = HD ** -0.5
    with Stage(k) as st:
        if kind == "mla":
            w_down = st.sb("w_down", [P, C, 2 * LAT])
            w_rk = st.sb("w_rk", [P, C, P])
            w_lat = st.sb("w_lat", [LAT, 3 * P + D])
            perm = st.sb("perm", [P, P])
            cos = st.sb("cos", [P, T])
            sin = st.sb("sin", [P, T])
            lat = st.sb("lat", [LAT, 2, T])
            raw = st.sb("raw", [P, 2, T])
            turn = st.sb("turn", [P, 2, T])
            n_loads = 6
        else:
            n_cols = 3 * D if kind == "mha" else D + 2 * HD
            w_in = st.sb("w_in", [P, C, n_cols])
            b_qk = st.sb("b_qk", [P, 4])
            b_v = st.sb("b_v", [P, D if kind == "mha" else HD])
            n_loads = 3
        parts = {"q": [st.sb(f"q{j}", [P, C, T], BF16) for j in range(3)],
                 "k": [st.sb(f"k{j}", [k_rows, 1 if kind == "mqa" else C, T], BF16) for j in range(3)]}
        left = {"q": st.sb("qr", [P, C, T]), "k": st.sb("kr", [k_rows, 1 if kind == "mqa" else C, T])}
        whole = {"q": qf, "k": kf}
        block = st.block()
        ps = k.ps
        rows_of = lambda side: P if side == "q" else k_rows

        def part_0(n):
            side, c, by = units[n]
            nc.scalar.wait_ge(by.sem, by.at(nth[n]))
            nc.scalar.copy(parts[side][0][:, c, :], whole[side][0:rows_of(side), c, :]).then_inc(first.sem, 1)

        def part_1(n):
            side, c, _ = units[n]
            nc.scalar.wait_ge(rest.sem, rest.at(n + 1))
            nc.scalar.copy(parts[side][1][:, c, :], left[side][:, c, :]).then_inc(second.sem, 1)

        def remainder(n):
            side, c, _ = units[n]
            nc.vector.wait_ge(first.sem, first.at(n + 1))
            nc.vector.tensor_tensor(left[side][:, c, :], whole[side][0:rows_of(side), c, :], parts[side][0][:, c, :],
                                    ALU.subtract).then_inc(rest.sem, 1)

        def part_2(n):
            side, c, _ = units[n]
            nc.vector.wait_ge(second.sem, second.at(n + 1))
            nc.vector.tensor_tensor(parts[side][2][:, c, :], left[side][:, c, :], parts[side][1][:, c, :],
                                    ALU.subtract).then_inc(third.sem, 1)

        @block.gpsimd
        def _(pool):
            nc.gpsimd.memset(ks[ROWS:ROWS_M, :], 1.0)

        @block.sync
        def _(sp):
            if kind == "mla":
                for tile, name in ((w_down, "mla_down"), (w_rk, "mla_rk"), (w_lat, "mla_lat"), (perm, "c_perm"),
                                   (cos, "c_cos"), (sin, "c_sin")):
                    sp.dma_start(tile[:], d[name]).then_inc(loaded.sem, 16)
            else:
                sp.dma_start(w_in[:], d[kind + "_w"]).then_inc(loaded.sem, 16)
                sp.dma_start(b_qk[:], d[kind + "_bqk"]).then_inc(loaded.sem, 16)
                sp.dma_start(b_v[:], bc(d[kind + "_bv"], list(b_v.shape))).then_inc(loaded.sem, 16)
            for n, (side, c, _) in enumerate(units):
                for j, done in enumerate((first, second, third)):
                    sp.wait_ge(done.sem, done.at(n + 1))
                    rows = rows_of(side)
                    size = HD // 2 if kind == "mla" else HD
                    heads = rows // size
                    dim, head = (c * size, 0) if kind == "mla" else (0, c * heads)
                    sp.dma_start(d[side + "_parts"][j, dim:dim + size, head:head + heads, :].rearrange("d h t -> h d t"),
                                 parts[side][j][:, c, :]).then_inc(stored.sem, 16)
                if n == (3 if kind == "mla" else 1):
                    sp.wait_ge(stored.sem, stored.at(48 * (n + 1)))
                    if kind == "mqa":
                        row = 0
                        for part in range(3):
                            again = (3 - part) * HD
                            sp.dma_start(ks[row:row + again, :], d["k_parts"][0:3 - part, :, 0, :].rearrange("j d t -> (j d) t"))\
                                .then_inc(shared_stacked.sem, 16)
                            row += again
                        sp.wait_ge(shared_stacked.sem, shared_stacked.at(48))
                    stack_pair(k, kind, sp, 0, qs, ks, stacked)
            sp.wait_ge(stored.sem, stored.at(48 * U))
            sp.wait_ge(stacked.sem, stacked.at(stacked_per_pair(kind)))
            stack_pair(k, kind, sp, 1, qs, ks, stacked)

        if kind == "mla":
            @block.tensor
            def _(pe):
                pe.wait_ge(loaded.sem, loaded.at(16 * n_loads))
                for m in range(2):
                    for n in range(2):
                        for c in range(C):
                            last = nc.tensor.matmul(ps[0:LAT, 2 * m + n, :], w_down[:, c, m * LAT:(m + 1) * LAT],
                                                    k.xt[:, c, n * BANK:(n + 1) * BANK], start=c == 0, stop=c == C - 1)
                        last.then_inc(made.sem, 1)
                for n in range(2):
                    for c in range(C):
                        last = nc.tensor.matmul(ps[:, 4 + n, :], w_rk[:, c, :], k.xt[:, c, n * BANK:(n + 1) * BANK],
                                                start=c == 0, stop=c == C - 1)
                    last.then_inc(made.sem, 1)
                for g, (bank, side, col) in enumerate(((6, 0, 0), (0, 1, P), (2, 1, 2 * P))):
                    pe.wait_ge(evac.sem, evac.at(2 if g == 0 else 4))
                    for n in range(2):
                        nc.tensor.matmul(ps[:, bank + n, :], w_lat[:, col:col + P],
                                         lat[:, side, n * BANK:(n + 1) * BANK], start=True, stop=True).then_inc(made.sem, 1)
                pe.wait_ge(evac.sem, evac.at(12))
                for m in range(2):
                    for n in range(2):
                        nc.tensor.matmul(ps[:, 4 + 2 * m + n, :], perm[:], raw[:, m, n * BANK:(n + 1) * BANK],
                                         start=True, stop=True).then_inc(made.sem, 1)
                for i in range(NT):
                    last = nc.tensor.matmul(ps[:, i // 2, (i % 2) * D:(i % 2 + 1) * D], lat[:, 0, i * P:(i + 1) * P],
                                            w_lat[:, 3 * P:3 * P + D], start=True, stop=True)
                    if i % 2:
                        last.then_inc(made.sem, 1)

            @block.scalar
            def _(act):
                for n in range(4):
                    act.wait_ge(made.sem, made.at(n + 1))
                    nc.scalar.activation(lat[:, n // 2, (n % 2) * BANK:(n % 2 + 1) * BANK], ps[0:LAT, n, :], ACT.Copy,
                                         scale=scale if n >= 2 else 1.0).then_inc(evac.sem, 1)
                for n in range(2):
                    act.wait_ge(made.sem, made.at(5 + n))
                    nc.scalar.copy(raw[:, 0, n * BANK:(n + 1) * BANK], ps[:, 4 + n, :]).then_inc(evac.sem, 1)
                for g, (bank, dst) in enumerate(((6, kf[:, 0, :]), (0, qf[:, 0, :]), (2, raw[:, 1, :]))):
                    for n in range(2):
                        act.wait_ge(made.sem, made.at(7 + 2 * g + n))
                        nc.scalar.copy(dst[:, n * BANK:(n + 1) * BANK], ps[:, bank + n, :]).then_inc(evac.sem, 1)
                    if g < 2:
                        act.wait_ge(evac.sem, evac.at(8 + 2 * g))
                        act.sem_inc(by_act.sem, 1)
                for n in range(U):
                    part_0(n)
                    if n:
                        part_1(n - 1)
                part_1(U - 1)
                for n in range(4):
                    act.wait_ge(made.sem, made.at(17 + n))
                    nc.scalar.copy(v[:, 2 * n:2 * n + 2, :], ps[:, n, :].rearrange("p (i n) -> p i n", i=2))

            @block.vector
            def _(dve):
                s = Steps(dve, k.count("dve_steps"))
                dve.wait_ge(evac.sem, evac.at(12))
                dve.wait_ge(loaded.sem, loaded.at(16 * n_loads))
                for m, dst in ((0, kf), (1, qf)):
                    for n in range(2):
                        dve.wait_ge(made.sem, made.at(13 + 2 * m + n))
                        cols = slice(n * BANK, (n + 1) * BANK)
                        s.mark(nc.vector.tensor_tensor(turn[:, m, cols], ps[:, 4 + 2 * m + n, :], sin[:, cols], ALU.mult))
                        s.link(nc.vector.tensor_tensor(dst[:, 1, cols], raw[:, m, cols], cos[:, cols], ALU.mult))
                        last = nc.vector.tensor_tensor(dst[:, 1, cols], dst[:, 1, cols], turn[:, m, cols], ALU.add)
                        if n:
                            last.then_inc(by_dve.sem, 1)
                        else:
                            s.mark(last)
                            s.wait()
                k.count("dve_steps").base += s.n
                for n in range(U):
                    remainder(n)
                    if n:
                        part_2(n - 1)
                part_2(U - 1)

            made.base += 20
            evac.base += 12
        else:
            v_cols = D if kind == "mha" else HD

            @block.tensor
            def _(pe):
                pe.wait_ge(loaded.sem, loaded.at(16 * n_loads))
                for side, m, _ in units:
                    g = int(side == "k")
                    rows = k_rows if g else P
                    col = g * D + m * P
                    for n in range(2):
                        for c in range(C):
                            last = nc.tensor.matmul(ps[0:rows, 4 * g + 2 * m + n, :], w_in[:, c, col:col + rows],
                                                    k.xt[:, c, n * BANK:(n + 1) * BANK], start=c == 0, stop=c == C - 1)
                    last.then_inc(made.sem, 1)
                v_at = 2 * D if kind == "mha" else D + HD
                for i in range(NT):
                    if i % 2 == 0:
                        pe.wait_ge(by_dve.sem, by_dve.at(i // 4 + 1))
                    for c in range(C):
                        last = nc.tensor.matmul(ps[:, i // 2, (i % 2) * D:(i % 2) * D + v_cols],
                                                k.xt[:, c, i * P:(i + 1) * P], w_in[:, c, v_at:v_at + v_cols],
                                                start=c == 0, stop=c == C - 1)
                    if i % 2:
                        last.then_inc(rooms.sem, 1)

            @block.vector
            def _(dve):
                dve.wait_ge(loaded.sem, loaded.at(16 * n_loads))
                def copy_queries(c):
                    dve.wait_ge(made.sem, made.at(2 * c + 1))
                    nc.vector.tensor_scalar(qf[:, c, :], k.ps_flat[:, c * T:(c + 1) * T], b_qk[:, c:c + 1], scale, ALU.add, ALU.mult)\
                        .then_inc(by_dve.sem, 1)

                copy_queries(0)
                remainder(0)
                copy_queries(1)
                for n in range(1, U):
                    remainder(n)
                    part_2(n - 1)
                part_2(U - 1)
                for n in range(4):
                    dve.wait_ge(rooms.sem, rooms.at(n + 1))
                    bank = ps[:, n, :].rearrange("p (i n) -> p i n", i=2)[:, :, 0:v_cols]
                    nc.vector.tensor_tensor(v[:, 2 * n:2 * n + 2, :], bank, bc(b_v[:].unsqueeze(1), [P, 2, v_cols]), ALU.add)

            @block.scalar
            def _(act):
                act.wait_ge(loaded.sem, loaded.at(16 * n_loads))
                for n, (side, c, _) in enumerate(units):
                    if side == "k":
                        act.wait_ge(made.sem, made.at(n + 1))
                        nc.scalar.activation(kf[0:k_rows, c, :], k.ps_flat[0:k_rows, (4 + 2 * c) * BANK:(6 + 2 * c) * BANK],
                                             ACT.Identity, bias=b_qk[0:k_rows, 2 + c:3 + c]).then_inc(by_act.sem, 1)
                    part_0(n)
                    if n:
                        part_1(n - 1)
                part_1(U - 1)

            made.base += U
            rooms.base += 4
        loaded.base += 16 * n_loads
        by_act.base += sum(by is by_act for _, _, by in units)
        by_dve.base += sum(by is by_dve for _, _, by in units)
        for c in (first, second, third, rest):
            c.base += U
        stored.base += 48 * U
        shared_stacked.base += 48 * int(kind == "mqa")


def small_attention_stage(k, kind, qs, ks, v):
    nc, d = k.nc, k.dram
    shared_k = kind == "mqa"
    stacked, per_pair = k.count("parts_stacked"), stacked_per_pair(kind)
    ready, freed, reduced = k.count("max_scores"), k.freed("max_scores_freed"), k.count("max_reduced")
    turned, parts_made, moved = k.count("max_turned"), k.count("max_parts"), k.count("max_moved")
    v_ready = k.count("values_of_head")
    st_ready, e_ready, used = k.count("scores_ready"), k.count("exps_ready"), k.freed("value_products")
    copied, stored = k.freed("head_copied"), [k.freed(f"head_stored_{u}") for u in range(2)]
    steps = k.count("dve_steps")
    pairs, ring, e_ring, ahead = H // 2, 3, 4, 2
    blocks = [(c, j, max(c * BANK, j * P), (c + 1) * BANK - max(c * BANK, j * P)) for c in range(2) for j in range(4 * c + 4)]
    per_head = len(blocks)
    B = 2 * per_head
    half_ends = {n: b[0] for n, b in enumerate(blocks) if b[1] == 4 * b[0] + 3}
    pieces = [(u, i, col, min(BANK, (i + 1) * P - col)) for u in range(2) for i in range(NT) for col in range(0, (i + 1) * P, BANK)]
    M = len(pieces)
    USES = M + 1
    order, done, r = [], 0, 0
    lead = [sum(p[3] for p in pieces[:n]) for n in range(M + 1)]
    for n in range(B):
        order.append(("scores", n))
        done += blocks[n % per_head][3]
        while r < M and lead[r] < done * MAXIMA_PACE:
            order.append(("piece", r))
            r += 1
            if r == M:
                order.append(("finish", None))
        order.append(("value", n))
    assert r == M

    with Stage(k) as st:
        e = st.sb("e", [P, e_ring, BANK])
        vb = st.sb("vb", [P, 2, NT, HD + 1])
        ob = st.sb("ob", [HD + 1, 2, T])
        raw = st.sb("raw", [P, 2, NT, 2])
        mx = st.sb("mx", [P, 2, NT])
        neg = st.sb("neg", [2 * NT, P])
        parts = [st.sb(f"neg{j}", [2 * NT, P], BF16) for j in range(3)]
        block = st.block()
        ps = k.ps_flat
        MAX_BANK, OUT_BANK = 5, 3

        @block.gpsimd
        def _(pool):
            nc.gpsimd.memset(vb[:, :, :, HD:HD + 1], 1.0).then_inc(v_ready.sem, 1)
            if shared_k:
                nc.gpsimd.tensor_copy(vb[:, 0, :, 0:HD], v[:]).then_inc(v_ready.sem, 1)
            else:
                with pool.Fori(0, pairs) as it:
                    for u in range(2):
                        pool.wait_ge(used.sem, used.at(it * B + (u - 1) * per_head))
                        nc.gpsimd.tensor_copy(vb[:, u, :, 0:HD], v[:, :, bass.ds((it * 2 + u) * HD, HD)]).then_inc(v_ready.sem, 1)

        @block.tensor
        def _(pe):
            def piece(pair, r):
                u, i, col, w = pieces[r]
                at = (MAX_BANK + r % ring) * BANK
                if r == 0:
                    pe.wait_ge(stacked.sem, stacked.at(pair * per_pair + per_pair))
                pe.wait_ge(freed.sem, freed.at(pair * USES + (r + 1 - ring if r >= ring else -((M - r) % ring))))
                keys = ks[0:ROWS, col:col + w] if shared_k else ks[0:ROWS, bass.ds((pair * 2 + u) * T + col, w)]
                diagonal = col + w == (i + 1) * P
                last = nc.tensor.matmul(ps[:, at:at + w], qs[0:ROWS, bass.ds((pair * 2 + u) * T + i * P, P)], keys,
                                        start=True, stop=not diagonal)
                if diagonal:
                    last = nc.tensor.matmul(ps[:, at + w - P:at + w], k.ident_bf[:], k.mask_q[:], start=False, stop=True)
                last.then_inc(ready.sem, 1)

            def turn_maxima(pair):
                at = (MAX_BANK + M % ring) * BANK
                pe.wait_ge(freed.sem, freed.at(pair * USES + M + 1 - ring))
                pe.wait_ge(reduced.sem, reduced.at(pair + 1))
                nc.tensor.transpose(ps[0:2 * NT, at:at + P], mx[:].rearrange("p u i -> p (u i)"), k.ident[:]).then_inc(turned.sem, 1)

            def scores(pair, n):
                u, (c, j, t0, w) = n // per_head, blocks[n % per_head]
                if n == 0:
                    pe.wait_ge(moved.sem, moved.at(pair * 48 + 48))
                base = (n % ring) * BANK
                diagonal = j * P >= c * BANK
                keys = ks[0:ROWS_M, j * P:(j + 1) * P] if shared_k else ks[0:ROWS_M, bass.ds((pair * 2 + u) * T + j * P, P)]
                last = nc.tensor.matmul(ps[:, base:base + w], keys, qs[0:ROWS_M, bass.ds((pair * 2 + u) * T + t0, w)],
                                        start=True, stop=not diagonal)
                if diagonal:
                    last = nc.tensor.matmul(ps[:, base:base + P], k.ident_bf[:], k.mask_k[:], start=False, stop=True)
                last.then_inc(st_ready.sem, 1)

            def value(pair, n):
                u, (c, j, t0, w) = n // per_head, blocks[n % per_head]
                pe.wait_ge(e_ready.sem, e_ready.at(pair * B + n + 1))
                if (c, j) == (0, 0) and not shared_k:
                    pe.wait_ge(v_ready.sem, v_ready.at(pair * 2 + u + 2))
                if j == 0:
                    pe.wait_ge(copied.sem, copied.at(pair * 4 + 2 * u + c + 1 - 2))
                col = (OUT_BANK + c) * BANK + t0 - c * BANK
                nc.tensor.matmul(ps[0:HD + 1, col:col + w], vb[:, 0 if shared_k else u, j, :], e[:, n % e_ring, 0:w],
                                 start=j == 0, stop=j == 4 * c + 3).then_inc(used.sem, 1)

            def turn(pair, maxima):
                for n in range(ahead):
                    scores(pair, n)
                for what, n in order:
                    if what == "scores" and n + ahead < B:
                        scores(pair, n + ahead)
                    elif what == "value":
                        value(pair, n)
                    elif what == "piece" and maxima:
                        piece(pair + 1, n)
                    elif what == "finish" and maxima:
                        turn_maxima(pair + 1)

            pe.wait_ge(v_ready.sem, v_ready.at(1 + shared_k))
            for r in range(M):
                piece(0, r)
            turn_maxima(0)
            with pe.Fori(0, pairs - 1) as it:
                turn(it, True)
            turn(pairs - 1, False)

        @block.scalar
        def _(act):
            with act.Fori(0, pairs) as it:
                if kind == "mha":
                    rows = d["expert_in"].rearrange("(p a) n -> p (a n)", p=P)
                    width = SLOTS * D // P // ZERO_DMAS
                    for n in range(ZERO_DMAS // pairs):
                        act.dma_start(rows[:, bass.ds((it * (ZERO_DMAS // pairs) + n) * width, width)], k.zero[:])\
                            .then_inc(k.count("slots_zeroed").sem, 16)
                for n in range(B):
                    w = blocks[n % per_head][3]
                    act.wait_ge(st_ready.sem, st_ready.at(it * B + n + 1))
                    act.wait_ge(used.sem, used.at(it * B + n + 1 - e_ring))
                    base = (n % ring) * BANK
                    nc.scalar.activation(e[:, n % e_ring, 0:w], ps[:, base:base + w], ACT.Exp).then_inc(e_ready.sem, 1)

        @block.vector
        def _(dve):
            def piece(pair, r):
                u, i, col, w = pieces[r]
                at = (MAX_BANK + r % ring) * BANK
                dve.wait_ge(ready.sem, ready.at(pair * M + r + 1))
                nc.vector.reduce_max(raw[:, u, i, col // BANK:col // BANK + 1], ps[:, at:at + w], X_AXIS).then_inc(freed.sem, 1)

            def finish(pair, first=False):
                s = Steps(dve, steps, pair)
                dve.wait_ge(freed.sem, freed.at(pair * USES + M))
                nc.vector.tensor_tensor(mx[:], raw[:, :, :, 0], raw[:, :, :, 1], ALU.max).then_inc(reduced.sem, 1)
                dve.wait_ge(turned.sem, turned.at(pair + 1))
                at = (MAX_BANK + M % ring) * BANK
                nc.vector.tensor_scalar(neg[:], ps[0:2 * NT, at:at + P], -1.0, None, ALU.mult).then_inc(freed.sem, 1)
                dve.wait_ge(freed.sem, freed.at(pair * USES + USES))
                if not first:
                    dve.wait_ge(moved.sem, moved.at(pair * 48))
                nc.vector.tensor_copy(parts[0][:], neg[:]).then_inc(parts_made.sem, 1)
                dve.wait_ge(parts_made.sem, parts_made.at(pair * 3 + 1))
                s.link(nc.vector.tensor_tensor(neg[:], neg[:], parts[0][:], ALU.subtract))
                nc.vector.tensor_copy(parts[1][:], neg[:]).then_inc(parts_made.sem, 1)
                dve.wait_ge(parts_made.sem, parts_made.at(pair * 3 + 2))
                nc.vector.tensor_tensor(parts[2][:], neg[:], parts[1][:], ALU.subtract).then_inc(parts_made.sem, 1)

            def copy_half(pair, u, c):
                last = max(n for n, half in half_ends.items() if half == c)
                if c == 0:
                    dve.wait_ge(stored[u].sem, stored[u].at(pair * 32))
                dve.wait_ge(used.sem, used.at(pair * B + u * per_head + last + 1))
                nc.vector.tensor_copy(ob[:, u, c * BANK:(c + 1) * BANK], ps[0:HD + 1, (OUT_BANK + c) * BANK:(OUT_BANK + c + 1) * BANK])\
                    .then_inc(copied.sem, 1)

            def turn(pair, maxima):
                for what, n in order:
                    if what == "piece" and maxima:
                        piece(pair + 1, n)
                    elif what == "finish" and maxima:
                        finish(pair + 1)
                    elif what == "value" and n % per_head in half_ends:
                        copy_half(pair, n // per_head, half_ends[n % per_head])

            s = Steps(dve, steps)
            s.link(nc.vector.memset(raw[:], -3.0e38))
            steps.base += s.n
            for r in range(M):
                piece(0, r)
            finish(0, first=True)
            with dve.Fori(0, pairs - 1) as it:
                turn(it, True)
            turn(pairs - 1, False)
            steps.base += pairs

        @block.sync
        def _(sp):
            def move_maxima(pair):
                for j in range(3):
                    sp.wait_ge(parts_made.sem, parts_made.at(pair * 3 + j + 1))
                    sp.dma_start(qs[ROWS + j:ROWS + j + 1, bass.ds(pair * (2 * T), 2 * T)].rearrange("a (r t) -> a r t", t=P),
                                 parts[j][:]).then_inc(moved.sem, 16)

            def store(pair):
                for u in range(2):
                    sp.wait_ge(copied.sem, copied.at(pair * 4 + 2 * u + 2))
                    sp.dma_start(d["head_out"][bass.ds((pair * 2 + u) * HD, HD), :], ob[0:HD, u, :]).then_inc(stored[u].sem, 16)
                    sp.dma_start(d["head_sum"][bass.ds(pair * 2 + u, 1), :], ob[HD:HD + 1, u, :]).then_inc(stored[u].sem, 16)

            move_maxima(0)
            with sp.Fori(0, pairs - 2) as it:
                sp.wait_ge(stacked.sem, stacked.at(it * per_pair + 2 * per_pair))
                stack_pair(k, kind, sp, it + 2, qs, ks, stacked)
                move_maxima(it + 1)
                store(it)
            move_maxima(pairs - 1)
            store(pairs - 2)
            store(pairs - 1)
            for u in range(2):
                sp.wait_ge(stored[u].sem, stored[u].at(16 * H))

        stacked.base += per_pair * pairs
        ready.base += M * pairs
        freed.base += USES * pairs
        reduced.base += pairs
        turned.base += pairs
        parts_made.base += 3 * pairs
        moved.base += 48 * pairs
        v_ready.base += 2 if shared_k else H + 1
        for n in (st_ready, e_ready, used):
            n.base += H * per_head
        copied.base += 2 * H
        for u in range(2):
            stored[u].base += 16 * H


def small_output_stage(k, w_name, b_name, target):
    nc, d = k.nc, k.dram
    loaded, inv, spread, normed = (k.count(n) for n in ("out_loaded", "out_inverse", "out_spread", "out_normed"))
    made = k.count("out_product")
    steps = k.count("dve_steps")
    with Stage(k) as st:
        ot = st.sb("ot", [P, C, T])
        sums = st.sb("sums", [H, T])
        wo = st.sb("wo", [P, C, D])
        bo = st.sb("bo", [P, D])
        block = st.block()
        n_loads = 3 + int(b_name is not None)

        @block.sync
        def _(sp):
            sp.dma_start(sums[:], d["head_sum"]).then_inc(loaded.sem, 16)
            sp.dma_start(ot[:], d["head_out"].rearrange("(c p) t -> p c t", p=P)).then_inc(loaded.sem, 16)
            sp.dma_start(wo[:], d[w_name]).then_inc(loaded.sem, 16)
            if b_name:
                sp.dma_start(bo[:], bc(d[b_name], [P, D])).then_inc(loaded.sem, 16)

        @block.tensor
        def _(pe):
            pe.wait_ge(loaded.sem, loaded.at(16 * n_loads))
            pe.wait_ge(inv.sem, inv.at(1))
            for c in range(C):
                for n in range(2):
                    nc.tensor.matmul(k.ps[:, 2 * c + n, :], k.sel[:, c, :], sums[:, n * BANK:(n + 1) * BANK],
                                     start=True, stop=True).then_inc(spread.sem, 1)
            for i in range(NT):
                pe.wait_ge(normed.sem, normed.at(4))
                for c in range(C):
                    last = nc.tensor.matmul(k.ps[:, 4 + i // 2, (i % 2) * D:(i % 2 + 1) * D], ot[:, c, i * P:(i + 1) * P],
                                            wo[:, c, :], start=c == 0, stop=c == C - 1)
                if i % 2:
                    last.then_inc(made.sem, 1)

        @block.vector
        def _(dve):
            s = Steps(dve, steps)
            dve.wait_ge(loaded.sem, loaded.at(16 * n_loads))
            nc.vector.reciprocal(sums[:], sums[:]).then_inc(inv.sem, 1)
            if b_name:
                s.link(nc.vector.tensor_tensor(target[:], target[:], bc(bo[:].unsqueeze(1), [P, NT, D]), ALU.add))
            for n in range(4):
                dve.wait_ge(spread.sem, spread.at(n + 1))
                cols = ot[:, n // 2, (n % 2) * BANK:(n % 2 + 1) * BANK]
                nc.vector.tensor_tensor(cols, cols, k.ps[:, n, :], ALU.mult).then_inc(normed.sem, 1)
            for n in range(NT // 2):
                dve.wait_ge(made.sem, made.at(n + 1))
                pair = target[:, 2 * n:2 * n + 2, :].rearrange("p i n -> p (i n)")
                nc.vector.tensor_tensor(pair, pair, k.ps[:, 4 + n, :], ALU.add)
            steps.base += s.n

        loaded.base += 16 * n_loads
        inv.base += 1
        spread.base += 4
        normed.base += 4
        made.base += NT // 2


def small_attention(k, kind, target):
    with Stage(k) as st:
        shared_k = kind == "mqa"
        qs = st.sb("qs", [ROWS_M, H * T], BF16)
        ks = st.sb("ks", [ROWS_M, (1 if shared_k else H) * T], BF16)
        v = st.sb("v", [P, NT, HD if shared_k else D])
        with Stage(k) as inner:
            qf = inner.sb("qf", [P, C, T])
            kf = inner.sb("kf", [P, C, T])
            small_projections(k, kind, qf, kf, v, qs, ks)
        small_attention_stage(k, kind, qs, ks, v)
    small_output_stage(k, kind + "_wo", None if kind == "mla" else kind + "_bo", target)


def route_stage(k, slot_in, slot_out, weights):
    nc, d = k.nc, k.dram
    loaded, logits, exps = k.count("router_loaded"), k.count("router_logits"), k.count("router_exps")
    shifted, chosen, places = k.count("router_shifted"), k.count("router_chosen"), k.count("router_places")
    steps = k.count("dve_steps")
    with Stage(k) as st:
        wr = st.sb("wr", [P, C, E0])
        s_ = st.sb("s", [P, NT, E0])
        col = st.sb("col", [P, NT])
        top = st.sb("top", [P, NT, 8])
        which = st.sb("which", [P, NT, 8], U32)
        which_f = st.sb("which_f", [P, NT, K0])
        pick = st.sb("pick", [P, NT * K0, E0])
        spent = st.sb("spent", [P, NT, E0], BF16)
        slot = st.sb("slot", [P, NT, E0])
        late = st.sb("late", [P, NT, E0])
        slot_f = st.sb("slot_f", [P, NT * K0])
        kept = st.sb("kept", [P, NT * K0])
        block = st.block()

        @block.sync
        def _(sp):
            sp.dma_start(wr[:], d["moe_router"]).then_inc(loaded.sem, 16)

        @block.tensor
        def _(pe):
            pe.wait_ge(loaded.sem, loaded.at(16))
            for i in range(NT):
                for c in range(C):
                    last = nc.tensor.matmul(k.ps[:, 0, i * E0:(i + 1) * E0], k.xt[:, c, i * P:(i + 1) * P], wr[:, c, :],
                                            start=c == 0, stop=c == C - 1)
            last.then_inc(logits.sem, 1)
            pe.wait_ge(chosen.sem, chosen.at(1))
            for i in range(NT):
                for j in range(i + 1):
                    last = nc.tensor.matmul(k.ps[:, 1, i * E0:(i + 1) * E0], (k.before_bf if j == i else k.ones_bf)[:],
                                            spent[:, j, :], start=j == 0, stop=j == i)
            last.then_inc(places.sem, 1)

        @block.scalar
        def _(act):
            act.wait_ge(shifted.sem, shifted.at(1))
            nc.scalar.activation(s_[:], s_[:], ACT.Exp).then_inc(exps.sem, 1)

        @block.vector
        def _(dve):
            s = Steps(dve, steps)
            wide = [P, NT, E0]
            dve.wait_ge(logits.sem, logits.at(1))
            bank = k.ps[:, 0, 0:NT * E0].rearrange("p (i e) -> p i e", e=E0)
            s.link(nc.vector.reduce_max(col[:], bank, X_AXIS))
            nc.vector.tensor_tensor(s_[:], bank, bc(col[:].unsqueeze(2), wide), ALU.subtract).then_inc(shifted.sem, 1)
            dve.wait_ge(exps.sem, exps.at(1))
            s.link(nc.vector.reduce_sum(col[:], s_[:], X_AXIS))
            s.link(nc.vector.reciprocal(col[:], col[:]))
            s.link(nc.vector.tensor_tensor(s_[:], s_[:], bc(col[:].unsqueeze(2), wide), ALU.mult))
            for i in range(NT):
                s.mark(nc.vector.max(top[:, i, :], s_[:, i, :]))
            s.wait()
            for i in range(NT):
                s.mark(nc.vector.max_index(which[:, i, :], top[:, i, :], s_[:, i, :]))
            s.link(nc.vector.reduce_sum(col[:], top[:, :, 0:K0], X_AXIS))
            s.link(nc.vector.tensor_scalar(col[:], col[:], 1e-20, None, ALU.add))
            s.link(nc.vector.reciprocal(col[:], col[:]))
            s.mark(nc.vector.tensor_tensor(weights[:], top[:, :, 0:K0], bc(col[:].unsqueeze(2), [P, NT, K0]), ALU.mult))
            s.link(nc.vector.tensor_copy(which_f[:], which[:, :, 0:K0]))
            flat = which_f[:].rearrange("p i r -> p (i r)")
            s.link(nc.vector.tensor_tensor(pick[:], bc(flat.unsqueeze(2), [P, NT * K0, E0]),
                                           bc(k.iota[:, 0:1, :], [P, NT * K0, E0]), ALU.is_equal))
            nc.vector.reduce_sum(late[:], pick[:].rearrange("p (i r) e -> p i e r", r=K0), X_AXIS).then_inc(steps.sem, 1)
            s.n += 1
            s.wait()
            nc.vector.tensor_copy(spent[:], late[:]).then_inc(chosen.sem, 1)
            dve.wait_ge(chosen.sem, chosen.at(1))
            dve.wait_ge(places.sem, places.at(1))
            bank = k.ps[:, 1, 0:NT * E0].rearrange("p (i e) -> p i e", e=E0)
            s.mark(nc.vector.tensor_scalar(late[:], bank, float(CAP), DROPPED, ALU.is_ge, ALU.mult))
            s.link(nc.vector.tensor_tensor(slot[:], bank, bc(k.iota[:, 1:2, :], wide), ALU.add))
            s.link(nc.vector.tensor_tensor(slot[:], slot[:], late[:], ALU.add))
            for i in range(NT):
                rows = pick[:, i * K0:(i + 1) * K0, :]
                s.mark(nc.vector.tensor_tensor(rows, rows, bc(slot[:, i:i + 1, :], [P, K0, E0]), ALU.mult))
            s.wait()
            s.link(nc.vector.reduce_sum(slot_f[:], pick[:], X_AXIS))
            s.mark(nc.vector.tensor_copy(slot_out[:], slot_f[:]))
            s.link(nc.vector.tensor_scalar(kept[:], slot_f[:], float(SLOTS), None, ALU.is_lt))
            w = weights[:].rearrange("p i r -> p (i r)")
            s.link(nc.vector.tensor_tensor(w, w, kept[:], ALU.mult))
            s.link(nc.vector.tensor_scalar(slot_f[:], slot_f[:], float(SLOTS - 1), None, ALU.min))
            s.link(nc.vector.tensor_copy(slot_in[:], slot_f[:]))
            steps.base += s.n

        for n in (logits, exps, shifted, chosen, places):
            n.base += 1
        loaded.base += 16


def dispatch_stage(k, slot_out):
    nc, d = k.nc, k.dram
    sent, loaded = k.count("rows_sent"), k.count("shared_loaded")
    made, silu, hidden = k.count("shared_products"), k.count("shared_silu"), k.count("shared_hidden")
    down, added = k.count("shared_down"), k.count("shared_added")
    with Stage(k) as st:
        w_in = st.sb("w_in", [P, 2, C, FS])
        w_out = st.sb("w_out", [FH, NS, D])
        act_t = st.sb("act_t", [FH, NS, T])
        block = st.block()

        @block.sync
        def _(sp):
            sp.dma_start(w_in[:], d["shared_in"]).then_inc(loaded.sem, 16)
            sp.dma_start(w_out[:], d["shared_out"]).then_inc(loaded.sem, 16)

        @block.gpsimd
        def _(pool):
            pool.wait_ge(k.count("slots_zeroed").sem, 16 * ZERO_DMAS)
            for i in range(NT):
                for r in range(K0):
                    n = i * K0 + r
                    nc.gpsimd.indirect_dma_start(out=d["expert_in"], out_offset=bass.IndirectOffsetOnAxis(slot_out[:, n:n + 1], 0),
                                                 in_=k.xn[:, i, :], in_offset=None, bounds_check=SLOTS - 1,
                                                 oob_is_err=False).then_inc(sent.sem, 16)
            pool.wait_ge(sent.sem, sent.at(16 * NT * K0))

        @block.tensor
        def _(pe):
            pe.wait_ge(loaded.sem, loaded.at(32))
            for m in range(NS):
                if m >= 2:
                    pe.wait_ge(hidden.sem, hidden.at(m - 1))
                for g in range(2):
                    for n in range(2):
                        for c in range(C):
                            last = nc.tensor.matmul(k.ps[0:FH, 4 * (m % 2) + 2 * g + n, :], w_in[:, g, c, m * FH:(m + 1) * FH],
                                                    k.xt[:, c, n * BANK:(n + 1) * BANK], start=c == 0, stop=c == C - 1)
                    last.then_inc(made.sem, 1)
            for n in range(NT // 2):
                pe.wait_ge(hidden.sem, hidden.at(NS))
                for i in (2 * n, 2 * n + 1):
                    for m in range(NS):
                        last = nc.tensor.matmul(k.ps[:, n, (i % 2) * D:(i % 2 + 1) * D], act_t[:, m, i * P:(i + 1) * P],
                                                w_out[:, m, :], start=m == 0, stop=m == NS - 1)
                last.then_inc(down.sem, 1)

        @block.scalar
        def _(act):
            for m in range(NS):
                act.wait_ge(made.sem, made.at(2 * m + 1))
                bank = 4 * (m % 2) * BANK
                nc.scalar.activation(act_t[:, m, :], k.ps_flat[0:FH, bank:bank + T], ACT.Silu).then_inc(silu.sem, 1)

        @block.vector
        def _(dve):
            for m in range(NS):
                dve.wait_ge(made.sem, made.at(2 * m + 2))
                dve.wait_ge(silu.sem, silu.at(m + 1))
                bank = (4 * (m % 2) + 2) * BANK
                nc.vector.tensor_tensor(act_t[:, m, :], act_t[:, m, :], k.ps_flat[0:FH, bank:bank + T], ALU.mult)\
                    .then_inc(hidden.sem, 1)
            for n in range(NT // 2):
                dve.wait_ge(down.sem, down.at(n + 1))
                pair = k.x[:, 2 * n:2 * n + 2, :].rearrange("p i n -> p (i n)")
                nc.vector.tensor_tensor(pair, pair, k.ps[:, n, :], ALU.add)

        sent.base += 16 * NT * K0
        loaded.base += 32
        made.base += 2 * NS
        silu.base += NS
        hidden.base += NS
        down.base += NT // 2


def experts_stage(k):
    nc, d = k.nc, k.dram
    loaded = [k.count(f"expert_loaded_{u}") for u in range(2)]
    turned, rows_t, made = k.count("expert_rows_turned"), k.freed("expert_rows"), k.count("expert_products")
    silu, hidden, down = k.count("expert_silu"), k.freed("expert_hidden"), k.freed("expert_down")
    copied, stored = k.freed("expert_copied"), [k.freed(f"expert_stored_{u}") for u in range(2)]
    with Stage(k) as st:
        rows = st.sb("rows", [P, 2, CT, D])
        w_in = st.sb("w_in", [P, 2, 2 * C * F0])
        w_out = st.sb("w_out", [FH, 2, 2 * D])
        xt = st.sb("xt", [P, 2, C, CAP])
        gate = st.sb("gate", [FH, 2, 2, CAP])
        hid = st.sb("hid", [FH, 2, 2, CAP])
        y = st.sb("y", [P, 2, CT * D])
        block = st.block()

        @block.sync
        def _(sp):
            with sp.Fori(0, E0 // 2) as it:
                for u in range(2):
                    sp.wait_ge(down.sem, down.at(it * 2 + u + 1 - 2))
                    e = it * 2 + u
                    sp.dma_start(rows[:, u], d["expert_in"][bass.ds(e * CAP, CAP), :].rearrange("(s p) n -> p s n", p=P))\
                        .then_inc(loaded[u].sem, 16)
                    sp.dma_start(w_in[:, u, :], d["expert_w_in"][bass.ds(e * P, P), :]).then_inc(loaded[u].sem, 16)
                    sp.dma_start(w_out[:, u, :], d["expert_w_out"][bass.ds(e * FH, FH), :]).then_inc(loaded[u].sem, 16)

        @block.tensor
        def _(pe):
            with pe.Fori(0, E0 // 2) as it:
                for u in range(2):
                    pe.wait_ge(loaded[u].sem, loaded[u].at(it * 48 + 48))
                    pe.wait_ge(hidden.sem, hidden.at(it * 2))
                    for c in range(C):
                        for s in range(CT):
                            last = nc.tensor.transpose(k.ps[:, 2 * u + c, s * P:(s + 1) * P], rows[:, u, s, c * P:(c + 1) * P],
                                                       k.ident[:])
                    last.then_inc(turned.sem, 1)
                for u in range(2):
                    w = w_in[:, u, :].rearrange("p (g c f) -> p g c f", g=2, c=C)
                    pe.wait_ge(rows_t.sem, rows_t.at(it * 2 + 1 + u))
                    pe.wait_ge(copied.sem, copied.at(it * 2))
                    for g in range(2):
                        for m in range(2):
                            for c in range(C):
                                last = nc.tensor.matmul(k.ps[0:FH, 4 * (1 - u) + 2 * g + m, 0:CAP], w[:, g, c, m * FH:(m + 1) * FH],
                                                        xt[:, u, c, :], start=c == 0, stop=c == C - 1)
                        last.then_inc(made.sem, 1)
                for u in range(2):
                    pe.wait_ge(hidden.sem, hidden.at(it * 2 + 1 + u))
                    for s in range(CT):
                        col = (4 + 2 * u) * BANK + s * D
                        for m in range(2):
                            last = nc.tensor.matmul(k.ps_flat[:, col:col + D], hid[:, u, m, s * P:(s + 1) * P],
                                                    w_out[:, u, m * D:(m + 1) * D], start=m == 0, stop=m == 1)
                    last.then_inc(down.sem, 1)

        @block.vector
        def _(dve):
            with dve.Fori(0, E0 // 2) as it:
                for u in range(2):
                    dve.wait_ge(turned.sem, turned.at(it * 2 + u + 1))
                    nc.vector.tensor_copy(xt[:, u], k.ps[:, 2 * u:2 * u + 2, 0:CAP]).then_inc(rows_t.sem, 1)
                for u in range(2):
                    dve.wait_ge(made.sem, made.at(it * 4 + 2 * u + 2))
                    dve.wait_ge(silu.sem, silu.at(it * 2 + u + 1))
                    bank = 4 * (1 - u) + 2
                    nc.vector.tensor_tensor(hid[:, u], gate[:, u], k.ps[0:FH, bank:bank + 2, 0:CAP], ALU.mult)\
                        .then_inc(hidden.sem, 1)

        @block.scalar
        def _(act):
            with act.Fori(0, E0 // 2) as it:
                for u in range(2):
                    act.wait_ge(made.sem, made.at(it * 4 + 2 * u + 1))
                    act.wait_ge(hidden.sem, hidden.at(it * 2 + u + 1 - 2))
                    bank = 4 * (1 - u)
                    nc.scalar.activation(gate[:, u], k.ps[0:FH, bank:bank + 2, 0:CAP], ACT.Silu).then_inc(silu.sem, 1)
                for u in range(2):
                    act.wait_ge(down.sem, down.at(it * 2 + u + 1))
                    act.wait_ge(stored[u].sem, stored[u].at(it * 16))
                    bank = (4 + 2 * u) * BANK
                    nc.scalar.copy(y[:, u, :], k.ps_flat[:, bank:bank + CT * D]).then_inc(copied.sem, 1)
                    act.wait_ge(copied.sem, copied.at(it * 2 + u + 1))
                    act.dma_start(d["expert_out"][bass.ds((it * 2 + u) * CAP, CAP), :].rearrange("(s p) n -> p s n", p=P),
                                  y[:, u, :].rearrange("p (s n) -> p s n", s=CT)).then_inc(stored[u].sem, 16)
            for u in range(2):
                act.wait_ge(stored[u].sem, stored[u].at(8 * E0))

        for u in range(2):
            loaded[u].base += 24 * E0
            stored[u].base += 8 * E0
        for n in (turned, rows_t, silu, hidden, down, copied):
            n.base += E0
        made.base += 2 * E0


def combine_stage(k, slot_in, weights):
    nc, d = k.nc, k.dram
    ring = 8
    fetched = [k.count(f"row_fetched_{n}") for n in range(ring)]
    added = k.freed("row_added")
    with Stage(k) as st:
        got = st.sb("got", [P, ring, D])
        block = st.block()

        @block.gpsimd
        def _(pool):
            for r in range(K0):
                for i in range(NT):
                    pool.wait_ge(added.sem, added.at(r * NT + i + 1 - ring))
                    n = i * K0 + r
                    nc.gpsimd.indirect_dma_start(out=got[:, i % ring, :], out_offset=None, in_=d["expert_out"],
                                                 in_offset=bass.IndirectOffsetOnAxis(slot_in[:, n:n + 1], 0))\
                        .then_inc(fetched[i % ring].sem, 16)

        @block.vector
        def _(dve):
            for r in range(K0):
                for i in range(NT):
                    dve.wait_ge(fetched[i].sem, fetched[i].at(16 * (r + 1)))
                    dve.wait_ge(added.sem, added.at(r * NT + i + 1 - NT))
                    nc.vector.scalar_tensor_tensor(k.x[:, i, :], got[:, i, :], weights[:, i, r:r + 1], k.x[:, i, :],
                                                   ALU.mult, ALU.add).then_inc(added.sem, 1)

        for f in fetched:
            f.base += 16 * K0
        added.base += NT * K0


def layer_moe(k):
    norm_stage(k, k.x, k.xn)
    with Stage(k) as st:
        slot_in, slot_out = st.sb("slot_in", [P, NT * K0], I32), st.sb("slot_out", [P, NT * K0], I32)
        weights = st.sb("weights", [P, NT, K0])
        route_stage(k, slot_in, slot_out, weights)
        dispatch_stage(k, slot_out)
        experts_stage(k)
        combine_stage(k, slot_in, weights)


def dense_route_stage(k, share):
    nc, d = k.nc, k.dram
    loaded, logits, biased, probs = (k.count(n) for n in ("gate_loaded", "gate_logits", "gate_biased", "gate_probs"))
    steps = k.count("dve_steps")
    with Stage(k) as st:
        wr = st.sb("wr", [P, C, E1 - 1])
        br = st.sb("br", [P, E1 - 1])
        s_ = st.sb("s", [P, NT, E1])
        top = st.sb("top", [P, NT, 8])
        which = st.sb("which", [P, NT, 8], U32)
        which_f = st.sb("which_f", [P, NT, K1])
        pick = st.sb("pick", [P, NT * K1, E1])
        col = st.sb("col", [P, NT])
        block = st.block()
        R = E1 - 1

        @block.sync
        def _(sp):
            sp.dma_start(wr[:], d["gate_router"]).then_inc(loaded.sem, 16)
            sp.dma_start(br[:], bc(d["gate_bias"], [P, R])).then_inc(loaded.sem, 16)

        @block.tensor
        def _(pe):
            pe.wait_ge(loaded.sem, loaded.at(32))
            for i in range(NT):
                for c in range(C):
                    last = nc.tensor.matmul(k.ps[:, 0, i * R:(i + 1) * R], k.xt[:, c, i * P:(i + 1) * P], wr[:, c, :],
                                            start=c == 0, stop=c == C - 1)
            last.then_inc(logits.sem, 1)

        @block.scalar
        def _(act):
            act.wait_ge(biased.sem, biased.at(1))
            nc.scalar.activation(s_[:, :, 0:R], s_[:, :, 0:R], ACT.Sigmoid).then_inc(probs.sem, 1)

        @block.vector
        def _(dve):
            s = Steps(dve, steps)
            s.mark(nc.vector.memset(s_[:, :, R:E1], -1.0))
            dve.wait_ge(loaded.sem, loaded.at(32))
            dve.wait_ge(logits.sem, logits.at(1))
            nc.vector.tensor_tensor(s_[:, :, 0:R], k.ps[:, 0, 0:NT * R].rearrange("p (i e) -> p i e", e=R),
                                    bc(br[:].unsqueeze(1), [P, NT, R]), ALU.add).then_inc(biased.sem, 1)
            dve.wait_ge(probs.sem, probs.at(1))
            s.wait()
            for i in range(NT):
                s.mark(nc.vector.max(top[:, i, :], s_[:, i, :]))
            s.wait()
            for i in range(NT):
                s.mark(nc.vector.max_index(which[:, i, :], top[:, i, :], s_[:, i, :]))
            s.link(nc.vector.reduce_sum(col[:], top[:, :, 0:K1], X_AXIS))
            s.link(nc.vector.reciprocal(col[:], col[:]))
            s.mark(nc.vector.tensor_tensor(top[:, :, 0:K1], top[:, :, 0:K1], bc(col[:].unsqueeze(2), [P, NT, K1]), ALU.mult))
            s.link(nc.vector.tensor_copy(which_f[:], which[:, :, 0:K1]))
            flat = which_f[:].rearrange("p i r -> p (i r)")
            wide = [P, NT * K1, E1]
            s.link(nc.vector.tensor_tensor(pick[:], bc(flat.unsqueeze(2), wide), bc(k.iota[:, 0:1, 0:E1], wide), ALU.is_equal))
            for r in range(K1):
                part = pick[:].rearrange("p (i r) e -> p i r e", r=K1)[:, :, r, :]
                s.mark(nc.vector.tensor_tensor(part, part, bc(top[:, :, r:r + 1], [P, NT, E1]), ALU.mult))
            s.wait()
            s.link(nc.vector.reduce_sum(s_[:], pick[:].rearrange("p (i r) e -> p i e r", r=K1), X_AXIS))
            s.mark(nc.vector.tensor_scalar(share[:, :, 1:E1], s_[:, :, 0:R], 1 / 8, None, ALU.mult))
            s.link(nc.vector.memset(share[:, :, 0:1], 1 / 8))
            steps.base += s.n

        for n in (logits, biased, probs):
            n.base += 1
        loaded.base += 32


def dense_experts_stage(k, share):
    nc, d = k.nc, k.dram
    loaded = [k.count(f"dense_loaded_{u}") for u in range(2)]
    made, silu, hidden = k.count("dense_products"), k.count("dense_silu"), k.freed("dense_hidden")
    down, added = k.freed("dense_down"), k.freed("dense_added")
    with Stage(k) as st:
        w_in = st.sb("w_in", [P, 2, 2 * C * I1])
        w_out = st.sb("w_out", [I1, 2, D])
        gate = st.sb("gate", [I1, 2, BANK])
        hid = st.sb("hid", [I1, T])
        block = st.block()

        @block.sync
        def _(sp):
            with sp.Fori(0, E1 // 2) as it:
                for u in range(2):
                    sp.wait_ge(down.sem, down.at(it * (2 * NT // 2) + (u - 1) * (NT // 2)))
                    e = it * 2 + u
                    sp.dma_start(w_in[:, u, :], d["dense_w_in"][bass.ds(e * P, P), :]).then_inc(loaded[u].sem, 16)
                    sp.dma_start(w_out[:, u, :], d["dense_w_out"][bass.ds(e * I1, I1), :]).then_inc(loaded[u].sem, 16)

        @block.tensor
        def _(pe):
            with pe.Fori(0, E1 // 2) as it:
                for u in range(2):
                    w = w_in[:, u, :].rearrange("p (g c f) -> p g c f", g=2, c=C)
                    pe.wait_ge(loaded[u].sem, loaded[u].at(it * 32 + 32))
                    for n in range(2):
                        pe.wait_ge(hidden.sem, hidden.at(it * 4 + 2 * u + n + 1 - 2))
                        for g in range(2):
                            for c in range(C):
                                last = nc.tensor.matmul(k.ps[:, 2 * n + g, :], w[:, g, c, :], k.xt[:, c, n * BANK:(n + 1) * BANK],
                                                        start=c == 0, stop=c == C - 1)
                            last.then_inc(made.sem, 1)
                    for n in range(NT // 2):
                        pe.wait_ge(hidden.sem, hidden.at(it * 4 + 2 * u + n // 2 + 1))
                        pe.wait_ge(added.sem, added.at(it * NT + u * (NT // 2) + n + 1 - 4))
                        for i in (2 * n, 2 * n + 1):
                            last = nc.tensor.matmul(k.ps[:, 4 + n, (i % 2) * D:(i % 2 + 1) * D], hid[:, i * P:(i + 1) * P],
                                                    w_out[:, u, :], start=True, stop=True)
                        last.then_inc(down.sem, 1)

        @block.scalar
        def _(act):
            with act.Fori(0, E1 // 2) as it:
                for u in range(2):
                    for n in range(2):
                        j = 2 * u + n
                        act.wait_ge(made.sem, made.at(it * 8 + 2 * j + 1))
                        act.wait_ge(hidden.sem, hidden.at(it * 4 + j + 1 - 2))
                        nc.scalar.activation(gate[:, n, :], k.ps[:, 2 * n, :], ACT.Silu).then_inc(silu.sem, 1)

        @block.vector
        def _(dve):
            s = Steps(dve, k.count("dve_steps"))
            s.link(nc.vector.tensor_tensor(k.x[:], k.x[:], k.xn[:], ALU.add))
            k.count("dve_steps").base += s.n
            with dve.Fori(0, E1 // 2) as it:
                for u in range(2):
                    for n in range(2):
                        j = 2 * u + n
                        dve.wait_ge(made.sem, made.at(it * 8 + 2 * j + 2))
                        dve.wait_ge(silu.sem, silu.at(it * 4 + j + 1))
                        dve.wait_ge(down.sem, down.at(it * NT + (u - 1) * (NT // 2) + 2 * n + 2))
                        nc.vector.tensor_tensor(hid[:, n * BANK:(n + 1) * BANK], gate[:, n, :], k.ps[:, 2 * n + 1, :], ALU.mult)\
                            .then_inc(hidden.sem, 1)
                    for n in range(NT // 2):
                        at = it * NT + u * (NT // 2) + n + 1
                        dve.wait_ge(down.sem, down.at(at))
                        dve.wait_ge(added.sem, added.at(at - NT // 2))
                        for i in (2 * n, 2 * n + 1):
                            last = nc.vector.scalar_tensor_tensor(k.x[:, i, :], k.ps[:, 4 + n, (i % 2) * D:(i % 2 + 1) * D],
                                                                  share[:, i, bass.ds(it * 2 + u, 1)], k.x[:, i, :],
                                                                  ALU.mult, ALU.add)
                        last.then_inc(added.sem, 1)

        for u in range(2):
            loaded[u].base += 16 * E1
        made.base += 4 * E1
        silu.base += 2 * E1
        hidden.base += 2 * E1
        down.base += NT // 2 * E1
        added.base += NT // 2 * E1


def layer_mla(k):
    norm_stage(k, k.x, k.xn, k.dram["ln1"])
    small_attention(k, "mla", k.xn)
    norm_stage(k, k.xn, None, k.dram["ln2"], layernorm=False)
    with Stage(k) as st:
        share = st.sb("share", [P, NT, E1])
        dense_route_stage(k, share)
        dense_experts_stage(k, share)


ZERO_DMAS = 24


def shifted_project_stage(k, qg, kg, mix, rk, rq):
    nc, d = k.nc, k.dram
    loaded = [k.count(f"qk_loaded_{u}") for u in range(2)]
    params, folded = k.count("qk_params"), k.count("qk_folded")
    made, squared, scaled = k.freed("qk_products"), k.freed("qk_squared"), k.freed("qk_scaled")
    summed = k.freed("qk_summed")
    totals, based, inverse, spread = (k.count(n) for n in ("qk_totals", "qk_based", "qk_inverse", "qk_spread"))
    steps = k.count("dve_steps")
    with Stage(k) as st:
        w = st.sb("w", [P, 2, 2 * C * P])
        bg = st.sb("bg", [P, 2, 2, H])
        bgain = st.sb("bgain", [P, 2, H])
        sq = st.sb("sq", [P, 2, T])
        acc = st.sb("acc", [P, 2, T])
        base = st.sb("base", [P, 2 * NT])
        inv = st.sb("inv", [P, 2 * NT])
        wide = st.sb("wide", [P, NT, P])
        roll = st.sb("roll", [P, len(ROLLS), P])
        w_mix = st.sb("w_mix", [P, len(ROLLS)])
        block = st.block()
        ps = k.ps_flat

        @block.sync
        def _(sp):
            sp.dma_start(bg[:], d["shifted_bg"]).then_inc(params.sem, 16)
            sp.dma_start(roll[:], d["c_roll"]).then_inc(params.sem, 16)
            sp.dma_start(w_mix[:], bc(d["shifted_mix"], [P, len(ROLLS)])).then_inc(params.sem, 16)
            with sp.Fori(0, H // 2) as it:
                for u in range(2):
                    sp.wait_ge(made.sem, made.at(it * 4 + 2 * (u - 1)))
                    sp.dma_start(w[:, u, :], d["shifted_w_qk"][bass.ds((it * 2 + u) * P, P), :]).then_inc(loaded[u].sem, 16)

        @block.tensor
        def _(pe):
            with pe.Fori(0, H // 2) as it:
                for u in range(2):
                    ww = w[:, u, :].rearrange("p (g c f) -> p g c f", g=2, c=C)
                    pe.wait_ge(loaded[u].sem, loaded[u].at(it * 16 + 16))
                    for g in range(2):
                        pe.wait_ge(scaled.sem, scaled.at(it * 4 + 2 * u + g + 1 - 4))
                        for n in range(2):
                            for c in range(C):
                                last = nc.tensor.matmul(k.ps[:, 4 * u + 2 * g + n, :], ww[:, g, c, :],
                                                        k.xt[:, c, n * BANK:(n + 1) * BANK], start=c == 0, stop=c == C - 1)
                        last.then_inc(made.sem, 1)
            pe.wait_ge(summed.sem, summed.at(2 * H))
            for g in range(2):
                for i in range(NT):
                    last = nc.tensor.matmul(ps[:, g * NT + i:g * NT + i + 1], acc[:, g, i * P:(i + 1) * P], k.ones[:, 0:1],
                                            start=True, stop=True)
            last.then_inc(totals.sem, 1)
            pe.wait_ge(inverse.sem, inverse.at(2))
            for i in range(NT):
                last = nc.tensor.matmul(ps[:, 2 * BANK + i * P:2 * BANK + (i + 1) * P], wide[:, i, :], k.ident[:],
                                        start=True, stop=True)
            last.then_inc(spread.sem, 1)

        @block.scalar
        def _(act):
            act.wait_ge(params.sem, params.at(48))
            with act.Fori(0, H // 2) as it:
                for u in range(2):
                    for g in range(2):
                        at = it * 4 + 2 * u + g
                        act.wait_ge(made.sem, made.at(at + 1))
                        act.wait_ge(summed.sem, summed.at(at - 1))
                        bank = (4 * u + 2 * g) * BANK
                        nc.scalar.activation(sq[:, g, :], ps[:, bank:bank + T], ACT.Square,
                                             bias=bg[:, g, 0, bass.ds(it * 2 + u, 1)]).then_inc(squared.sem, 1)

        @block.gpsimd
        def _(pool):
            pool.wait_ge(based.sem, based.at(1))
            nc.gpsimd.tensor_tensor(inv[:], base[:], k.minus_half[:], ALU.pow).then_inc(inverse.sem, 1)

        @block.vector
        def _(dve):
            s = Steps(dve, steps)
            dve.wait_ge(params.sem, params.at(48))
            s.link(nc.vector.tensor_tensor(bgain[:], bg[:, :, 0, :], bg[:, :, 1, :], ALU.mult))
            s.link(nc.vector.tensor_scalar(mix[:], roll[:, 0, :], w_mix[:, 0:1], None, ALU.mult))
            for n in range(1, len(ROLLS)):
                s.link(nc.vector.scalar_tensor_tensor(mix[:], roll[:, n, :], w_mix[:, n:n + 1], mix[:], ALU.mult, ALU.add))
            s.link(nc.vector.memset(acc[:], 0.0))
            with dve.Fori(0, H // 2) as it:
                for u in range(2):
                    for g, dst in ((0, qg), (1, kg)):
                        at = it * 4 + 2 * u + g
                        dve.wait_ge(made.sem, made.at(at + 1))
                        dve.wait_ge(squared.sem, squared.at(at + 1))
                        h = it * 2 + u
                        bank = (4 * u + 2 * g) * BANK
                        nc.vector.tensor_scalar(dst[:, bass.ds(h * T, T)], ps[:, bank:bank + T],
                                                bg[:, g, 1, bass.ds(h, 1)], bgain[:, g, bass.ds(h, 1)], ALU.mult, ALU.add)\
                            .then_inc(scaled.sem, 1)
                        dve.wait_ge(summed.sem, summed.at(at - 1))
                        nc.vector.tensor_tensor(acc[:, g, :], acc[:, g, :], sq[:, g, :], ALU.add).then_inc(summed.sem, 1)
            dve.wait_ge(totals.sem, totals.at(1))
            nc.vector.tensor_scalar(base[:], ps[:, 0:2 * NT], 1.0 / (H * D2), EPS_SHIFTED, ALU.mult, ALU.add)\
                .then_inc(based.sem, 1)
            dve.wait_ge(inverse.sem, inverse.at(1))
            nc.vector.tensor_scalar(rq[:], inv[:, 0:NT], D2 ** -0.5, None, ALU.mult)
            nc.vector.tensor_copy(wide[:], bc(inv[:, NT:2 * NT].unsqueeze(2), [P, NT, P])).then_inc(inverse.sem, 1)
            dve.wait_ge(spread.sem, spread.at(1))
            nc.vector.tensor_copy(rk[:], ps[:, 2 * BANK:2 * BANK + T])
            steps.base += s.n

        params.base += 48
        for u in range(2):
            loaded[u].base += 8 * H
        for n in (made, squared, scaled):
            n.base += 2 * H
        summed.base += 2 * H
        for n in (totals, based, spread):
            n.base += 1
        inverse.base += 2


def shifted_attention_stage(k, qg, kg, mix, rk, rq):
    nc, d = k.nc, k.dram
    loaded = [k.count(f"vo_loaded_{u}") for u in range(2)]
    keys_ready, mixed_made, mixed = k.count("band_keys"), k.count("mixed_products"), k.count("mixed_copied")
    v_made, v_copied = k.count("head_values"), k.count("head_values_copied")
    scored, shifted, exped, probs = (k.count(n) for n in ("band_scored", "band_shift", "band_exps", "band_probs"))
    turned, turned_copied = k.count("band_turned"), k.freed("band_turned_copied")
    summed, copied = k.freed("band_summed"), k.freed("band_copied")
    projected, added, params = k.freed("band_projected"), k.freed("band_added"), k.count("band_params")
    steps = k.count("dve_steps")
    W = PAD_L + T + PAD_R
    N = 2 * NT
    with Stage(k) as st:
        wv = st.sb("wv", [P, 2, C * P])
        wo = st.sb("wo", [P, 2, D])
        bv = st.sb("bv", [P, H])
        bo = st.sb("bo", [P, D])
        nrq = st.sb("nrq", [P, NT])
        kb = st.sb("kb", [P, 2, W])
        qm = st.sb("qm", [P, 2, T])
        vh = st.sb("vh", [P, 2, T])
        pr = st.sb("pr", [P, 4, BAND])
        pt = st.sb("pt", [P, 2, 3 * P])
        stat = st.sb("stat", [P, 4, N])
        ot = k.xn[:].rearrange("p i n -> p (i n)").rearrange("p (u t) -> p u t", u=2)
        block = st.block()
        ps = k.ps_flat

        @block.sync
        def _(sp):
            sp.dma_start(bv[:], d["shifted_bv"]).then_inc(params.sem, 16)
            sp.dma_start(bo[:], bc(d["shifted_bo"], [P, D])).then_inc(params.sem, 16)
            with sp.Fori(0, H // 2) as it:
                for u in range(2):
                    sp.wait_ge(projected.sem, projected.at(it * 2 + u + 1 - 2))
                    h = it * 2 + u
                    sp.dma_start(wv[:, u, :], d["shifted_w_v"][bass.ds(h * P, P), :]).then_inc(loaded[u].sem, 16)
                    sp.dma_start(wo[:, u, :], d["shifted_wo"][bass.ds(h * P, P), :]).then_inc(loaded[u].sem, 16)

        @block.tensor
        def _(pe):
            with pe.Fori(0, H // 2) as it:
                pe.wait_ge(added.sem, added.at(it * 8))
                for u in range(2):
                    h = it * 2 + u
                    for n in range(2):
                        last = nc.tensor.matmul(k.ps[:, 4 * u + n, :], mix[:], qg[:, bass.ds(h * T + n * BANK, BANK)],
                                                start=True, stop=True)
                    last.then_inc(mixed_made.sem, 1)
                    pe.wait_ge(loaded[u].sem, loaded[u].at(it * 32 + 32))
                    for i in range(NT):
                        for c in range(C):
                            last = nc.tensor.matmul(k.ps[:, 4 * u + 2 + i // 4, (i % 4) * P:(i % 4 + 1) * P],
                                                    k.xt[:, c, i * P:(i + 1) * P], wv[:, u, c * P:(c + 1) * P],
                                                    start=c == 0, stop=c == C - 1)
                    last.then_inc(v_made.sem, 1)

                def score(n):
                    u, i = n // NT, n % NT
                    if i == 0:
                        pe.wait_ge(mixed.sem, mixed.at(it * 2 + u + 1))
                        pe.wait_ge(v_copied.sem, v_copied.at(it * 2 + u + 1))
                        pe.wait_ge(keys_ready.sem, keys_ready.at(it * 2 + u + 1))
                    nc.tensor.matmul(k.ps[:, n % 4, 0:BAND], qm[:, u, i * P:(i + 1) * P], kb[:, u, i * P:i * P + BAND],
                                     start=True, stop=False)
                    nc.tensor.matmul(k.ps[:, n % 4, 0:BAND], k.ident_bf[:], k.mask_band[:], start=False, stop=True)\
                        .then_inc(scored.sem, 1)

                def turn(n):
                    if n == 0:
                        pe.wait_ge(v_copied.sem, v_copied.at(it * 2 + 2))
                    pe.wait_ge(probs.sem, probs.at(it * N + n + 1))
                    pe.wait_ge(turned_copied.sem, turned_copied.at(it * N + n + 1 - 2))
                    for b in range(3):
                        rows = min(P, BAND - b * P)
                        last = nc.tensor.transpose(k.ps[0:rows, 4 + n % 2, b * P:(b + 1) * P], pr[:, n % 4, b * P:b * P + rows],
                                                   k.ident[:])
                    last.then_inc(turned.sem, 1)

                def value(n):
                    u, i = n // NT, n % NT
                    pe.wait_ge(turned_copied.sem, turned_copied.at(it * N + n + 1))
                    pe.wait_ge(copied.sem, copied.at(it * N + n + 1 - 2))
                    for b in range(3):
                        rows, j = min(P, BAND - b * P), (i - 1 + b) % NT
                        last = nc.tensor.matmul(k.ps[:, 6 + n % 2, 0:P], vh[0:rows, u, j * P:(j + 1) * P],
                                                pt[0:rows, n % 2, b * P:(b + 1) * P], start=b == 0, stop=b == 2)
                    last.then_inc(summed.sem, 1)

                for n in range(N + 3):
                    if n < N:
                        score(n)
                    if 2 <= n < N + 2:
                        turn(n - 2)
                    if n >= 3:
                        value(n - 3)
                pe.wait_ge(copied.sem, copied.at(it * N + N))
                for u in range(2):
                    for n in range(NT // 2):
                        for i in (2 * n, 2 * n + 1):
                            last = nc.tensor.matmul(k.ps[:, 4 * u + n, (i % 2) * D:(i % 2 + 1) * D], ot[:, u, i * P:(i + 1) * P],
                                                    wo[:, u, :], start=True, stop=True)
                    last.then_inc(projected.sem, 1)

        @block.scalar
        def _(act):
            with act.Fori(0, H // 2) as it:
                for u in range(2):
                    act.wait_ge(mixed_made.sem, mixed_made.at(it * 2 + u + 1))
                    nc.scalar.copy(qm[:, u, :], ps[:, 4 * u * BANK:(4 * u + 2) * BANK]).then_inc(mixed.sem, 1)
                    act.wait_ge(v_made.sem, v_made.at(it * 2 + u + 1))
                    nc.scalar.copy(vh[:, u, :], ps[:, (4 * u + 2) * BANK:(4 * u + 4) * BANK]).then_inc(v_copied.sem, 1)
                for n in range(N + 2):
                    if n < N:
                        act.wait_ge(shifted.sem, shifted.at(it * N + n + 1))
                        nc.scalar.activation(pr[:, n % 4, :], k.ps[:, n % 4, 0:BAND], ACT.Exp, bias=stat[:, 1, n:n + 1],
                                             scale=rq[:, n % NT:n % NT + 1], accum_out=stat[:, 2, n:n + 1]).then_inc(exped.sem, 1)
                    if n >= 2:
                        m = n - 2
                        act.wait_ge(turned.sem, turned.at(it * N + m + 1))
                        act.wait_ge(summed.sem, summed.at(it * N + m + 1 - 2))
                        nc.scalar.copy(pt[:, m % 2, 0:2 * P], k.ps[:, 4 + m % 2, 0:2 * P])
                        nc.scalar.copy(pt[0:PAD_R, m % 2, 2 * P:3 * P], k.ps[0:PAD_R, 4 + m % 2, 2 * P:3 * P])\
                            .then_inc(turned_copied.sem, 1)

        @block.vector
        def _(dve):
            s = Steps(dve, steps)
            dve.wait_ge(params.sem, params.at(32))
            s.mark(nc.vector.tensor_scalar(nrq[:], rq[:], -1.0, None, ALU.mult))
            s.link(nc.vector.tensor_tensor(k.x[:], k.x[:], bc(bo[:].unsqueeze(1), [P, NT, D]), ALU.add))
            steps.base += s.n
            before = 0
            with dve.Fori(0, H // 2) as it:
                s = Steps(dve, steps, it * (2 * N))
                for u in range(2):
                    h = it * 2 + u
                    nc.vector.tensor_tensor(kb[:, u, PAD_L:PAD_L + T], kg[:, bass.ds(h * T, T)], rk[:], ALU.mult)
                    nc.vector.tensor_tensor(kb[:, u, 0:PAD_L], kg[:, bass.ds(h * T + T - PAD_L, PAD_L)], rk[:, T - PAD_L:T], ALU.mult)
                    nc.vector.tensor_tensor(kb[:, u, PAD_L + T:W], kg[:, bass.ds(h * T, PAD_R)], rk[:, 0:PAD_R], ALU.mult)\
                        .then_inc(keys_ready.sem, 1)
                for n in range(N + 4):
                    if n < N:
                        dve.wait_ge(scored.sem, scored.at(it * N + n + 1))
                        s.link(nc.vector.reduce_max(stat[:, 0, n:n + 1], k.ps[:, n % 4, 0:BAND], X_AXIS))
                        nc.vector.tensor_tensor(stat[:, 1, n:n + 1], stat[:, 0, n:n + 1], nrq[:, n % NT:n % NT + 1], ALU.mult)\
                            .then_inc(shifted.sem, 1)
                    if 1 <= n <= N:
                        m = n - 1
                        dve.wait_ge(exped.sem, exped.at(it * N + m + 1))
                        s.link(nc.vector.reciprocal(stat[:, 3, m:m + 1], stat[:, 2, m:m + 1]))
                        nc.vector.tensor_scalar(pr[:, m % 4, :], pr[:, m % 4, :], stat[:, 3, m:m + 1], None, ALU.mult)\
                            .then_inc(probs.sem, 1)
                    if n >= 4:
                        m = n - 4
                        u, i = m // NT, m % NT
                        dve.wait_ge(summed.sem, summed.at(it * N + m + 1))
                        nc.vector.tensor_scalar(ot[:, u, i * P:(i + 1) * P], k.ps[:, 6 + m % 2, 0:P], bv[:, bass.ds(it * 2 + u, 1)],
                                                None, ALU.add).then_inc(copied.sem, 1)
                assert s.n == 2 * N
                for u in range(2):
                    dve.wait_ge(projected.sem, projected.at(it * 2 + u + 1))
                    for n in range(NT // 2):
                        pair = k.x[:, 2 * n:2 * n + 2, :].rearrange("p i n -> p (i n)")
                        dve.wait_ge(added.sem, added.at(it * 8 + 4 * u + n + 1 - 4))
                        nc.vector.tensor_tensor(pair, pair, k.ps[:, 4 * u + n, :], ALU.add).then_inc(added.sem, 1)
            steps.base += H // 2 * 2 * N

        params.base += 32
        for u in range(2):
            loaded[u].base += 16 * H
        for n in (keys_ready, mixed_made, mixed, v_made, v_copied, projected):
            n.base += H
        for n in (scored, shifted, exped, probs, turned, turned_copied, summed, copied):
            n.base += H * NT
        added.base += 4 * H


def layer_shifted(k):
    norm_stage(k, k.x, k.xn)
    with Stage(k) as st:
        qg, kg = st.sb("qg", [P, H * T]), st.sb("kg", [P, H * T])
        mix, rk, rq = st.sb("mix", [P, P]), st.sb("rk", [P, T]), st.sb("rq", [P, NT])
        shifted_project_stage(k, qg, kg, mix, rk, rq)
        shifted_attention_stage(k, qg, kg, mix, rk, rq)


def differential_stage(k):
    nc, d = k.nc, k.dram
    params, lam_dot, lam_exp = k.count("diff_params"), k.count("diff_dots"), k.count("diff_dot_exps")
    w_loaded, wo_loaded = k.count("diff_w_loaded"), k.count("diff_wo_loaded")
    made, by_act, by_dve = k.freed("diff_made"), k.freed("diff_copied_act"), k.freed("diff_copied_dve")
    scored, shifted, exped, probs = (k.count(n) for n in ("diff_scored", "diff_shift", "diff_exps", "diff_probs"))
    turned, turned_copied = k.count("diff_turned"), k.freed("diff_turned_copied")
    summed, taken = k.freed("diff_summed"), k.freed("diff_taken")
    rows = k.count("diff_rows")
    projected, added = k.freed("diff_projected"), k.freed("diff_added")
    steps, pool_steps = k.count("dve_steps"), k.count("pool_steps")
    G, Q = 4, 6
    N = 2 * NT
    V = 2 * D2
    scale = D2 ** -0.5
    BEHIND = 3
    R = N + BEHIND
    DV = 2 * N + 2 * N
    with Stage(k) as st:
        w = st.sb("w", [P, C * (Q * P + V) + Q])
        wo = st.sb("wo", [P, 4 * D])
        bv = st.sb("bv", [P, V])
        bo = st.sb("bo", [P, D])
        sub = st.sb("sub", [P, C])
        lam_in = st.sb("lam_in", [P, 4, D2])
        lam = st.sb("lam", [P, 4])
        qt = st.sb("qt", [P, 4, T])
        kt = st.sb("kt", [P, 2, T])
        v = st.sb("v", [P, NT, V])
        e = st.sb("e", [P, 2, 2, T])
        pt = st.sb("pt", [P, 2, T])
        o = st.sb("o", [P, N, V])
        square = st.sb("square", [P, 2, V])
        stat = st.sb("stat", [P, 4, 2, N])
        ss = st.sb("ss", [P, 3, N])
        eps = st.sb("eps", [P, 1])
        block = st.block()
        ps = k.ps_flat
        weights = w[:, 0:C * (Q * P + V)].rearrange("p (c n) -> p c n", c=C)
        bias = w[:, C * (Q * P + V):]

        @block.sync
        def _(sp):
            sp.dma_start(bo[:], bc(d["diff_bo"], [P, D])).then_inc(params.sem, 16)
            sp.dma_start(sub[:], d["diff_sub"]).then_inc(params.sem, 16)
            sp.dma_start(lam_in[:], bc(d["diff_lambda"].unsqueeze(0), [P, 4, D2])).then_inc(params.sem, 16)
            with sp.Fori(0, G) as it:
                sp.wait_ge(made.sem, made.at(it * (Q + 1)))
                sp.wait_ge(by_act.sem, by_act.at(it * 3))
                sp.wait_ge(by_dve.sem, by_dve.at(it * 4))
                sp.dma_start(w[:], d["diff_w"][bass.ds(it * P, P), :]).then_inc(w_loaded.sem, 16)
                sp.dma_start(bv[:], bc(d["diff_bv"][bass.ds(it, 1), :], [P, V])).then_inc(w_loaded.sem, 16)
                sp.wait_ge(projected.sem, projected.at(it))
                sp.dma_start(wo[:], d["diff_wo"][bass.ds(it * P, P), :]).then_inc(wo_loaded.sem, 16)

        @block.tensor
        def _(pe):
            with pe.Fori(0, G) as it:
                pe.wait_ge(w_loaded.sem, w_loaded.at(it * 32 + 32))
                for h in range(Q):
                    if h in (2, 3):
                        pe.wait_ge(added.sem, added.at(it * 4 + 2 * (h - 1) - 4))
                    if h == 4:
                        pe.wait_ge(by_act.sem, by_act.at(it * 3 + 1))
                    if h == 5:
                        pe.wait_ge(by_dve.sem, by_dve.at(it * 4 + 1))
                    for n in range(2):
                        for c in range(C):
                            last = nc.tensor.matmul(k.ps[:, (2 * h + 4 + n) % 8, :], weights[:, c, h * P:(h + 1) * P],
                                                    k.xt[:, c, n * BANK:(n + 1) * BANK], start=c == 0, stop=c == C - 1)
                    last.then_inc(made.sem, 1)
                pe.wait_ge(by_act.sem, by_act.at(it * 3 + 2))
                pe.wait_ge(by_dve.sem, by_dve.at(it * 4 + 2))
                for i in range(NT):
                    for c in range(C):
                        last = nc.tensor.matmul(k.ps[:, i // 2, (i % 2) * V:(i % 2 + 1) * V], k.xt[:, c, i * P:(i + 1) * P],
                                                weights[:, c, Q * P:Q * P + V], start=c == 0, stop=c == C - 1)
                last.then_inc(made.sem, 1)
                pe.wait_ge(by_act.sem, by_act.at(it * 3 + 3))
                pe.wait_ge(by_dve.sem, by_dve.at(it * 4 + 4))

                def score(n):
                    u, i = n // NT, n % NT
                    for m in range(2):
                        if n:
                            pe.wait_ge(exped.sem, exped.at(it * (2 * N) + 2 * n - 1 + m))
                        width = (i + 1) * P
                        for col in range(0, width, BANK):
                            x = min(BANK, width - col)
                            nc.tensor.matmul(ps[:, m * T + col:m * T + col + x], qt[:, 2 * u + m, i * P:(i + 1) * P],
                                             kt[:, m, col:col + x], start=True, stop=col + x < width)
                        nc.tensor.matmul(ps[:, m * T + i * P:m * T + (i + 1) * P], k.ident_bf[:], k.mask_q[:],
                                         start=False, stop=True).then_inc(scored.sem, 1)

                def turn(n):
                    i = n % NT
                    pe.wait_ge(probs.sem, probs.at(it * N + n + 1))
                    pe.wait_ge(turned_copied.sem, turned_copied.at(it * N + n))
                    for j in range(i + 1):
                        last = nc.tensor.transpose(ps[:, 4 * BANK + j * P:4 * BANK + (j + 1) * P], e[:, n % 2, 0, j * P:(j + 1) * P],
                                                   k.ident[:])
                    last.then_inc(turned.sem, 1)

                def value(n):
                    i = n % NT
                    pe.wait_ge(taken.sem, taken.at(it * R + n + 1 - 2))
                    if n >= BEHIND:
                        pe.wait_ge(rows.sem, rows.at(it * N + n - BEHIND + 1))
                        for c in range(2):
                            last = nc.tensor.transpose(k.ps[:, 6 + n % 2, V + c * P:V + (c + 1) * P],
                                                       o[:, n - BEHIND, c * P:(c + 1) * P], k.ident[:])
                    if n < N:
                        pe.wait_ge(turned_copied.sem, turned_copied.at(it * N + n + 1))
                        for j in range(i + 1):
                            last = nc.tensor.matmul(k.ps[:, 6 + n % 2, 0:V], pt[:, n % 2, j * P:(j + 1) * P], v[:, j, :],
                                                    start=j == 0, stop=j == i)
                    last.then_inc(summed.sem, 1)

                for n in range(R + 2):
                    if n < N:
                        score(n)
                    if n >= 2:
                        value(n - 2)
                    if 1 <= n <= N:
                        turn(n - 1)
                pe.wait_ge(taken.sem, taken.at(it * R + R))
                pe.wait_ge(wo_loaded.sem, wo_loaded.at(it * 16 + 16))
                for n in range(NT // 2):
                    for i in (2 * n, 2 * n + 1):
                        for ch in range(4):
                            last = nc.tensor.matmul(k.ps[:, n, (i % 2) * D:(i % 2 + 1) * D], qt[:, ch, i * P:(i + 1) * P],
                                                    wo[:, ch * D:(ch + 1) * D], start=ch == 0, stop=ch == 3)
                last.then_inc(projected.sem, 1)

        @block.scalar
        def _(act):
            act.wait_ge(lam_dot.sem, lam_dot.at(1))
            nc.scalar.activation(lam[:, 0:2], lam[:, 0:2], ACT.Exp).then_inc(lam_exp.sem, 1)
            act.wait_ge(lam_dot.sem, lam_dot.at(2))
            with act.Fori(0, G) as it:
                for h in (0, 2, 4):
                    act.wait_ge(made.sem, made.at(it * (Q + 1) + h + 1))
                    dst = qt[:, h, :] if h < 4 else kt[:, h - 4, :]
                    bank = (2 * h + 4) % 8 * BANK
                    nc.scalar.activation(dst, ps[:, bank:bank + T], ACT.Identity, bias=bias[:, h:h + 1]).then_inc(by_act.sem, 1)
                for n in range(R + 2):
                    i = n % NT
                    if n < N:
                        for m in range(2):
                            act.wait_ge(shifted.sem, shifted.at(it * (2 * N) + 2 * n + m + 1))
                            if m == 0 and n >= 2:
                                act.wait_ge(turned.sem, turned.at(it * N + n - 1))
                            width = (i + 1) * P
                            nc.scalar.activation(e[:, n % 2, m, 0:width], ps[:, m * T:m * T + width], ACT.Exp,
                                                 bias=stat[:, 1, m, n:n + 1], scale=scale, accum_out=stat[:, 2, m, n:n + 1])\
                                .then_inc(exped.sem, 1)
                    if n >= 2:
                        m = n - 2
                        act.wait_ge(summed.sem, summed.at(it * R + m + 1))
                        if m >= BEHIND:
                            u, tile = divmod(m - BEHIND, NT)
                            for c in range(2):
                                last = nc.scalar.activation(qt[:, 2 * u + c, tile * P:(tile + 1) * P],
                                                            k.ps[:, 6 + m % 2, V + c * P:V + (c + 1) * P], ACT.Copy,
                                                            scale=sub[:, c:c + 1])
                        if m < N:
                            if m >= 2:
                                act.wait_ge(taken.sem, taken.at(it * R + m + 1 - 2))
                            nc.scalar.activation(o[:, m, :], k.ps[:, 6 + m % 2, 0:V], ACT.Copy, scale=stat[:, 3, 0, m:m + 1])
                            last = nc.scalar.activation(square[:, m % 2, :], k.ps[:, 6 + m % 2, 0:V], ACT.Square,
                                                        scale=stat[:, 3, 0, m:m + 1], accum_out=ss[:, 0, m:m + 1])
                        last.then_inc(taken.sem, 1)
                    if 1 <= n <= N:
                        m = n - 1
                        width = (m % NT + 1) * P
                        act.wait_ge(turned.sem, turned.at(it * N + m + 1))
                        if m >= 2:
                            act.wait_ge(summed.sem, summed.at(it * R + m + 1 - 2))
                        nc.scalar.copy(pt[:, m % 2, 0:width], ps[:, 4 * BANK:4 * BANK + width]).then_inc(turned_copied.sem, 1)

        @block.vector
        def _(dve):
            s = Steps(dve, steps)
            dve.wait_ge(params.sem, params.at(48))
            for n in range(2):
                s.link(nc.vector.tensor_tensor(lam_in[:, 2 * n, :], lam_in[:, 2 * n, :], lam_in[:, 2 * n + 1, :], ALU.mult))
            s.mark(nc.vector.reduce_sum(lam[:, 0:1], lam_in[:, 0, :], X_AXIS))
            nc.vector.reduce_sum(lam[:, 1:2], lam_in[:, 2, :], X_AXIS).then_inc(lam_dot.sem, 1)
            dve.wait_ge(lam_exp.sem, lam_exp.at(1))
            s.link(nc.vector.tensor_tensor(lam[:, 2:3], lam[:, 1:2], lam[:, 0:1], ALU.subtract))
            s.link(nc.vector.tensor_scalar(lam[:, 3:4], lam[:, 2:3], -LAMBDA_INIT, None, ALU.add))
            nc.vector.tensor_scalar(sub[:], sub[:], (1.0 - LAMBDA_INIT) * V ** 0.5, None, ALU.mult).then_inc(lam_dot.sem, 1)
            s.link(nc.vector.tensor_tensor(k.x[:], k.x[:], bc(bo[:].unsqueeze(1), [P, NT, D]), ALU.add))
            steps.base += s.n
            with dve.Fori(0, G) as it:
                s = Steps(dve, steps, it * DV)
                dve.wait_ge(w_loaded.sem, w_loaded.at(it * 32 + 32))
                for h in (1, 3, 5):
                    dve.wait_ge(made.sem, made.at(it * (Q + 1) + h + 1))
                    dst = qt[:, h, :] if h < 4 else kt[:, h - 4, :]
                    bank = (2 * h + 4) % 8 * BANK
                    nc.vector.tensor_scalar(dst, ps[:, bank:bank + T], bias[:, h:h + 1], None, ALU.add).then_inc(by_dve.sem, 1)
                dve.wait_ge(made.sem, made.at(it * (Q + 1) + Q + 1))
                nc.vector.tensor_tensor(v[:], ps[:, 0:4 * BANK].rearrange("p (i n) -> p i n", n=V),
                                        bc(bv[:].unsqueeze(1), [P, NT, V]), ALU.add).then_inc(by_dve.sem, 1)
                for n in range(N + 1):
                    if n >= 1:
                        m = n - 1
                        width = (m % NT + 1) * P
                        first, second = e[:, m % 2, 0, 0:width], e[:, m % 2, 1, 0:width]
                        dve.wait_ge(exped.sem, exped.at(it * (2 * N) + 2 * m + 2))
                        s.link(nc.vector.reciprocal(stat[:, 3, :, m], stat[:, 2, :, m]))
                        s.link(nc.vector.scalar_tensor_tensor(stat[:, 3, 1, m:m + 1], stat[:, 3, 1, m:m + 1], lam[:, 3:4],
                                                              stat[:, 2, 0, m:m + 1], ALU.mult, ALU.mult))
                        nc.vector.scalar_tensor_tensor(first, second, stat[:, 3, 1, m:m + 1], first, ALU.mult, ALU.add)\
                            .then_inc(probs.sem, 1)
                    if n < N:
                        width = (n % NT + 1) * P
                        for m in range(2):
                            dve.wait_ge(scored.sem, scored.at(it * (2 * N) + 2 * n + m + 1))
                            s.link(nc.vector.reduce_max(stat[:, 0, m, n:n + 1], ps[:, m * T:m * T + width], X_AXIS))
                            nc.vector.tensor_scalar(stat[:, 1, m, n:n + 1], stat[:, 0, m, n:n + 1], -scale, None, ALU.mult)\
                                .then_inc(shifted.sem, 1)
                assert s.n == DV, s.n
                dve.wait_ge(projected.sem, projected.at(it + 1))
                for n in range(NT // 2):
                    pair = k.x[:, 2 * n:2 * n + 2, :].rearrange("p i n -> p (i n)")
                    dve.wait_ge(added.sem, added.at(it * 4 + n + 1 - 4))
                    nc.vector.tensor_tensor(pair, pair, k.ps[:, n, :], ALU.add).then_inc(added.sem, 1)
            steps.base += G * DV

        @block.gpsimd
        def _(pool):
            s = Steps(pool, pool_steps)
            s.link(nc.gpsimd.memset(eps[:], V * EPS))
            pool_steps.base += s.n
            with pool.Fori(0, G) as it:
                s = Steps(pool, pool_steps, it * (2 * N))
                for n in range(N):
                    pool.wait_ge(taken.sem, taken.at(it * R + n + 1))
                    s.link(nc.gpsimd.tensor_tensor(ss[:, 1, n:n + 1], ss[:, 0, n:n + 1], eps[:], ALU.add))
                    s.link(nc.gpsimd.tensor_tensor(ss[:, 2, n:n + 1], ss[:, 1, n:n + 1], k.minus_half[:, 0:1], ALU.pow))
                    nc.gpsimd.tensor_tensor(o[:, n, :], o[:, n, :], bc(ss[:, 2, n:n + 1], [P, V]), ALU.mult)\
                        .then_inc(rows.sem, 1)
            pool_steps.base += G * 2 * N

        params.base += 48
        lam_dot.base += 2
        lam_exp.base += 1
        w_loaded.base += 32 * G
        wo_loaded.base += 16 * G
        made.base += (Q + 1) * G
        by_act.base += 3 * G
        by_dve.base += 4 * G
        for n in (scored, shifted, exped):
            n.base += 2 * N * G
        for n in (probs, turned, turned_copied, rows):
            n.base += N * G
        for n in (summed, taken):
            n.base += R * G
        projected.base += G
        added.base += 4 * G


def layer_differential(k):
    norm_stage(k, k.x, k.xn)
    differential_stage(k)


def program(nc, dram, out, layers):
    with ExitStack() as ctx:
        k = Kernel(nc, ctx, dram)
        sb = lambda name, shape, dt=F32: ctx.enter_context(nc.sbuf_tensor(name, shape, dt))
        k.ps = ctx.enter_context(nc.psum_tensor("ps", [P, 8, BANK], F32))
        k.ps_flat = k.ps[:].rearrange("p b n -> p (b n)")
        k.x, k.xn, k.xt = sb("x", [P, NT, D]), sb("xn", [P, NT, D]), sb("xt", [P, C, T])
        k.ident, k.ones = sb("ident", [P, P]), sb("ones", [P, P])
        k.ident_bf, k.ones_bf, k.before_bf = (sb(n, [P, P], BF16) for n in ("ident_bf", "ones_bf", "before_bf"))
        k.mask_q, k.mask_k, k.mask_band = sb("mask_q", [P, P], BF16), sb("mask_k", [P, P], BF16), sb("mask_band", [P, BAND], BF16)
        k.zero = sb("zero", [P, SLOTS * D // P // ZERO_DMAS])
        k.zero_bf = sb("zero_bf", [P, BANK], BF16)
        k.iota, k.sel, k.minus_half = sb("iota", [P, 2, E0]), sb("sel", [H, C, P]), sb("minus_half", [P, 2 * NT])
        for name in FREED:
            k.freed(name)
        constants_stage(k)
        for layer in layers:
            LAYERS[layer](k)
        stored = k.count("output_stored")
        with Stage(k) as st:
            block = st.block()

            @block.sync
            def _(sp):
                sp.dma_start(out.rearrange("(i p) n -> p i n", p=P), k.x[:]).then_inc(stored.sem, 16)
                sp.wait_ge(stored.sem, 16)


def layer_mha(k):
    norm_stage(k, k.x, k.xn)
    small_attention(k, "mha", k.x)


def layer_mqa(k):
    norm_stage(k, k.x, k.xn)
    small_attention(k, "mqa", k.x)


FREED = ["max_scores_freed", "value_products", "head_copied", "expert_rows", "expert_hidden", "expert_down", "expert_copied",
         "row_added", "dense_hidden", "dense_down", "dense_added", "qk_products", "qk_squared", "qk_scaled",
         "band_turned_copied", "band_summed", "band_copied", "band_projected", "band_added",
         "diff_made", "diff_copied_act", "diff_copied_dve", "diff_turned_copied", "diff_summed", "diff_taken",
         "diff_projected", "diff_added", "head_stored_0", "head_stored_1", "expert_stored_0", "expert_stored_1",
         "qk_summed"]
LAYERS = {"mha": layer_mha, "mqa": layer_mqa, "moe": layer_moe, "mla": layer_mla,
          "shifted": layer_shifted, "differential": layer_differential}


def constant_arrays():
    f = np.float32
    r = np.arange(P)
    square = np.concatenate([np.eye(P), np.where(r[None, :] > r[:, None], MASKED, 0.0),
                             np.where(r[None, :] < r[:, None], MASKED, 0.0), np.ones((P, P)),
                             (r[:, None] < r[None, :]) * 1.0], axis=1).astype(f)
    away = r[:, None] + PAD_L - np.arange(BAND)[None, :]
    band = np.where(np.isin(away, SHIFTS), 0.0, MASKED).astype(f)
    iota = np.stack([np.broadcast_to(np.arange(E0), (P, E0)), np.broadcast_to(np.arange(E0) * CAP, (P, E0))], axis=1).astype(f)
    sel = (np.arange(D)[None, :] // HD == np.arange(H)[:, None]).astype(f).reshape(H, C, P)
    rd = HD // 2
    perm = np.zeros((P, P), f)
    for h in range(H):
        for j in range(rd // 2):
            perm[h * rd + rd // 2 + j, h * rd + j] = -1.0
            perm[h * rd + j, h * rd + rd // 2 + j] = 1.0
    inv = (1.0 / f(10000.0) ** (np.arange(0, rd, 2, dtype=f) / f(rd))).astype(f)
    ang = np.outer(np.arange(T, dtype=f), inv).astype(f)
    row = np.arange(P) % (rd // 2)
    roll = np.stack([np.roll(np.eye(P), s, axis=1) for s in ROLLS], axis=1).astype(f)
    return {"c_square": square, "c_band": band, "c_iota": np.ascontiguousarray(iota), "c_sel": sel, "c_perm": perm,
            "c_cos": np.cos(ang).T[row].astype(f), "c_sin": np.sin(ang).T[row].astype(f), "c_roll": roll}


def lay_out(a):
    g = {n: np.asarray(v) for n, v in a.items()}
    cut = lambda w: w.reshape(-1, P, w.shape[-1]).transpose(1, 0, 2)
    col = lambda b: b.reshape(-1, P).T
    o = {"x": g["L0_attn_a_x"].reshape(T, D)}
    p = "L0_attn_a_"
    o["mha_w"] = cut(np.concatenate([g[p + n].transpose(1, 0, 2).reshape(D, D) for n in ("Wq", "Wk", "Wv")], axis=1))
    o["mha_bqk"] = np.concatenate([col(g[p + "bq"].reshape(-1)), col(g[p + "bk"].reshape(-1))], axis=1)
    o["mha_bv"] = g[p + "bv"].reshape(1, D)
    o["mha_wo"], o["mha_bo"] = cut(g[p + "Wo"]), g[p + "bo"].reshape(1, D)
    p = "L1_attn_a_"
    b = g[p + "b_qkv"]
    o["mqa_w"] = cut(g[p + "w_qkv"])
    bk = np.zeros((P, 2), np.float32)
    bk[0:HD, 0] = b[D:D + HD]
    o["mqa_bqk"] = np.concatenate([col(b[0:D]), bk], axis=1)
    o["mqa_bv"] = b[D + HD:].reshape(1, HD)
    o["mqa_wo"], o["mqa_bo"] = cut(g[p + "w_fc"]), g[p + "b_fc"].reshape(1, D)
    p = "L1_ffn_"
    o["mla_down"] = cut(np.concatenate([g[p + "kv_d_w"], g[p + "q_d_w"]], axis=1))
    o["mla_rk"] = cut(g[p + "rope_k_w"])
    o["mla_lat"] = np.concatenate([g[p + n] for n in ("k_u_w", "q_u_w", "rope_q_w", "v_u_w")], axis=1)
    o["mla_wo"] = cut(g[p + "o_w"])
    o["ln1"], o["ln2"] = col(g[p + "ln1_w"]), col(g[p + "ln2_w"])
    lay_out_more(g, o, cut, col)
    return {n: np.ascontiguousarray(v) for n, v in o.items()}


def lay_out_more(g, o, cut, col):
    p = "L0_ffn_"
    o["moe_router"] = cut(g[p + "wg_router"].T)
    gu = np.stack([g[p + "w_gate"], g[p + "w_up"]], axis=1)
    o["expert_w_in"] = gu.reshape(E0, 2, C, P, F0).transpose(0, 3, 1, 2, 4).reshape(E0 * P, 2 * C * F0)
    o["expert_w_out"] = g[p + "w_down"].reshape(E0, 2, FH, D).transpose(0, 2, 1, 3).reshape(E0 * FH, 2 * D)
    gu = np.stack([g[p + "ws_gate"], g[p + "ws_up"]])
    o["shared_in"] = gu.reshape(2, C, P, FS).transpose(2, 0, 1, 3)
    o["shared_out"] = g[p + "ws_down"].reshape(NS, FH, D).transpose(1, 0, 2)
    p = "L0_attn_b_"
    head = lambda w: w.reshape(H, D2, C, P).transpose(0, 3, 2, 1)
    o["shifted_w_qk"] = np.stack([head(g[p + "wq"]), head(g[p + "wk"])], axis=2).reshape(H * P, 2 * C * P)
    o["shifted_bg"] = np.stack([np.stack([col(g[p + b]), col(g[p + n])], axis=1) for b, n in (("bq", "gq"), ("bk", "gk"))], axis=1)
    o["shifted_mix"] = g[p + "w_mix"]
    o["shifted_w_v"] = head(g[p + "wv"]).reshape(H * P, C * P)
    o["shifted_wo"] = g[p + "wo"].T
    o["shifted_bv"], o["shifted_bo"] = col(g[p + "bv"]), g[p + "bo"].reshape(1, D)
    p = "L1_attn_b_"
    w, b = g[p + "Wqkv_w"], g[p + "Wqkv_b"]
    qw, kw, vw = (x.reshape(4, -1, D) for x in (w[0:2048], w[2048:3072], w[3072:4096]))
    qb, kb, vb = (x.reshape(4, -1) for x in (b[0:2048], b[2048:3072], b[3072:4096]))
    ww = np.concatenate([qw, kw, vw], axis=1).reshape(4, -1, C, P).transpose(0, 3, 2, 1).reshape(4, P, -1)
    bb = np.concatenate([qb, kb], axis=1).reshape(4, -1, P).transpose(0, 2, 1)
    o["diff_w"] = np.concatenate([ww, bb], axis=2).reshape(4 * P, -1)
    o["diff_bv"] = vb
    o["diff_wo"] = g[p + "out_w"].T.reshape(4, 4, P, D).transpose(0, 2, 1, 3).reshape(4 * P, 4 * D)
    o["diff_bo"], o["diff_sub"] = g[p + "out_b"].reshape(1, D), col(g[p + "subln_w"])
    o["diff_lambda"] = np.stack([g[p + n] for n in ("lambda_q1", "lambda_k1", "lambda_q2", "lambda_k2")])
    p = "L1_ffn_"
    o["gate_router"], o["gate_bias"] = cut(g[p + "router_w"]), g[p + "router_b"].reshape(1, E1 - 1)
    gate = np.concatenate([g[p + "sh_gate"][None], g[p + "r_gate"]])
    up = np.concatenate([g[p + "sh_up"][None], g[p + "r_up"]])
    down = np.concatenate([g[p + "sh_down"][None], g[p + "r_down"]])
    o["dense_w_in"] = np.stack([gate, up], axis=1).reshape(E1, 2, C, P, I1).transpose(0, 3, 1, 2, 4).reshape(E1 * P, 2 * C * I1)
    o["dense_w_out"] = down.reshape(E1 * I1, D)


SCRATCH = {"q_parts": ([3, HD, H, T], BF16), "k_parts": ([3, HD, H, T], BF16), "head_out": ([D, T], F32), "head_sum": ([H, T], F32),
           "expert_in": ([SLOTS, D], F32), "expert_out": ([SLOTS, D], F32)}


def kernel(**inputs):
    import concourse.bacc as bacc
    from concourse.bass_utils import run_bass_kernel_spmd

    nc = bacc.Bacc("TRN2", target_bir_lowering=False, num_devices=1)
    arrays = {**lay_out(inputs), **constant_arrays()}
    dram = {n: nc.dram_tensor(f"in_{n}", a.shape, mybir.dt.from_np(a.dtype), kind="ExternalInput").ap() for n, a in arrays.items()}
    for name, (shape, dt) in SCRATCH.items():
        dram[name] = nc.dram_tensor(f"scratch_{name}", shape, dt, kind="Internal").ap()
    out = nc.dram_tensor("out_x", [T, D], F32, kind="ExternalOutput").ap()
    program(nc, dram, out, SEQUENCE)
    r = run_bass_kernel_spmd(nc, [{f"in_{n}": a for n, a in arrays.items()}], core_ids=[0])
    return r.results[0]["out_x"].reshape(1, T, D)


SEQUENCE = ["mha", "moe", "shifted", "moe", "mqa", "mla", "differential", "mla"]
```

```python
from contextlib import ExitStack
import math

import numpy as np

import concourse.bass as bass
from concourse import mybir

F32 = mybir.dt.float32
BF16 = mybir.dt.bfloat16
U32 = mybir.dt.uint32
I32 = mybir.dt.int32
ALU = mybir.AluOpType
ACT = mybir.ActivationFunctionType
X_AXIS = mybir.AxisListType.X

P = 128
T = 1024
NT = T // P
D = 256
C = D // P
H = 16
HD = 16
BANK = 512
MASKED = -1.0e30
MAXIMA_PACE = 1.6

PAIRS = [(0, 0), (0, 1), (0, 2), (1, 0), (1, 1), (2, 0)]
ROWS = len(PAIRS) * HD
ROWS_M = ROWS + 3

E0, F0, K0 = 32, 176, 6
FH = F0 // 2
CAP = 2 * (T * K0 // E0)
CT = CAP // P
SLOTS = E0 * CAP
FS = 2 * F0
NS = FS // FH
DROPPED = 65536.0

D2 = 128
SHIFTS = [0, 1, -1, 2, -2, 4, -4, 8, -8, 16, -16, 32, -32, 64, -64, 128]
ROLLS = [0, 1, 2, 4, 8]
PAD_L, PAD_R = 128, 64
BAND = PAD_L + P + PAD_R
EPS = 1e-5
EPS_SHIFTED = 1e-6

E1, K1, I1 = 8, 2, 128
LAT = 64
LAMBDA_INIT = 0.8 - 0.6 * math.exp(-0.3)

BUSY_NORM, BUSY_EXPERTS = 25, 25
CREDIT = 32


class Count:

    def __init__(self, sem, base=0):
        self.sem, self.base = sem, base

    def at(self, n):
        return n + self.base


class Kernel:

    def __init__(self, nc, ctx, dram):
        self.nc, self.ctx, self.dram, self.counts, self.serial = nc, ctx, dram, {}, 0
        self.credited = []
        self.bn_made = False

    def count(self, name):
        if name not in self.counts:
            self.counts[name] = Count(self.ctx.enter_context(self.nc.semaphore(name)))
        return self.counts[name]

    def freed(self, name):
        if name not in self.counts:
            c = self.count(name)
            c.base = CREDIT
            self.credited.append(c)
        return self.counts[name]


class Stage:

    def __init__(self, k):
        self.k, self.ctx = k, ExitStack()

    def __enter__(self):
        self.ctx.__enter__()
        self.k.serial += 1
        return self

    def __exit__(self, *a):
        return self.ctx.__exit__(*a)

    def sb(self, name, shape, dt=F32):
        return self.ctx.enter_context(self.k.nc.sbuf_tensor(f"{name}_{self.k.serial}", shape, dt))

    def block(self):
        return self.ctx.enter_context(self.k.nc.Block())


class Steps:

    def __init__(self, eng, count, offset=0):
        self.eng, self.count, self.offset, self.n = eng, count, offset, 0

    def mark(self, ins):
        ins.then_inc(self.count.sem, 1)
        self.n += 1
        return self.n

    def wait(self, n=None):
        self.eng.wait_ge(self.count.sem, self.count.at(self.offset + (self.n if n is None else n)))

    def link(self, ins):
        self.mark(ins)
        self.wait()


def bc(ap, shape):
    return ap.broadcast_to(shape)


def keep_busy(k, matmuls, bank=7):
    for _ in range(matmuls):
        k.nc.tensor.matmul(k.ps[:, bank, 0:BAND], k.ident_bf[:], k.mask_band[:], start=True, stop=True)


def constants_stage(k):
    nc, d = k.nc, k.dram
    loaded, late = k.count("constants_loaded"), k.count("late_constants")
    with Stage(k) as st:
        raw = st.sb("raw", [P, 5 * P])
        raw_band = st.sb("raw_band", [P, BAND])
        block = st.block()

        @block.sync
        def _(sp):
            sp.dma_start(k.x[:], d["x"].rearrange("(i p) n -> p i n", p=P)).then_inc(loaded.sem, 16)
            sp.dma_start(raw[:], d["c_square"]).then_inc(loaded.sem, 16)
            sp.dma_start(raw_band[:], d["c_band"]).then_inc(loaded.sem, 16)
            sp.dma_start(k.iota[:], d["c_iota"]).then_inc(late.sem, 16)
            sp.dma_start(k.sel[:], d["c_sel"]).then_inc(late.sem, 16)
            sp.wait_ge(loaded.sem, 48)

        @block.gpsimd
        def _(pool):
            nc.gpsimd.memset(k.minus_half[:], -0.5)
            for c in k.credited:
                pool.sem_inc(c.sem, CREDIT)

        @block.vector
        def _(dve):
            dve.wait_ge(loaded.sem, 48)
            nc.vector.tensor_copy(k.ident[:], raw[:, 0:P])
            nc.vector.tensor_copy(k.ident_bf[:], raw[:, 0:P])
            nc.vector.tensor_copy(k.mask_q[:], raw[:, P:2 * P])
            nc.vector.tensor_copy(k.mask_k[:], raw[:, 2 * P:3 * P])
            nc.vector.tensor_copy(k.ones[:], raw[:, 3 * P:4 * P])
            nc.vector.tensor_copy(k.ones_bf[:], raw[:, 3 * P:4 * P])
            nc.vector.tensor_copy(k.before_bf[:], raw[:, 4 * P:5 * P])
            nc.vector.tensor_copy(k.mask_band[:], raw_band[:])


def norm_stage(k, src, nat, rms_weight=None, layernorm=True, preload=None):
    nc = k.nc
    stats, spread, rows = k.count("norm_stats"), k.count("norm_spread"), k.count("norm_rows")
    turned, weight = k.count("norm_turned"), k.count("norm_weight")
    steps = k.count("dve_steps")
    rms = rms_weight is not None
    roots = 2 * int(layernorm) + int(rms)
    halves = [range(0, NT // 2), range(NT // 2, NT)]
    with Stage(k) as st:
        bn = k.bn
        mv = st.sb("mv", [P, NT, 2])
        base = st.sb("base", [P, 2, NT])
        scale = st.sb("scale", [P, 2, NT])
        second = st.sb("second", [P, NT])
        scaled = st.sb("scaled", [P, NT, D]) if rms else nat
        w = st.sb("w", [P, C]) if rms else None
        block = st.block()

        @block.sync
        def _(sp):
            if rms:
                sp.dma_start(w[:], rms_weight).then_inc(weight.sem, 16)
            if preload:
                preload(sp)

        @block.vector
        def _(dve):
            s = Steps(dve, steps)
            for half in halves:
                if not k.bn_made:
                    for i in half:
                        s.mark(nc.vector.bn_stats(bn[:, i, :], src[:, i, :]))
                    s.wait()
                for i in half:
                    s.mark(nc.vector.bn_aggr(mv[:, i, :], bn[:, i, :]))
                s.wait()
                if layernorm:
                    tiles = slice(half.start, half.stop)
                    nc.vector.tensor_scalar(base[:, 0, tiles], mv[:, tiles, 1], EPS, None, ALU.add).then_inc(stats.sem, 1)
            if layernorm:
                for i in range(NT):
                    if i % (NT // 2) == 0:
                        dve.wait_ge(spread.sem, spread.at(1 + i // (NT // 2)))
                    last = nc.vector.tensor_scalar(nat[:, i, :], src[:, i, :], mv[:, i, 0:1], scale[:, 0, i:i + 1],
                                                   ALU.subtract, ALU.mult)
                    if rms:
                        s.mark(last)
                    else:
                        last.then_inc(rows.sem, 1)
            if rms:
                if layernorm:
                    s.link(nc.vector.tensor_tensor(second[:], mv[:, :, 1], scale[:, 0, :], ALU.mult))
                    s.link(nc.vector.tensor_tensor(second[:], second[:], scale[:, 0, :], ALU.mult))
                else:
                    s.link(nc.vector.tensor_tensor(second[:], mv[:, :, 0], mv[:, :, 0], ALU.mult))
                    s.link(nc.vector.tensor_tensor(second[:], second[:], mv[:, :, 1], ALU.add))
                nc.vector.tensor_scalar(base[:, 1, :], second[:], EPS, None, ALU.add).then_inc(stats.sem, 1)
                dve.wait_ge(spread.sem, spread.at(roots))
                for i in range(NT):
                    nc.vector.tensor_scalar(scaled[:, i, :], (nat if layernorm else src)[:, i, :], scale[:, 1, i:i + 1],
                                            None, ALU.mult).then_inc(rows.sem, 1)
                dve.wait_ge(weight.sem, weight.at(16))
            for n in (1, 3):
                dve.wait_ge(turned.sem, turned.at(n + 1))
                out, bank = k.xt[:, n % 2, (n // 2) * BANK:(n // 2 + 1) * BANK], k.ps[:, n, :]
                if rms:
                    nc.vector.tensor_scalar(out, bank, w[:, 1:2], None, ALU.mult)
                else:
                    nc.vector.tensor_copy(out, bank)
            steps.base += s.n
            k.bn_made = False

        @block.scalar
        def _(act):
            if rms:
                act.wait_ge(weight.sem, weight.at(16))
            for n in (0, 2):
                act.wait_ge(turned.sem, turned.at(n + 1))
                out, bank = k.xt[:, n % 2, (n // 2) * BANK:(n // 2 + 1) * BANK], k.ps[:, n, :]
                if rms:
                    nc.scalar.activation(out, bank, ACT.Copy, scale=w[:, 0:1])
                else:
                    nc.scalar.copy(out, bank)

        @block.gpsimd
        def _(pool):
            for n in range(roots):
                pool.wait_ge(stats.sem, stats.at(n + 1))
                if n:
                    pool.wait_ge(spread.sem, spread.at(n))
                g = 0 if n < 2 * int(layernorm) else 1
                tiles = slice(n * NT // 2, (n + 1) * NT // 2) if g == 0 else slice(0, NT)
                nc.gpsimd.tensor_tensor(scale[:, g, tiles], base[:, g, tiles], k.minus_half[:, tiles], ALU.pow).then_inc(spread.sem, 1)

        @block.tensor
        def _(pe):
            keep_busy(k, BUSY_NORM)
            for half in range(2):
                for c in range(C):
                    for j in range(4):
                        i = 4 * half + j
                        pe.wait_ge(rows.sem, rows.at(i + 1))
                        last = nc.tensor.transpose(k.ps[:, 2 * half + c, j * P:(j + 1) * P],
                                                   scaled[:, i, c * P:(c + 1) * P], k.ident[:])
                    last.then_inc(turned.sem, 1)

        stats.base += roots
        spread.base += roots
        rows.base += NT
        turned.base += 4
        weight.base += 16 * int(rms)


def stack_pair(k, kind, sp, pair, qs, ks, stacked):
    cols = bass.ds(pair * (2 * T), 2 * T)
    row = 0
    for part in range(3):
        again = (3 - part) * HD
        src = k.dram["q_parts"][part, :, bass.ds(pair * 2, 2), :].rearrange("d h t -> d (h t)")
        sp.dma_start(qs[row:row + again, cols], bc(src.unsqueeze(0), [3 - part, HD, 2 * T])).then_inc(stacked.sem, 16)
        if kind != "mqa":
            src = k.dram["k_parts"][0:3 - part, :, bass.ds(pair * 2, 2), :].rearrange("j d h t -> (j d) (h t)")
            sp.dma_start(ks[row:row + again, cols], src).then_inc(stacked.sem, 16)
        row += again


def stacked_per_pair(kind):
    return 16 * 3 * (1 if kind == "mqa" else 2)


class SmallWeights:

    def __init__(self, k, kind, st):
        self.k, self.kind = k, kind
        if kind == "mla":
            self.down = st.sb("w_down", [P, C, 2 * LAT])
            self.rk = st.sb("w_rk", [P, C, P])
            self.lat = st.sb("w_lat", [LAT, 3 * P + D])
            self.perm = st.sb("perm", [P, P])
            self.cos = st.sb("cos", [P, T])
            self.sin = st.sb("sin", [P, T])
            self.n_loads = 6
        else:
            self.w_in = st.sb("w_in", [P, C, 3 * D if kind == "mha" else D + 2 * HD])
            self.b_qk = st.sb("b_qk", [P, 4])
            self.b_v = st.sb("b_v", [P, D if kind == "mha" else HD])
            self.n_loads = 3

    def load(self, sp):
        d, kind, loaded = self.k.dram, self.kind, self.k.count("small_weights")
        if kind == "mla":
            for tile, name in ((self.down, "mla_down"), (self.rk, "mla_rk"), (self.lat, "mla_lat"), (self.perm, "c_perm"),
                               (self.cos, "c_cos"), (self.sin, "c_sin")):
                sp.dma_start(tile[:], d[name]).then_inc(loaded.sem, 16)
        else:
            sp.dma_start(self.w_in[:], d[kind + "_w"]).then_inc(loaded.sem, 16)
            sp.dma_start(self.b_qk[:], d[kind + "_bqk"]).then_inc(loaded.sem, 16)
            sp.dma_start(self.b_v[:], bc(d[kind + "_bv"], list(self.b_v.shape))).then_inc(loaded.sem, 16)


def small_projections(k, kind, weights, qf, kf, v, qs, ks):
    nc, d = k.nc, k.dram
    loaded, made, evac = k.count("small_weights"), k.count("small_products"), k.count("small_copied")
    rooms, swapped, turned = k.count("small_turned"), k.count("rotary_swapped"), k.count("rotary_turned")
    by_act, by_dve = k.count("operand_by_act"), k.count("operand_by_dve")
    first, second, third, rest = (k.count(n) for n in ("part_0", "part_1", "part_2", "part_rest"))
    stored, stacked, shared_stacked = k.count("parts_stored"), k.count("parts_stacked"), k.count("shared_stacked")
    late_stored = k.count("late_parts_stored")
    k_rows = HD if kind == "mqa" else P
    if kind == "mla":
        units = [("k", 0, evac, 4), ("q", 0, evac, 5), ("k", 1, by_dve, 1), ("q", 1, by_dve, 2)]
    else:
        units = [("q", 0, by_dve, 1), ("k", 0, by_act, 1), ("q", 1, by_dve, 2), ("k", 1, by_act, 2)][:3 if kind == "mqa" else 4]
    U = len(units)
    EARLY = U if kind == "mla" else 2
    scale = HD ** -0.5
    with Stage(k) as st:
        if kind == "mla":
            w_down, w_rk, w_lat, perm, cos, sin = weights.down, weights.rk, weights.lat, weights.perm, weights.cos, weights.sin
            lat = st.sb("lat", [LAT, 2, T])
            raw = st.sb("raw", [P, 2, T])
            turn = st.sb("turn", [P, 2, T])
        else:
            w_in, b_qk, b_v = weights.w_in, weights.b_qk, weights.b_v
        n_loads = weights.n_loads
        parts = {"q": [st.sb(f"q{j}", [P, C, T], BF16) for j in range(3)],
                 "k": [st.sb(f"k{j}", [k_rows, 1 if kind == "mqa" else C, T], BF16) for j in range(3)]}
        left = {"q": st.sb("qr", [P, C, T]), "k": st.sb("kr", [k_rows, 1 if kind == "mqa" else C, T])}
        whole = {"q": qf, "k": kf}
        block = st.block()
        ps = k.ps
        rows_of = lambda side: P if side == "q" else k_rows

        def part_0(n):
            side, c, there, value = units[n]
            nc.scalar.wait_ge(there.sem, there.at(value))
            nc.scalar.copy(parts[side][0][:, c, :], whole[side][0:rows_of(side), c, :]).then_inc(first.sem, 1)

        def part_1(n):
            side, c, _, _ = units[n]
            nc.scalar.wait_ge(rest.sem, rest.at(n + 1))
            nc.scalar.copy(parts[side][1][:, c, :], left[side][:, c, :]).then_inc(second.sem, 1)

        def remainder(n):
            side, c, _, _ = units[n]
            nc.vector.wait_ge(first.sem, first.at(n + 1))
            nc.vector.tensor_tensor(left[side][:, c, :], whole[side][0:rows_of(side), c, :], parts[side][0][:, c, :],
                                    ALU.subtract).then_inc(rest.sem, 1)

        def part_2(n):
            side, c, _, _ = units[n]
            nc.vector.wait_ge(second.sem, second.at(n + 1))
            nc.vector.tensor_tensor(parts[side][2][:, c, :], left[side][:, c, :], parts[side][1][:, c, :],
                                    ALU.subtract).then_inc(third.sem, 1)

        def store_part(eng, n, j):
            side, c, _, _ = units[n]
            rows = rows_of(side)
            size = HD // 2 if kind == "mla" else HD
            heads = rows // size
            dim, head = (c * size, 0) if kind == "mla" else (0, c * heads)
            done = (first, second, third)[j]
            eng.wait_ge(done.sem, done.at(n + 1))
            eng.dma_start(d[side + "_parts"][j, dim:dim + size, head:head + heads, :].rearrange("d h t -> h d t"),
                          parts[side][j][:, c, :]).then_inc((stored if n < EARLY else late_stored).sem, 16)

        @block.sync
        def _(sp):
            for n in range(EARLY):
                for j in range(3):
                    store_part(sp, n, j)
            sp.wait_ge(stored.sem, stored.at(48 * EARLY))
            if kind == "mqa":
                row = 0
                for part in range(3):
                    again = (3 - part) * HD
                    sp.dma_start(ks[row:row + again, :], d["k_parts"][0:3 - part, :, 0, :].rearrange("j d t -> (j d) t"))\
                        .then_inc(shared_stacked.sem, 16)
                    row += again
            stack_pair(k, kind, sp, 0, qs, ks, stacked)
            if EARLY < U:
                sp.wait_ge(late_stored.sem, late_stored.at(48 * (U - EARLY)))

        if kind == "mla":
            @block.tensor
            def _(pe):
                pe.wait_ge(loaded.sem, loaded.at(16 * n_loads))
                def product(bank, rows, parts):
                    for n in range(2):
                        for c, (weight, tile) in enumerate(parts):
                            last = nc.tensor.matmul(ps[0:rows, bank + n, :], weight, tile[:, n * BANK:(n + 1) * BANK],
                                                    start=c == 0, stop=c == len(parts) - 1)
                    last.then_inc(made.sem, 1)

                chunks = range(C)
                product(0, LAT, [(w_down[:, c, 0:LAT], k.xt[:, c, :]) for c in chunks])
                product(2, LAT, [(w_down[:, c, LAT:2 * LAT], k.xt[:, c, :]) for c in chunks])
                product(4, P, [(w_rk[:, c, :], k.xt[:, c, :]) for c in chunks])
                pe.wait_ge(evac.sem, evac.at(1))
                product(6, P, [(w_lat[:, 0:P], lat[:, 0, :])])
                pe.wait_ge(evac.sem, evac.at(3))
                product(0, P, [(perm[:], raw[:, 0, :])])
                product(2, P, [(w_lat[:, P:2 * P], lat[:, 1, :])])
                product(4, P, [(w_lat[:, 2 * P:3 * P], lat[:, 1, :])])
                pe.wait_ge(evac.sem, evac.at(6))
                product(6, P, [(perm[:], raw[:, 1, :])])
                pe.wait_ge(swapped.sem, swapped.at(1))
                for i in range(NT):
                    last = nc.tensor.matmul(ps[:, i // 2, (i % 2) * D:(i % 2 + 1) * D], lat[:, 0, i * P:(i + 1) * P],
                                            w_lat[:, 3 * P:3 * P + D], start=True, stop=True)
                    if i % 4 == 3:
                        last.then_inc(made.sem, 1)

            @block.scalar
            def _(act):
                def copy(nth, dst, bank, rows=P, by=1.0):
                    act.wait_ge(made.sem, made.at(nth))
                    return nc.scalar.activation(dst, k.ps_flat[0:rows, bank * BANK:bank * BANK + T], ACT.Copy, scale=by)

                copy(1, lat[:, 0, :], 0, LAT).then_inc(evac.sem, 1)
                copy(2, lat[:, 1, :], 2, LAT, scale).then_inc(evac.sem, 1)
                copy(3, raw[:, 0, :], 4).then_inc(evac.sem, 1)
                copy(4, kf[:, 0, :], 6).then_inc(evac.sem, 1)
                copy(6, qf[:, 0, :], 2).then_inc(evac.sem, 1)
                copy(7, raw[:, 1, :], 4).then_inc(evac.sem, 1)
                for n in range(2):
                    part_0(n)
                for n in range(2):
                    part_1(n)
                for n in range(2, U):
                    part_0(n)
                for n in range(2, U):
                    part_1(n)
                for n in range(2):
                    copy(9 + n, v[:, 4 * n:4 * n + 4, :].rearrange("p i n -> p (i n)"), 2 * n)

            @block.vector
            def _(dve):
                def swap(nth, m, bank):
                    dve.wait_ge(made.sem, made.at(nth))
                    nc.vector.tensor_tensor(turn[:, m, :], k.ps_flat[:, bank * BANK:bank * BANK + T], sin[:], ALU.mult)\
                        .then_inc(swapped.sem, 1)

                def add(m, dst):
                    dve.wait_ge(swapped.sem, swapped.at(m + 1))
                    dve.wait_ge(turned.sem, turned.at(m + 1))
                    nc.vector.tensor_tensor(dst[:, 1, :], dst[:, 1, :], turn[:, m, :], ALU.add).then_inc(by_dve.sem, 1)

                dve.wait_ge(loaded.sem, loaded.at(16 * n_loads))
                swap(5, 0, 0)
                add(0, kf)
                remainder(0)
                remainder(1)
                swap(8, 1, 6)
                add(1, qf)
                part_2(0)
                part_2(1)
                for n in range(2, U):
                    remainder(n)
                for n in range(2, U):
                    part_2(n)

            @block.gpsimd
            def _(pool):
                pool.wait_ge(loaded.sem, loaded.at(16 * n_loads))
                for m, dst in ((0, kf), (1, qf)):
                    pool.wait_ge(evac.sem, evac.at(3 + 3 * m))
                    nc.gpsimd.tensor_tensor(dst[:, 1, :], raw[:, m, :], cos[:], ALU.mult).then_inc(turned.sem, 1)
                pool.wait_ge(turned.sem, turned.at(2))
                nc.gpsimd.memset(ks[ROWS:ROWS_M, :], 1.0)

            made.base += 10
            evac.base += 6
            swapped.base += 2
            turned.base += 2
        else:
            v_cols = D if kind == "mha" else HD

            @block.tensor
            def _(pe):
                pe.wait_ge(loaded.sem, loaded.at(16 * n_loads))
                for side, m, _, _ in units:
                    g = int(side == "k")
                    rows = k_rows if g else P
                    col = g * D + m * P
                    for n in range(2):
                        for c in range(C):
                            last = nc.tensor.matmul(ps[0:rows, 4 * g + 2 * m + n, :], w_in[:, c, col:col + rows],
                                                    k.xt[:, c, n * BANK:(n + 1) * BANK], start=c == 0, stop=c == C - 1)
                    last.then_inc(made.sem, 1)
                v_at = 2 * D if kind == "mha" else D + HD
                for i in range(NT):
                    if i % 2 == 0:
                        pe.wait_ge(by_dve.sem, by_dve.at(i // 4 + 1))
                    for c in range(C):
                        last = nc.tensor.matmul(ps[:, i // 2, (i % 2) * D:(i % 2) * D + v_cols],
                                                k.xt[:, c, i * P:(i + 1) * P], w_in[:, c, v_at:v_at + v_cols],
                                                start=c == 0, stop=c == C - 1)
                    if i % 2:
                        last.then_inc(rooms.sem, 1)

            @block.vector
            def _(dve):
                dve.wait_ge(loaded.sem, loaded.at(16 * n_loads))
                def copy_queries(c):
                    dve.wait_ge(made.sem, made.at(2 * c + 1))
                    nc.vector.tensor_scalar(qf[:, c, :], k.ps_flat[:, c * T:(c + 1) * T], b_qk[:, c:c + 1], scale, ALU.add, ALU.mult)\
                        .then_inc(by_dve.sem, 1)

                copy_queries(0)
                remainder(0)
                remainder(1)
                part_2(0)
                copy_queries(1)
                part_2(1)
                for n in range(2, U):
                    remainder(n)
                for n in range(2, U):
                    part_2(n)
                for n in range(4):
                    dve.wait_ge(rooms.sem, rooms.at(n + 1))
                    bank = ps[:, n, :].rearrange("p (i n) -> p i n", i=2)[:, :, 0:v_cols]
                    nc.vector.tensor_tensor(v[:, 2 * n:2 * n + 2, :], bank, bc(b_v[:].unsqueeze(1), [P, 2, v_cols]), ALU.add)

            @block.scalar
            def _(act):
                act.wait_ge(loaded.sem, loaded.at(16 * n_loads))
                for pair in (range(0, 2), range(2, U)):
                    for n in pair:
                        side, c, _, _ = units[n]
                        if side == "k":
                            act.wait_ge(made.sem, made.at(n + 1))
                            nc.scalar.activation(kf[0:k_rows, c, :], k.ps_flat[0:k_rows, (4 + 2 * c) * BANK:(6 + 2 * c) * BANK],
                                                 ACT.Identity, bias=b_qk[0:k_rows, 2 + c:3 + c]).then_inc(by_act.sem, 1)
                        part_0(n)
                    for n in pair:
                        part_1(n)
                for j in range(3):
                    for n in range(EARLY, U):
                        store_part(act, n, j)

            @block.gpsimd
            def _(pool):
                nc.gpsimd.memset(ks[ROWS:ROWS_M, :], 1.0)

            made.base += U
            rooms.base += 4
        loaded.base += 16 * n_loads
        by_act.base += {"mha": 2, "mqa": 1, "mla": 0}[kind]
        by_dve.base += 2
        for c in (first, second, third, rest):
            c.base += U
        stored.base += 48 * EARLY
        late_stored.base += 48 * (U - EARLY)
        shared_stacked.base += 48 * int(kind == "mqa")


def small_attention_stage(k, kind, qs, ks, v, ot, wo, bo):
    nc, d = k.nc, k.dram
    shared_k = kind == "mqa"
    stacked, shared_stacked, per_pair = k.count("parts_stacked"), k.count("shared_stacked"), stacked_per_pair(kind)
    ready, freed, reduced = k.count("max_scores"), k.freed("max_scores_freed"), k.count("max_reduced")
    turned, parts_made, moved = k.count("max_turned"), k.count("max_parts"), k.count("max_moved")
    v_ready = k.count("values_of_head")
    st_ready, e_ready, used = k.count("scores_ready"), k.count("exps_ready"), k.freed("value_products")
    copied, stored = k.freed("head_copied"), [k.freed(f"head_stored_{u}") for u in range(2)]
    steps, early, zeros = k.count("dve_steps"), k.count("out_early"), k.count("zeros_made")
    pairs, ring, e_ring, ahead = H // 2, 3, 4, 2
    blocks = [(c, j, max(c * BANK, j * P), (c + 1) * BANK - max(c * BANK, j * P)) for c in range(2) for j in range(4 * c + 4)]
    per_head = len(blocks)
    B = 2 * per_head
    half_ends = {n: b[0] for n, b in enumerate(blocks) if b[1] == 4 * b[0] + 3}
    pieces = [(u, i, col, min(BANK, (i + 1) * P - col)) for u in range(2) for i in range(NT) for col in range(0, (i + 1) * P, BANK)]
    M = len(pieces)
    USES = M + 1
    order, done, r = [], 0, 0
    lead = [sum(p[3] for p in pieces[:n]) for n in range(M + 1)]
    for n in range(B):
        order.append(("scores", n))
        done += blocks[n % per_head][3]
        while r < M and lead[r] < done * MAXIMA_PACE:
            order.append(("piece", r))
            r += 1
            if r == M:
                order.append(("reduce", None))
                turn_at = n + 1
        order.append(("value", n))
        if r == M and n == turn_at:
            order.append(("turn", None))
    assert ("turn", None) in order and per_head % ring == 0

    with Stage(k) as st:
        zero = st.sb("zero", [P, SLOTS * D // P // ZERO_DMAS]) if kind == "mha" else None
        e = st.sb("e", [P, e_ring, BANK])
        vb = st.sb("vb", [P, 2, NT, HD + 1])
        ob = st.sb("ob", [HD + 1, 2, T])
        raw = st.sb("raw", [P, 2, NT, 2])
        mx = st.sb("mx", [P, 2, NT])
        neg = st.sb("neg", [2 * NT, P])
        parts = [st.sb(f"neg{j}", [2 * NT, P], BF16) for j in range(3)]
        block = st.block()
        ps = k.ps_flat
        MAX_BANK, OUT_BANK = 5, 3
        TURN_AT = MAX_BANK * BANK
        HEAD, BOTH = (slice(0, 1), slice(1, 2)), slice(0, 2)

        @block.gpsimd
        def _(pool):
            if kind == "mha":
                nc.gpsimd.memset(zero[:], 0.0).then_inc(zeros.sem, 1)
            nc.gpsimd.memset(vb[:, :, :, HD:HD + 1], 1.0).then_inc(v_ready.sem, 1)
            if shared_k:
                nc.gpsimd.tensor_copy(vb[:, 0, :, 0:HD], v[:]).then_inc(v_ready.sem, 1)
            else:
                with pool.Fori(0, pairs) as it:
                    for u in range(2):
                        pool.wait_ge(used.sem, used.at(it * B + (u - 1) * per_head))
                        nc.gpsimd.tensor_copy(vb[:, u, :, 0:HD], v[:, :, bass.ds((it * 2 + u) * HD, HD)]).then_inc(v_ready.sem, 1)

        @block.tensor
        def _(pe):
            def piece(pair, r, first=False):
                u, i, col, w = pieces[r]
                at = (MAX_BANK + r % ring) * BANK
                if r == 0:
                    pe.wait_ge(stacked.sem, stacked.at(pair * per_pair + per_pair))
                if first:
                    pe.wait_ge(freed.sem, freed.at(r + 1 - ring if r < per_head else max(per_head + 1, r + 2 - ring)))
                else:
                    pe.wait_ge(freed.sem, freed.at(pair * USES + 1 + (r + 1 - ring if r >= ring else -((M - r) % ring))))
                keys = ks[0:ROWS, col:col + w] if shared_k else ks[0:ROWS, bass.ds((pair * 2 + u) * T + col, w)]
                diagonal = col + w == (i + 1) * P
                last = nc.tensor.matmul(ps[:, at:at + w], qs[0:ROWS, bass.ds((pair * 2 + u) * T + i * P, P)], keys,
                                        start=True, stop=not diagonal)
                if diagonal:
                    last = nc.tensor.matmul(ps[:, at + w - P:at + w], k.ident_bf[:], k.mask_q[:], start=False, stop=True)
                last.then_inc(ready.sem, 1)

            def turn_maxima(round_, heads):
                pe.wait_ge(reduced.sem, reduced.at(round_ + 1))
                nc.tensor.transpose(ps[0:(heads.stop - heads.start) * NT, TURN_AT:TURN_AT + P],
                                    mx[:, heads, :].rearrange("p u i -> p (u i)"), k.ident[:]).then_inc(turned.sem, 1)

            def scores(pair, n, first=False):
                u, (c, j, t0, w) = n // per_head, blocks[n % per_head]
                if n in (0, per_head):
                    rounds = 1 if first else pair + 2
                    pe.wait_ge(moved.sem, moved.at(rounds * 48))
                base = (n % ring) * BANK
                diagonal = j * P >= c * BANK
                keys = ks[0:ROWS_M, j * P:(j + 1) * P] if shared_k else ks[0:ROWS_M, bass.ds((pair * 2 + u) * T + j * P, P)]
                last = nc.tensor.matmul(ps[:, base:base + w], keys, qs[0:ROWS_M, bass.ds((pair * 2 + u) * T + t0, w)],
                                        start=True, stop=not diagonal)
                if diagonal:
                    last = nc.tensor.matmul(ps[:, base:base + P], k.ident_bf[:], k.mask_k[:], start=False, stop=True)
                last.then_inc(st_ready.sem, 1)

            def value(pair, n):
                u, (c, j, t0, w) = n // per_head, blocks[n % per_head]
                pe.wait_ge(e_ready.sem, e_ready.at(pair * B + n + 1))
                if (c, j) == (0, 0) and not shared_k:
                    pe.wait_ge(v_ready.sem, v_ready.at(pair * 2 + u + 2))
                if j == 0:
                    pe.wait_ge(copied.sem, copied.at(pair * 4 + 2 * u + c + 1 - 2))
                col = (OUT_BANK + c) * BANK + t0 - c * BANK
                nc.tensor.matmul(ps[0:HD + 1, col:col + w], vb[:, 0 if shared_k else u, j, :], e[:, n % e_ring, 0:w],
                                 start=j == 0, stop=j == 4 * c + 3).then_inc(used.sem, 1)

            def turn(pair, maxima):
                for what, n in order:
                    if what == "scores" and n + ahead < B:
                        scores(pair, n + ahead)
                    elif what == "scores" and maxima:
                        scores(pair + 1, n + ahead - B)
                    elif what == "value":
                        value(pair, n)
                    elif what == "piece" and maxima:
                        piece(pair + 1, n)
                    elif what == "turn" and maxima:
                        turn_maxima(pair + 2, BOTH)

            if shared_k:
                pe.wait_ge(shared_stacked.sem, shared_stacked.base)
            for u, head in enumerate(HEAD):
                for r in range(u * per_head, (u + 1) * per_head):
                    piece(0, r, first=True)
                turn_maxima(u, head)
            for n in range(ahead):
                scores(0, n, first=True)
            pe.wait_ge(v_ready.sem, v_ready.at(1 + shared_k))
            with pe.Fori(0, pairs - 1) as it:
                turn(it, True)
            turn(pairs - 1, False)

        @block.scalar
        def _(act):
            if kind == "mha":
                act.wait_ge(zeros.sem, 1)
            with act.Fori(0, pairs) as it:
                if kind == "mha":
                    rows = d["expert_in"].rearrange("(p a) n -> p (a n)", p=P)
                    width = SLOTS * D // P // ZERO_DMAS
                    for n in range(ZERO_DMAS // pairs):
                        act.dma_start(rows[:, bass.ds((it * (ZERO_DMAS // pairs) + n) * width, width)], zero[:])\
                            .then_inc(k.count("slots_zeroed").sem, 16)
                for n in range(B):
                    w = blocks[n % per_head][3]
                    act.wait_ge(st_ready.sem, st_ready.at(it * B + n + 1))
                    act.wait_ge(used.sem, used.at(it * B + n + 1 - e_ring))
                    base = (n % ring) * BANK
                    nc.scalar.activation(e[:, n % e_ring, 0:w], ps[:, base:base + w], ACT.Exp).then_inc(e_ready.sem, 1)
            if kind == "mha":
                act.wait_ge(k.count("slots_zeroed").sem, 16 * ZERO_DMAS)

        @block.vector
        def _(dve):
            def piece(pair, r):
                u, i, col, w = pieces[r]
                at = (MAX_BANK + r % ring) * BANK
                dve.wait_ge(ready.sem, ready.at(pair * M + r + 1))
                nc.vector.reduce_max(raw[:, u, i, col // BANK:col // BANK + 1], ps[:, at:at + w], X_AXIS).then_inc(freed.sem, 1)

            def reduce(uses, heads):
                dve.wait_ge(freed.sem, freed.at(uses))
                nc.vector.tensor_tensor(mx[:, heads, :], raw[:, heads, :, 0], raw[:, heads, :, 1], ALU.max).then_inc(reduced.sem, 1)

            def negate(round_, uses, heads, first=False):
                rows = (heads.stop - heads.start) * NT
                s = Steps(dve, steps, round_)
                dve.wait_ge(turned.sem, turned.at(round_ + 1))
                nc.vector.tensor_scalar(neg[0:rows, :], ps[0:rows, TURN_AT:TURN_AT + P], -1.0, None, ALU.mult).then_inc(freed.sem, 1)
                dve.wait_ge(freed.sem, freed.at(uses))
                if not first:
                    dve.wait_ge(moved.sem, moved.at(round_ * 48))
                nc.vector.tensor_copy(parts[0][0:rows, :], neg[0:rows, :]).then_inc(parts_made.sem, 1)
                dve.wait_ge(parts_made.sem, parts_made.at(round_ * 3 + 1))
                s.link(nc.vector.tensor_tensor(neg[0:rows, :], neg[0:rows, :], parts[0][0:rows, :], ALU.subtract))
                nc.vector.tensor_copy(parts[1][0:rows, :], neg[0:rows, :]).then_inc(parts_made.sem, 1)
                dve.wait_ge(parts_made.sem, parts_made.at(round_ * 3 + 2))
                nc.vector.tensor_tensor(parts[2][0:rows, :], neg[0:rows, :], parts[1][0:rows, :], ALU.subtract)\
                    .then_inc(parts_made.sem, 1)

            def copy_half(pair, u, c):
                last = max(n for n, half in half_ends.items() if half == c)
                if c == 0:
                    dve.wait_ge(stored[u].sem, stored[u].at(pair * 32))
                dve.wait_ge(used.sem, used.at(pair * B + u * per_head + last + 1))
                nc.vector.tensor_copy(ob[:, u, c * BANK:(c + 1) * BANK], ps[0:HD + 1, (OUT_BANK + c) * BANK:(OUT_BANK + c + 1) * BANK])\
                    .then_inc(copied.sem, 1)

            def turn(pair, maxima):
                for what, n in order:
                    if what == "piece" and maxima:
                        piece(pair + 1, n)
                    elif what == "reduce" and maxima:
                        reduce((pair + 1) * USES + 1 + M, BOTH)
                    elif what == "turn" and maxima:
                        negate(pair + 2, (pair + 2) * USES + 1, BOTH)
                    elif what == "value" and n % per_head in half_ends:
                        copy_half(pair, n // per_head, half_ends[n % per_head])

            s = Steps(dve, steps)
            s.link(nc.vector.memset(raw[:], -3.0e38))
            steps.base += s.n
            for u, head in enumerate(HEAD):
                for r in range(u * per_head, (u + 1) * per_head):
                    piece(0, r)
                reduce((u + 1) * per_head + u, head)
                negate(u, (u + 1) * (per_head + 1), head, first=u == 0)
            with dve.Fori(0, pairs - 1) as it:
                turn(it, True)
            turn(pairs - 1, False)
            steps.base += pairs + 1

        @block.sync
        def _(sp):
            def move_maxima(round_, head, heads):
                for j in range(3):
                    sp.wait_ge(parts_made.sem, parts_made.at(round_ * 3 + j + 1))
                    sp.dma_start(qs[ROWS + j:ROWS + j + 1, bass.ds(head * T, heads * T)].rearrange("a (r t) -> a r t", t=P),
                                 parts[j][0:heads * NT, :]).then_inc(moved.sem, 16)

            def store(pair):
                for u in range(2):
                    sp.wait_ge(copied.sem, copied.at(pair * 4 + 2 * u + 2))
                    sp.dma_start(d["head_out"][bass.ds((pair * 2 + u) * HD, HD), :], ob[0:HD, u, :]).then_inc(stored[u].sem, 16)
                    sp.dma_start(d["head_sum"][bass.ds(pair * 2 + u, 1), :], ob[HD:HD + 1, u, :]).then_inc(stored[u].sem, 16)

            sp.wait_ge(stacked.sem, stacked.at(per_pair))
            stack_pair(k, kind, sp, 1, qs, ks, stacked)
            for u in range(2):
                move_maxima(u, u, 1)
            with sp.Fori(0, pairs - 2) as it:
                sp.wait_ge(stacked.sem, stacked.at(it * per_pair + 2 * per_pair))
                stack_pair(k, kind, sp, it + 2, qs, ks, stacked)
                move_maxima(it + 2, it * 2 + 2, 2)
                store(it)
            move_maxima(pairs, H - 2, 2)
            store(pairs - 2)
            for u in range(2):
                sp.wait_ge(stored[u].sem, stored[u].at(32 * (pairs - 1)))
            sp.dma_start(wo[:], d[kind + "_wo"]).then_inc(early.sem, 16)
            if bo is not None:
                sp.dma_start(bo[:], bc(d[kind + "_bo"], [P, D])).then_inc(early.sem, 16)
            sp.dma_start(ot[:, 0, :], d["head_out"][0:P, :]).then_inc(early.sem, 16)
            store(pairs - 1)
            early_loads = 48 if bo is not None else 32
            sp.wait_ge(early.sem, early.at(early_loads))
            early.base += early_loads
            for u in range(2):
                sp.wait_ge(stored[u].sem, stored[u].at(16 * H))

        stacked.base += per_pair * pairs
        ready.base += M * pairs
        freed.base += USES * pairs + 1
        reduced.base += pairs + 1
        turned.base += pairs + 1
        parts_made.base += 3 * (pairs + 1)
        moved.base += 48 * (pairs + 1)
        v_ready.base += 2 if shared_k else H + 1
        for n in (st_ready, e_ready, used):
            n.base += H * per_head
        copied.base += 2 * H
        for u in range(2):
            stored[u].base += 16 * H


def small_output_stage(k, ot, wo, bo, target):
    nc, d = k.nc, k.dram
    loaded, inv, spread, normed = (k.count(n) for n in ("out_loaded", "out_inverse", "out_spread", "out_normed"))
    made, sums_loaded = k.count("out_product"), k.count("out_sums_loaded")
    steps = k.count("dve_steps")
    with Stage(k) as st:
        sums = st.sb("sums", [P, P])
        block = st.block()

        @block.sync
        def _(sp):
            sp.dma_start(sums[:], d["head_sum"].rearrange("h (i t) -> (h i) t", t=P)).then_inc(sums_loaded.sem, 16)
            sp.dma_start(ot[:, 1, :], d["head_out"][P:2 * P, :]).then_inc(loaded.sem, 16)

        @block.tensor
        def _(pe):
            pe.wait_ge(k.count("late_constants").sem, 32)
            pe.wait_ge(inv.sem, inv.at(1))
            for c in range(C):
                for n in range(2):
                    for i in range(4 * n, 4 * n + 4):
                        last = nc.tensor.matmul(k.ps[:, 2 * c + n, (i - 4 * n) * P:(i - 4 * n + 1) * P], k.sel[:, i, c, :], sums[:],
                                                start=True, stop=True)
                    last.then_inc(spread.sem, 1)
            for i in range(NT):
                pe.wait_ge(normed.sem, normed.at(3 + i // 4))
                for c in range(C):
                    last = nc.tensor.matmul(k.ps[:, 4 + i // 2, (i % 2) * D:(i % 2 + 1) * D], ot[:, c, i * P:(i + 1) * P],
                                            wo[:, c, :], start=c == 0, stop=c == C - 1)
                if i % 2:
                    last.then_inc(made.sem, 1)

        @block.vector
        def _(dve):
            s = Steps(dve, steps)
            if bo is not None:
                s.mark(nc.vector.tensor_tensor(target[:], target[:], bc(bo[:].unsqueeze(1), [P, NT, D]), ALU.add))
            dve.wait_ge(sums_loaded.sem, sums_loaded.at(16))
            nc.vector.reciprocal(sums[:], sums[:]).then_inc(inv.sem, 1)
            for n in range(4):
                if n == 2:
                    dve.wait_ge(loaded.sem, loaded.at(16))
                dve.wait_ge(spread.sem, spread.at(n + 1))
                cols = ot[:, n // 2, (n % 2) * BANK:(n % 2 + 1) * BANK]
                nc.vector.tensor_tensor(cols, cols, k.ps[:, n, :], ALU.mult).then_inc(normed.sem, 1)
            if bo is not None:
                s.wait()
            for n in range(NT // 2):
                dve.wait_ge(made.sem, made.at(n + 1))
                pair = target[:, 2 * n:2 * n + 2, :].rearrange("p i n -> p (i n)")
                s.link(nc.vector.tensor_tensor(pair, pair, k.ps[:, 4 + n, :], ALU.add))
                for i in (2 * n, 2 * n + 1):
                    nc.vector.bn_stats(k.bn[:, i, :], target[:, i, :])
            steps.base += s.n
            k.bn_made = True

        loaded.base += 16
        sums_loaded.base += 16
        inv.base += 1
        spread.base += 4
        normed.base += 4
        made.base += NT // 2


def small_attention(k, kind):
    with Stage(k) as st:
        shared_k = kind == "mqa"
        qs = st.sb("qs", [ROWS_M, H * T], BF16)
        ks = st.sb("ks", [ROWS_M, (1 if shared_k else H) * T], BF16)
        v = st.sb("v", [P, NT, HD if shared_k else D])
        with Stage(k) as inner:
            weights = SmallWeights(k, kind, inner)
            norm_stage(k, k.x, k.xn, k.dram["ln1"] if kind == "mla" else None, preload=weights.load)
            qf = inner.sb("qf", [P, C, T])
            kf = inner.sb("kf", [P, C, T])
            small_projections(k, kind, weights, qf, kf, v, qs, ks)
        ot = st.sb("ot", [P, C, T])
        wo = st.sb("wo", [P, C, D])
        bo = None if kind == "mla" else st.sb("bo", [P, D])
        small_attention_stage(k, kind, qs, ks, v, ot, wo, bo)
        small_output_stage(k, ot, wo, bo, k.xn if kind == "mla" else k.x)


def route_stage(k, wr, s_, col, chosen_by, slot, slot_out):
    nc, d = k.nc, k.dram
    loaded, logits, exps = k.count("router_loaded"), k.count("router_logits"), k.count("router_exps")
    shifted, chosen, places = k.count("router_shifted"), k.count("router_chosen"), k.count("router_places")
    steps = k.count("dve_steps")
    with Stage(k) as st:
        top = st.sb("top", [P, NT, 8])
        which = st.sb("which", [P, NT, 8], U32)
        which_f = st.sb("which_f", [P, NT, K0])
        pick = st.sb("pick", [P, NT * K0, E0])
        spent = st.sb("spent", [P, NT, E0], BF16)
        over = st.sb("over", [P, NT, E0])
        slot_f = st.sb("slot_f", [P, NT * K0])
        block = st.block()

        @block.tensor
        def _(pe):
            pe.wait_ge(loaded.sem, loaded.at(16))
            for i in range(NT):
                for c in range(C):
                    last = nc.tensor.matmul(k.ps[:, 0, i * E0:(i + 1) * E0], k.xt[:, c, i * P:(i + 1) * P], wr[:, c, :],
                                            start=c == 0, stop=c == C - 1)
            last.then_inc(logits.sem, 1)
            pe.wait_ge(chosen.sem, chosen.at(1))
            for i in range(NT):
                for j in range(i + 1):
                    last = nc.tensor.matmul(k.ps[:, 1, i * E0:(i + 1) * E0], (k.before_bf if j == i else k.ones_bf)[:],
                                            spent[:, j, :], start=j == 0, stop=j == i)
            last.then_inc(places.sem, 1)

        @block.scalar
        def _(act):
            act.wait_ge(shifted.sem, shifted.at(1))
            nc.scalar.activation(s_[:], s_[:], ACT.Exp).then_inc(exps.sem, 1)

        @block.vector
        def _(dve):
            s = Steps(dve, steps)
            wide = [P, NT, E0]
            dve.wait_ge(logits.sem, logits.at(1))
            bank = k.ps[:, 0, 0:NT * E0].rearrange("p (i e) -> p i e", e=E0)
            s.link(nc.vector.reduce_max(col[:], bank, X_AXIS))
            nc.vector.tensor_tensor(s_[:], bank, bc(col[:].unsqueeze(2), wide), ALU.subtract).then_inc(shifted.sem, 1)
            dve.wait_ge(exps.sem, exps.at(1))
            s.link(nc.vector.reduce_sum(col[:], s_[:], X_AXIS))
            s.link(nc.vector.reciprocal(col[:], col[:]))
            s.link(nc.vector.tensor_tensor(s_[:], s_[:], bc(col[:].unsqueeze(2), wide), ALU.mult))
            for i in range(NT):
                s.mark(nc.vector.max(top[:, i, :], s_[:, i, :]))
            s.wait()
            for i in range(NT):
                s.mark(nc.vector.max_index(which[:, i, :], top[:, i, :], s_[:, i, :]))
            s.link(nc.vector.reduce_sum(col[:], top[:, :, 0:K0], X_AXIS))
            s.link(nc.vector.tensor_scalar(col[:], col[:], 1e-20, None, ALU.add))
            s.mark(nc.vector.reciprocal(col[:], col[:]))
            s.link(nc.vector.tensor_copy(which_f[:], which[:, :, 0:K0]))
            flat = which_f[:].rearrange("p i r -> p (i r)")
            s.link(nc.vector.tensor_tensor(pick[:], bc(flat.unsqueeze(2), [P, NT * K0, E0]),
                                           bc(k.iota[:, 0:1, :], [P, NT * K0, E0]), ALU.is_equal))
            nc.vector.reduce_sum(chosen_by[:], pick[:].rearrange("p (i r) e -> p i e r", r=K0), X_AXIS).then_inc(steps.sem, 1)
            s.n += 1
            s.wait()
            nc.vector.tensor_copy(spent[:], chosen_by[:]).then_inc(chosen.sem, 1)
            dve.wait_ge(chosen.sem, chosen.at(1))
            dve.wait_ge(places.sem, places.at(1))
            bank = k.ps[:, 1, 0:NT * E0].rearrange("p (i e) -> p i e", e=E0)
            s.mark(nc.vector.tensor_scalar(over[:], bank, float(CAP), DROPPED, ALU.is_ge, ALU.mult))
            s.link(nc.vector.tensor_tensor(slot[:], bank, bc(k.iota[:, 1:2, :], wide), ALU.add))
            s.link(nc.vector.tensor_tensor(slot[:], slot[:], over[:], ALU.add))
            for i in range(NT):
                rows = pick[:, i * K0:(i + 1) * K0, :]
                s.mark(nc.vector.tensor_tensor(rows, rows, bc(slot[:, i:i + 1, :], [P, K0, E0]), ALU.mult))
            s.wait()
            s.link(nc.vector.reduce_sum(slot_f[:], pick[:], X_AXIS))
            nc.vector.tensor_copy(slot_out[:], slot_f[:])
            steps.base += s.n

        for n in (logits, exps, shifted, chosen, places):
            n.base += 1
        loaded.base += 16


def dispatch_stage(k, s_, col, chosen_by, slot, slot_out, slot_in, weights):
    nc, d = k.nc, k.dram
    sent, loaded = k.count("rows_sent"), k.count("shared_loaded")
    made, silu, hidden = k.count("shared_products"), k.count("shared_silu"), k.count("shared_hidden")
    down, added = k.count("shared_down"), k.count("shared_added")
    with Stage(k) as st:
        w_in = st.sb("w_in", [P, 2, C, FS])
        w_out = st.sb("w_out", [FH, NS, D])
        act_t = st.sb("act_t", [FH, NS, T])
        top = st.sb("top", [P, NT, 8])
        which = st.sb("which", [P, NT, 8], U32)
        which_f = st.sb("which_f", [P, NT, K0])
        pick = st.sb("pick", [P, NT * K0, E0])
        picked = st.sb("picked", [P, NT * K0, E0])
        key = st.sb("key", [P, NT, E0])
        slot_f = st.sb("slot_f", [P, NT * K0])
        kept = st.sb("kept", [P, NT * K0])
        block = st.block()

        @block.sync
        def _(sp):
            sp.dma_start(w_in[:], d["shared_in"]).then_inc(loaded.sem, 16)
            sp.dma_start(w_out[:], d["shared_out"]).then_inc(loaded.sem, 16)

        @block.gpsimd
        def _(pool):
            pool.wait_ge(k.count("slots_zeroed").sem, 16 * ZERO_DMAS)
            for i in range(NT):
                for r in range(K0):
                    n = i * K0 + r
                    nc.gpsimd.indirect_dma_start(out=d["expert_in"], out_offset=bass.IndirectOffsetOnAxis(slot_out[:, n:n + 1], 0),
                                                 in_=k.xn[:, i, :], in_offset=None, bounds_check=SLOTS - 1,
                                                 oob_is_err=False).then_inc(sent.sem, 16)
            pool.wait_ge(sent.sem, sent.at(16 * NT * K0))

        @block.tensor
        def _(pe):
            pe.wait_ge(loaded.sem, loaded.at(32))
            for m in range(NS):
                if m >= 2:
                    pe.wait_ge(hidden.sem, hidden.at(m - 1))
                for g in range(2):
                    for n in range(2):
                        for c in range(C):
                            last = nc.tensor.matmul(k.ps[0:FH, 4 * (m % 2) + 2 * g + n, :], w_in[:, g, c, m * FH:(m + 1) * FH],
                                                    k.xt[:, c, n * BANK:(n + 1) * BANK], start=c == 0, stop=c == C - 1)
                    last.then_inc(made.sem, 1)
            for n in range(NT // 2):
                pe.wait_ge(hidden.sem, hidden.at(NS))
                for i in (2 * n, 2 * n + 1):
                    for m in range(NS):
                        last = nc.tensor.matmul(k.ps[:, n, (i % 2) * D:(i % 2 + 1) * D], act_t[:, m, i * P:(i + 1) * P],
                                                w_out[:, m, :], start=m == 0, stop=m == NS - 1)
                last.then_inc(down.sem, 1)

        @block.scalar
        def _(act):
            for m in range(NS):
                act.wait_ge(made.sem, made.at(2 * m + 1))
                bank = 4 * (m % 2) * BANK
                nc.scalar.activation(act_t[:, m, :], k.ps_flat[0:FH, bank:bank + T], ACT.Silu).then_inc(silu.sem, 1)

        @block.vector
        def _(dve):
            for m in range(NS):
                dve.wait_ge(made.sem, made.at(2 * m + 2))
                dve.wait_ge(silu.sem, silu.at(m + 1))
                bank = (4 * (m % 2) + 2) * BANK
                nc.vector.tensor_tensor(act_t[:, m, :], act_t[:, m, :], k.ps_flat[0:FH, bank:bank + T], ALU.mult)\
                    .then_inc(hidden.sem, 1)
            s = Steps(dve, k.count("dve_steps"))
            wide = [P, NT, E0]
            s.link(nc.vector.tensor_scalar(key[:], bc(k.iota[:, 0:1, :], wide), -1.0, float(E0), ALU.mult, ALU.add))
            s.link(nc.vector.tensor_tensor(key[:], key[:], chosen_by[:], ALU.mult))
            for i in range(NT):
                s.mark(nc.vector.max(top[:, i, :], key[:, i, :]))
            s.wait()
            for i in range(NT):
                s.mark(nc.vector.max_index(which[:, i, :], top[:, i, :], key[:, i, :]))
            s.wait()
            s.link(nc.vector.tensor_copy(which_f[:], which[:, :, 0:K0]))
            flat = which_f[:].rearrange("p i r -> p (i r)")
            s.link(nc.vector.tensor_tensor(pick[:], bc(flat.unsqueeze(2), [P, NT * K0, E0]),
                                           bc(k.iota[:, 0:1, :], [P, NT * K0, E0]), ALU.is_equal))
            for what, out in ((s_, weights[:].rearrange("p i r -> p (i r)")), (slot, slot_f[:])):
                for i in range(NT):
                    rows = slice(i * K0, (i + 1) * K0)
                    s.mark(nc.vector.tensor_tensor(picked[:, rows, :], pick[:, rows, :], bc(what[:, i:i + 1, :], [P, K0, E0]), ALU.mult))
                s.wait()
                s.link(nc.vector.reduce_sum(out, picked[:], X_AXIS))
            s.mark(nc.vector.tensor_tensor(weights[:], weights[:], bc(col[:].unsqueeze(2), [P, NT, K0]), ALU.mult))
            s.link(nc.vector.tensor_scalar(kept[:], slot_f[:], float(SLOTS), None, ALU.is_lt))
            w = weights[:].rearrange("p i r -> p (i r)")
            s.link(nc.vector.tensor_tensor(w, w, kept[:], ALU.mult))
            s.link(nc.vector.tensor_tensor(slot_f[:], slot_f[:], kept[:], ALU.mult))
            nc.vector.tensor_copy(slot_in[:], slot_f[:])
            k.count("dve_steps").base += s.n
            for n in range(NT // 2):
                dve.wait_ge(down.sem, down.at(n + 1))
                pair = k.x[:, 2 * n:2 * n + 2, :].rearrange("p i n -> p (i n)")
                nc.vector.tensor_tensor(pair, pair, k.ps[:, n, :], ALU.add)

        sent.base += 16 * NT * K0
        loaded.base += 32
        made.base += 2 * NS
        silu.base += NS
        hidden.base += NS
        down.base += NT // 2


def experts_stage(k, slot_in, weights):
    nc, d = k.nc, k.dram
    rows_loaded = [k.count(f"expert_rows_loaded_{u}") for u in range(2)]
    in_loaded = [k.count(f"expert_in_loaded_{u}") for u in range(2)]
    out_loaded = [k.count(f"expert_out_loaded_{u}") for u in range(2)]
    turned, rows_t, made = k.freed("expert_turned"), k.freed("expert_rows"), k.freed("expert_products")
    silu, hidden, hidden_turned = k.count("expert_silu"), k.freed("expert_hidden"), k.count("expert_hidden_turned")
    hidden_t, down = k.freed("expert_hidden_copied"), k.freed("expert_down")
    copied, shared_copied = k.freed("expert_copied"), k.freed("expert_shared_copied")
    stored = [k.freed(f"expert_stored_{u}") for u in range(2)]
    fetched = [[k.count(f"row_fetched_{n}_{i}") for i in range(NT)] for n in range(2)]
    added = k.freed("row_added")
    ROWS_T, DOWN, HIDDEN_T = 3 * BANK, 5 * BANK, 6 * BANK + D
    with Stage(k) as st:
        rows = st.sb("rows", [P, 2, CT, D])
        w_in = st.sb("w_in", [P, 2, 2 * C * F0])
        w_out = st.sb("w_out", [FH, 2, 2 * D])
        xt = st.sb("xt", [P, 2, C, CAP])
        gate = st.sb("gate", [P, 2, CT, F0])
        hid = st.sb("hid", [P, 2, CT, F0])
        hid_t = st.sb("hid_t", [FH, 2, 2, CAP])
        y = st.sb("y", [P, 2, CT * D])
        got = st.sb("got", [P, K0, NT, D])
        block = st.block()
        ps = k.ps_flat

        @block.sync
        def _(sp):
            def load_in(e, u):
                sp.wait_ge(turned.sem, turned.at(e + 1 - 2))
                sp.dma_start(rows[:, u], d["expert_in"][bass.ds(e * CAP, CAP), :].rearrange("(s p) n -> p s n", p=P))\
                    .then_inc(rows_loaded[u].sem, 16)
                sp.wait_ge(made.sem, made.at(e + 1 - 2))
                sp.dma_start(w_in[:, u, :], d["expert_w_in"][bass.ds(e * P, P), :]).then_inc(in_loaded[u].sem, 16)

            def load_out(e, u):
                sp.wait_ge(down.sem, down.at(e + 1 - 2))
                sp.dma_start(w_out[:, u, :], d["expert_w_out"][bass.ds(e * FH, FH), :]).then_inc(out_loaded[u].sem, 16)

            load_in(0, 0)
            with sp.Fori(0, E0 // 2 - 1) as it:
                load_in(it * 2 + 1, 1)
                load_out(it * 2, 0)
                load_in(it * 2 + 2, 0)
                load_out(it * 2 + 1, 1)
            load_in(E0 - 1, 1)
            load_out(E0 - 2, 0)
            load_out(E0 - 1, 1)

        @block.gpsimd
        def _(pool):
            for r in range(K0):
                last = E0 - K0 + r
                for e in (last - 1, last):
                    pool.wait_ge(stored[e % 2].sem, stored[e % 2].at(16 * (e // 2 + 1)))
                for i in range(NT):
                    sem = fetched[r % 2][i]
                    if r >= 2:
                        pool.wait_ge(sem.sem, sem.at(16 * (r // 2)))
                    n = i * K0 + r
                    nc.gpsimd.indirect_dma_start(out=got[:, r, i, :], out_offset=None, in_=d["expert_out"][0:(last + 1) * CAP, :],
                                                 in_offset=bass.IndirectOffsetOnAxis(slot_in[:, n:n + 1], 0)).then_inc(sem.sem, 16)

        @block.tensor
        def _(pe):
            def turn_rows(e, u, nth):
                pe.wait_ge(rows_loaded[u].sem, rows_loaded[u].at(nth * 16 + 16))
                pe.wait_ge(rows_t.sem, rows_t.at(e))
                for c in range(C):
                    for s in range(CT):
                        at = ROWS_T + (c * CT + s) * P
                        last = nc.tensor.transpose(ps[:, at:at + P], rows[:, u, s, c * P:(c + 1) * P], k.ident[:])
                last.then_inc(turned.sem, 1)

            def turn_hidden(e, u):
                pe.wait_ge(hidden.sem, hidden.at(e + 1))
                pe.wait_ge(hidden_t.sem, hidden_t.at(e))
                pe.wait_ge(shared_copied.sem, shared_copied.at(e))
                for m in range(2):
                    for s in range(CT):
                        at = HIDDEN_T + (m * CT + s) * P
                        last = nc.tensor.transpose(ps[0:FH, at:at + P], hid[:, u, s, m * FH:(m + 1) * FH], k.ident[:])
                last.then_inc(hidden_turned.sem, 1)

            def gate_up(e, u, nth):
                w = w_in[:, u, :].rearrange("p (g c f) -> p g c f", g=2, c=C)
                pe.wait_ge(in_loaded[u].sem, in_loaded[u].at(nth * 16 + 16))
                pe.wait_ge(rows_t.sem, rows_t.at(e + 1))
                pe.wait_ge(hidden.sem, hidden.at(e))
                for s in range(CT):
                    for c in range(C):
                        last = nc.tensor.matmul(k.ps[:, s, 0:2 * F0], xt[:, u, c, s * P:(s + 1) * P], w[:, :, c, :],
                                                start=c == 0, stop=c == C - 1)
                last.then_inc(made.sem, 1)

            def project(e, u, nth):
                pe.wait_ge(out_loaded[u].sem, out_loaded[u].at(nth * 16 + 16))
                pe.wait_ge(hidden_t.sem, hidden_t.at(e + 1))
                pe.wait_ge(copied.sem, copied.at(e))
                for s in range(CT):
                    for m in range(2):
                        last = nc.tensor.matmul(ps[:, DOWN + s * D:DOWN + (s + 1) * D], hid_t[:, u, m, s * P:(s + 1) * P],
                                                w_out[:, u, m * D:(m + 1) * D], start=m == 0, stop=m == 1)
                last.then_inc(down.sem, 1)

            keep_busy(k, BUSY_EXPERTS)
            turn_rows(0, 0, 0)
            turn_rows(1, 1, 0)
            gate_up(0, 0, 0)
            turn_rows(2, 0, 1)
            turn_hidden(0, 0)
            gate_up(1, 1, 0)
            project(0, 0, 0)
            with pe.Fori(0, E0 // 2 - 2) as it:
                for u in range(2):
                    e, nth = it * 2 + 2 + u, it + 1
                    turn_rows(e + 1, 1 - u, nth + u)
                    turn_hidden(e - 1, 1 - u)
                    gate_up(e, u, nth)
                    project(e - 1, 1 - u, nth - 1 + u)
            half = E0 // 2 - 1
            turn_rows(E0 - 1, 1, half)
            turn_hidden(E0 - 3, 1)
            gate_up(E0 - 2, 0, half)
            project(E0 - 3, 1, half - 1)
            turn_hidden(E0 - 2, 0)
            gate_up(E0 - 1, 1, half)
            project(E0 - 2, 0, half)
            turn_hidden(E0 - 1, 1)
            project(E0 - 1, 1, half)

        @block.vector
        def _(dve):
            def copy_rows(e, u):
                dve.wait_ge(turned.sem, turned.at(e + 1))
                dve.wait_ge(made.sem, made.at(e + 1 - 2))
                nc.vector.tensor_copy(xt[:, u].rearrange("p c n -> p (c n)"), ps[:, ROWS_T:ROWS_T + C * CAP]).then_inc(rows_t.sem, 1)

            def copy_hidden(e, u):
                dve.wait_ge(hidden_turned.sem, hidden_turned.at(e + 1))
                dve.wait_ge(down.sem, down.at(e + 1 - 2))
                nc.vector.tensor_copy(hid_t[:, u].rearrange("p m n -> p (m n)"), ps[0:FH, HIDDEN_T:HIDDEN_T + 2 * CAP])\
                    .then_inc(hidden_t.sem, 1)

            def multiply(e, u):
                dve.wait_ge(silu.sem, silu.at(e + 1))
                nc.vector.tensor_tensor(hid[:, u], gate[:, u], k.ps[:, 0:CT, F0:2 * F0], ALU.mult).then_inc(hidden.sem, 1)

            copy_rows(0, 0)
            copy_rows(1, 1)
            multiply(0, 0)
            copy_rows(2, 0)
            copy_hidden(0, 0)
            multiply(1, 1)
            with dve.Fori(0, E0 // 2 - 2) as it:
                for u in range(2):
                    e = it * 2 + 2 + u
                    copy_rows(e + 1, 1 - u)
                    copy_hidden(e - 1, 1 - u)
                    multiply(e, u)
            copy_rows(E0 - 1, 1)
            copy_hidden(E0 - 3, 1)
            multiply(E0 - 2, 0)
            copy_hidden(E0 - 2, 0)
            multiply(E0 - 1, 1)
            copy_hidden(E0 - 1, 1)
            for r in range(K0):
                for i in range(NT):
                    sem = fetched[r % 2][i]
                    dve.wait_ge(sem.sem, sem.at(16 * (r // 2 + 1)))
                    dve.wait_ge(added.sem, added.at(r * NT + i + 1 - NT))
                    nc.vector.scalar_tensor_tensor(k.x[:, i, :], got[:, r, i, :], weights[:, i, r:r + 1], k.x[:, i, :],
                                                   ALU.mult, ALU.add).then_inc(added.sem, 1)
                    if r == K0 - 1:
                        dve.wait_ge(added.sem, added.at(r * NT + i + 1))
                        nc.vector.bn_stats(k.bn[:, i, :], k.x[:, i, :])
            k.bn_made = True

        @block.scalar
        def _(act):
            def gate_silu(e, u):
                act.wait_ge(made.sem, made.at(e + 1))
                act.wait_ge(hidden.sem, hidden.at(e + 1 - 2))
                nc.scalar.activation(gate[:, u], k.ps[:, 0:CT, 0:F0], ACT.Silu).then_inc(silu.sem, 1)

            def output(e, u, nth):
                act.wait_ge(down.sem, down.at(e + 1))
                act.wait_ge(stored[u].sem, stored[u].at(nth * 16))
                nc.scalar.copy(y[:, u, BANK:CT * D], ps[:, DOWN + BANK:DOWN + CT * D]).then_inc(shared_copied.sem, 1)
                nc.scalar.copy(y[:, u, 0:BANK], ps[:, DOWN:DOWN + BANK]).then_inc(copied.sem, 1)
                act.wait_ge(shared_copied.sem, shared_copied.at(e + 1))
                act.wait_ge(copied.sem, copied.at(e + 1))
                act.dma_start(d["expert_out"][bass.ds(e * CAP, CAP), :].rearrange("(s p) n -> p s n", p=P),
                              y[:, u, :].rearrange("p (s n) -> p s n", s=CT)).then_inc(stored[u].sem, 16)

            gate_silu(0, 0)
            with act.Fori(0, E0 // 2 - 1) as it:
                gate_silu(it * 2 + 1, 1)
                output(it * 2, 0, it)
                gate_silu(it * 2 + 2, 0)
                output(it * 2 + 1, 1, it)
            gate_silu(E0 - 1, 1)
            for u in range(2):
                output(E0 - 2 + u, u, E0 // 2 - 1)
            for u in range(2):
                act.wait_ge(stored[u].sem, stored[u].at(8 * E0))

        for u in range(2):
            for n in (rows_loaded[u], in_loaded[u], out_loaded[u], stored[u]):
                n.base += 8 * E0
        for n in (turned, rows_t, made, silu, hidden, hidden_turned, hidden_t, down, copied, shared_copied):
            n.base += E0
        for n in fetched[0] + fetched[1]:
            n.base += 16 * (K0 // 2)
        added.base += NT * K0


def layer_moe(k):
    with Stage(k) as st:
        wr = st.sb("wr", [P, C, E0])
        norm_stage(k, k.x, k.xn,
                   preload=lambda sp: sp.dma_start(wr[:], k.dram["moe_router"]).then_inc(k.count("router_loaded").sem, 16))
        slot_in, slot_out = st.sb("slot_in", [P, NT * K0], I32), st.sb("slot_out", [P, NT * K0], I32)
        weights, col = st.sb("weights", [P, NT, K0]), st.sb("col", [P, NT])
        s_, chosen_by, slot = (st.sb(n, [P, NT, E0]) for n in ("s", "chosen_by", "slot"))
        route_stage(k, wr, s_, col, chosen_by, slot, slot_out)
        dispatch_stage(k, s_, col, chosen_by, slot, slot_out, slot_in, weights)
        experts_stage(k, slot_in, weights)


def dense_experts_stage(k, wr, br):
    nc, d = k.nc, k.dram
    loaded = [k.count(f"dense_loaded_{u}") for u in range(2)]
    made, silu, hidden = k.count("dense_products"), k.count("dense_silu"), k.freed("dense_hidden")
    down, added = k.freed("dense_down"), k.freed("dense_added")
    routed, logits, biased, probs = (k.count(n) for n in ("gate_loaded", "gate_logits", "gate_biased", "gate_probs"))
    steps = k.count("dve_steps")
    R = E1 - 1
    with Stage(k) as st:
        w_in = st.sb("w_in", [P, 2, 2 * C * I1])
        w_out = st.sb("w_out", [I1, 2, D])
        gate = st.sb("gate", [I1, 2, BANK])
        hid = st.sb("hid", [I1, T])
        share = st.sb("share", [P, NT, E1])
        s_ = st.sb("s", [P, NT, E1])
        top = st.sb("top", [P, NT, 8])
        which = st.sb("which", [P, NT, 8], U32)
        which_f = st.sb("which_f", [P, NT, K1])
        pick = st.sb("pick", [P, NT * K1, E1])
        col = st.sb("col", [P, NT])
        block = st.block()

        @block.sync
        def _(sp):
            with sp.Fori(0, E1 // 2) as it:
                for u in range(2):
                    sp.wait_ge(down.sem, down.at(it * (2 * NT // 2) + (u - 1) * (NT // 2)))
                    e = it * 2 + u
                    sp.dma_start(w_in[:, u, :], d["dense_w_in"][bass.ds(e * P, P), :]).then_inc(loaded[u].sem, 16)
                    sp.dma_start(w_out[:, u, :], d["dense_w_out"][bass.ds(e * I1, I1), :]).then_inc(loaded[u].sem, 16)

        @block.tensor
        def _(pe):
            pe.wait_ge(routed.sem, routed.at(32))
            for i in range(NT):
                for c in range(C):
                    last = nc.tensor.matmul(k.ps[:, 7, i * R:(i + 1) * R], k.xt[:, c, i * P:(i + 1) * P], wr[:, c, :],
                                            start=c == 0, stop=c == C - 1)
            last.then_inc(logits.sem, 1)
            with pe.Fori(0, E1 // 2) as it:
                for u in range(2):
                    w = w_in[:, u, :].rearrange("p (g c f) -> p g c f", g=2, c=C)
                    pe.wait_ge(loaded[u].sem, loaded[u].at(it * 32 + 32))
                    for n in range(2):
                        pe.wait_ge(hidden.sem, hidden.at(it * 4 + 2 * u + n + 1 - 2))
                        for g in range(2):
                            for c in range(C):
                                last = nc.tensor.matmul(k.ps[:, 2 * n + g, :], w[:, g, c, :], k.xt[:, c, n * BANK:(n + 1) * BANK],
                                                        start=c == 0, stop=c == C - 1)
                            last.then_inc(made.sem, 1)
                    for n in range(NT // 2):
                        pe.wait_ge(hidden.sem, hidden.at(it * 4 + 2 * u + n // 2 + 1))
                        pe.wait_ge(added.sem, added.at(it * NT + u * (NT // 2) + n + 1 - 4))
                        for i in (2 * n, 2 * n + 1):
                            last = nc.tensor.matmul(k.ps[:, 4 + n, (i % 2) * D:(i % 2 + 1) * D], hid[:, i * P:(i + 1) * P],
                                                    w_out[:, u, :], start=True, stop=True)
                        last.then_inc(down.sem, 1)

        @block.scalar
        def _(act):
            act.wait_ge(biased.sem, biased.at(1))
            nc.scalar.activation(s_[:, :, 0:R], s_[:, :, 0:R], ACT.Sigmoid).then_inc(probs.sem, 1)
            with act.Fori(0, E1 // 2) as it:
                for u in range(2):
                    for n in range(2):
                        j = 2 * u + n
                        act.wait_ge(made.sem, made.at(it * 8 + 2 * j + 1))
                        act.wait_ge(hidden.sem, hidden.at(it * 4 + j + 1 - 2))
                        nc.scalar.activation(gate[:, n, :], k.ps[:, 2 * n, :], ACT.Silu).then_inc(silu.sem, 1)

        @block.vector
        def _(dve):
            s = Steps(dve, steps)
            s.mark(nc.vector.memset(s_[:, :, R:E1], -1.0))
            dve.wait_ge(routed.sem, routed.at(32))
            dve.wait_ge(logits.sem, logits.at(1))
            nc.vector.tensor_tensor(s_[:, :, 0:R], k.ps[:, 7, 0:NT * R].rearrange("p (i e) -> p i e", e=R),
                                    bc(br[:].unsqueeze(1), [P, NT, R]), ALU.add).then_inc(biased.sem, 1)
            dve.wait_ge(probs.sem, probs.at(1))
            s.wait()
            for i in range(NT):
                s.mark(nc.vector.max(top[:, i, :], s_[:, i, :]))
            s.wait()
            for i in range(NT):
                s.mark(nc.vector.max_index(which[:, i, :], top[:, i, :], s_[:, i, :]))
            s.link(nc.vector.reduce_sum(col[:], top[:, :, 0:K1], X_AXIS))
            s.link(nc.vector.reciprocal(col[:], col[:]))
            s.mark(nc.vector.tensor_tensor(top[:, :, 0:K1], top[:, :, 0:K1], bc(col[:].unsqueeze(2), [P, NT, K1]), ALU.mult))
            s.link(nc.vector.tensor_copy(which_f[:], which[:, :, 0:K1]))
            flat = which_f[:].rearrange("p i r -> p (i r)")
            wide = [P, NT * K1, E1]
            s.link(nc.vector.tensor_tensor(pick[:], bc(flat.unsqueeze(2), wide), bc(k.iota[:, 0:1, 0:E1], wide), ALU.is_equal))
            for r in range(K1):
                part = pick[:].rearrange("p (i r) e -> p i r e", r=K1)[:, :, r, :]
                s.mark(nc.vector.tensor_tensor(part, part, bc(top[:, :, r:r + 1], [P, NT, E1]), ALU.mult))
            s.wait()
            s.link(nc.vector.reduce_sum(s_[:], pick[:].rearrange("p (i r) e -> p i e r", r=K1), X_AXIS))
            s.mark(nc.vector.tensor_scalar(share[:, :, 1:E1], s_[:, :, 0:R], 1 / 8, None, ALU.mult))
            s.mark(nc.vector.memset(share[:, :, 0:1], 1 / 8))
            s.link(nc.vector.tensor_tensor(k.x[:], k.x[:], k.xn[:], ALU.add))
            steps.base += s.n
            with dve.Fori(0, E1 // 2) as it:
                for u in range(2):
                    for n in range(2):
                        j = 2 * u + n
                        dve.wait_ge(made.sem, made.at(it * 8 + 2 * j + 2))
                        dve.wait_ge(silu.sem, silu.at(it * 4 + j + 1))
                        dve.wait_ge(down.sem, down.at(it * NT + (u - 1) * (NT // 2) + 2 * n + 2))
                        nc.vector.tensor_tensor(hid[:, n * BANK:(n + 1) * BANK], gate[:, n, :], k.ps[:, 2 * n + 1, :], ALU.mult)\
                            .then_inc(hidden.sem, 1)
                    for n in range(NT // 2):
                        at = it * NT + u * (NT // 2) + n + 1
                        dve.wait_ge(down.sem, down.at(at))
                        dve.wait_ge(added.sem, added.at(at - NT // 2))
                        for i in (2 * n, 2 * n + 1):
                            last = nc.vector.scalar_tensor_tensor(k.x[:, i, :], k.ps[:, 4 + n, (i % 2) * D:(i % 2 + 1) * D],
                                                                  share[:, i, bass.ds(it * 2 + u, 1)], k.x[:, i, :],
                                                                  ALU.mult, ALU.add)
                        last.then_inc(added.sem, 1)

        for u in range(2):
            loaded[u].base += 16 * E1
        for n in (logits, biased, probs):
            n.base += 1
        routed.base += 32
        made.base += 4 * E1
        silu.base += 2 * E1
        hidden.base += 2 * E1
        down.base += NT // 2 * E1
        added.base += NT // 2 * E1


def layer_mla(k):
    small_attention(k, "mla")
    with Stage(k) as st:
        wr = st.sb("wr", [P, C, E1 - 1])
        br = st.sb("br", [P, E1 - 1])

        def load_router(sp):
            sp.dma_start(wr[:], k.dram["gate_router"]).then_inc(k.count("gate_loaded").sem, 16)
            sp.dma_start(br[:], bc(k.dram["gate_bias"], [P, E1 - 1])).then_inc(k.count("gate_loaded").sem, 16)

        norm_stage(k, k.xn, None, k.dram["ln2"], layernorm=False, preload=load_router)
        dense_experts_stage(k, wr, br)


ZERO_DMAS = 24


def shifted_project_stage(k, w, load_head, qg, kg, mix, rk, rq):
    nc, d = k.nc, k.dram
    loaded = [k.count(f"qk_loaded_{u}") for u in range(2)]
    params, folded = k.count("qk_params"), k.count("qk_folded")
    made, squared, scaled = k.freed("qk_products"), k.freed("qk_squared"), k.freed("qk_scaled")
    summed = k.freed("qk_summed")
    totals, based, inverse, spread = (k.count(n) for n in ("qk_totals", "qk_based", "qk_inverse", "qk_spread"))
    steps = k.count("dve_steps")
    with Stage(k) as st:
        bg = st.sb("bg", [P, 2, 2, H])
        bgain = st.sb("bgain", [P, 2, H])
        sq = st.sb("sq", [P, 2, T])
        acc = st.sb("acc", [P, 2, T])
        base = st.sb("base", [P, 2 * NT])
        inv = st.sb("inv", [P, 2 * NT])
        wide = st.sb("wide", [P, NT, P])
        roll = st.sb("roll", [P, len(ROLLS), P])
        w_mix = st.sb("w_mix", [P, len(ROLLS)])
        block = st.block()
        ps = k.ps_flat

        @block.sync
        def _(sp):
            sp.dma_start(bg[:], d["shifted_bg"]).then_inc(params.sem, 16)
            sp.dma_start(roll[:], d["c_roll"]).then_inc(params.sem, 16)
            sp.dma_start(w_mix[:], bc(d["shifted_mix"], [P, len(ROLLS)])).then_inc(params.sem, 16)
            with sp.Fori(0, H // 2 - 1) as it:
                for u in range(2):
                    sp.wait_ge(made.sem, made.at(it * 4 + 2 * u + 2))
                    load_head(sp, it * 2 + 2 + u, u)

        @block.tensor
        def _(pe):
            with pe.Fori(0, H // 2) as it:
                for u in range(2):
                    ww = w[:, u, :].rearrange("p (g c f) -> p g c f", g=2, c=C)
                    pe.wait_ge(loaded[u].sem, loaded[u].at(it * 16 + 16))
                    for g in range(2):
                        pe.wait_ge(scaled.sem, scaled.at(it * 4 + 2 * u + g + 1 - 4))
                        for n in range(2):
                            for c in range(C):
                                last = nc.tensor.matmul(k.ps[:, 4 * u + 2 * g + n, :], ww[:, g, c, :],
                                                        k.xt[:, c, n * BANK:(n + 1) * BANK], start=c == 0, stop=c == C - 1)
                        last.then_inc(made.sem, 1)
            pe.wait_ge(summed.sem, summed.at(2 * H))
            for g in range(2):
                for i in range(NT):
                    last = nc.tensor.matmul(ps[:, g * NT + i:g * NT + i + 1], acc[:, g, i * P:(i + 1) * P], k.ones[:, 0:1],
                                            start=True, stop=True)
            last.then_inc(totals.sem, 1)
            pe.wait_ge(inverse.sem, inverse.at(2))
            for i in range(NT):
                last = nc.tensor.matmul(ps[:, 2 * BANK + i * P:2 * BANK + (i + 1) * P], wide[:, i, :], k.ident[:],
                                        start=True, stop=True)
            last.then_inc(spread.sem, 1)

        @block.scalar
        def _(act):
            act.wait_ge(params.sem, params.at(48))
            with act.Fori(0, H // 2) as it:
                for u in range(2):
                    for g in range(2):
                        at = it * 4 + 2 * u + g
                        act.wait_ge(made.sem, made.at(at + 1))
                        act.wait_ge(summed.sem, summed.at(at - 1))
                        bank = (4 * u + 2 * g) * BANK
                        nc.scalar.activation(sq[:, g, :], ps[:, bank:bank + T], ACT.Square,
                                             bias=bg[:, g, 0, bass.ds(it * 2 + u, 1)]).then_inc(squared.sem, 1)

        @block.gpsimd
        def _(pool):
            pool.wait_ge(based.sem, based.at(1))
            nc.gpsimd.tensor_tensor(inv[:], base[:], k.minus_half[:], ALU.pow).then_inc(inverse.sem, 1)

        @block.vector
        def _(dve):
            s = Steps(dve, steps)
            dve.wait_ge(params.sem, params.at(48))
            s.link(nc.vector.tensor_tensor(bgain[:], bg[:, :, 0, :], bg[:, :, 1, :], ALU.mult))
            s.link(nc.vector.tensor_scalar(mix[:], roll[:, 0, :], w_mix[:, 0:1], None, ALU.mult))
            for n in range(1, len(ROLLS)):
                s.link(nc.vector.scalar_tensor_tensor(mix[:], roll[:, n, :], w_mix[:, n:n + 1], mix[:], ALU.mult, ALU.add))
            s.link(nc.vector.memset(acc[:], 0.0))
            with dve.Fori(0, H // 2) as it:
                for u in range(2):
                    for g, dst in ((0, qg), (1, kg)):
                        at = it * 4 + 2 * u + g
                        dve.wait_ge(made.sem, made.at(at + 1))
                        dve.wait_ge(squared.sem, squared.at(at + 1))
                        h = it * 2 + u
                        bank = (4 * u + 2 * g) * BANK
                        nc.vector.tensor_scalar(dst[:, bass.ds(h * T, T)], ps[:, bank:bank + T],
                                                bg[:, g, 1, bass.ds(h, 1)], bgain[:, g, bass.ds(h, 1)], ALU.mult, ALU.add)\
                            .then_inc(scaled.sem, 1)
                        dve.wait_ge(summed.sem, summed.at(at - 1))
                        nc.vector.tensor_tensor(acc[:, g, :], acc[:, g, :], sq[:, g, :], ALU.add).then_inc(summed.sem, 1)
            dve.wait_ge(totals.sem, totals.at(1))
            nc.vector.tensor_scalar(base[:], ps[:, 0:2 * NT], 1.0 / (H * D2), EPS_SHIFTED, ALU.mult, ALU.add)\
                .then_inc(based.sem, 1)
            dve.wait_ge(inverse.sem, inverse.at(1))
            nc.vector.tensor_scalar(rq[:], inv[:, 0:NT], D2 ** -0.5, None, ALU.mult)
            nc.vector.tensor_copy(wide[:], bc(inv[:, NT:2 * NT].unsqueeze(2), [P, NT, P])).then_inc(inverse.sem, 1)
            dve.wait_ge(spread.sem, spread.at(1))
            nc.vector.tensor_copy(rk[:], ps[:, 2 * BANK:2 * BANK + T])
            steps.base += s.n

        params.base += 48
        for u in range(2):
            loaded[u].base += 8 * H
        for n in (made, squared, scaled):
            n.base += 2 * H
        summed.base += 2 * H
        for n in (totals, based, spread):
            n.base += 1
        inverse.base += 2


def shifted_attention_stage(k, qg, kg, mix, rk, rq):
    nc, d = k.nc, k.dram
    loaded = [k.count(f"vo_loaded_{u}") for u in range(2)]
    keys_ready, mixed_made, mixed = k.count("band_keys"), k.count("mixed_products"), k.count("mixed_copied")
    v_made, v_copied = k.count("head_values"), k.count("head_values_copied")
    scored, shifted, exped, probs = (k.count(n) for n in ("band_scored", "band_shift", "band_exps", "band_probs"))
    turned, turned_copied = k.count("band_turned"), k.freed("band_turned_copied")
    summed, copied = k.freed("band_summed"), k.freed("band_copied")
    projected, added, params = k.freed("band_projected"), k.freed("band_added"), k.count("band_params")
    steps = k.count("dve_steps")
    W = PAD_L + T + PAD_R
    N = 2 * NT
    with Stage(k) as st:
        wv = st.sb("wv", [P, 2, C * P])
        wo = st.sb("wo", [P, 2, D])
        bv = st.sb("bv", [P, H])
        bo = st.sb("bo", [P, D])
        nrq = st.sb("nrq", [P, NT])
        kb = st.sb("kb", [P, 2, W])
        qm = st.sb("qm", [P, 2, T])
        vh = st.sb("vh", [P, 2, T])
        pr = st.sb("pr", [P, 4, BAND])
        pt = st.sb("pt", [P, 2, 3 * P])
        stat = st.sb("stat", [P, 4, N])
        ot = k.xn[:].rearrange("p i n -> p (i n)").rearrange("p (u t) -> p u t", u=2)
        block = st.block()
        ps = k.ps_flat

        @block.sync
        def _(sp):
            sp.dma_start(bv[:], d["shifted_bv"]).then_inc(params.sem, 16)
            sp.dma_start(bo[:], bc(d["shifted_bo"], [P, D])).then_inc(params.sem, 16)
            with sp.Fori(0, H // 2) as it:
                for u in range(2):
                    sp.wait_ge(projected.sem, projected.at(it * 2 + u + 1 - 2))
                    h = it * 2 + u
                    sp.dma_start(wv[:, u, :], d["shifted_w_v"][bass.ds(h * P, P), :]).then_inc(loaded[u].sem, 16)
                    sp.dma_start(wo[:, u, :], d["shifted_wo"][bass.ds(h * P, P), :]).then_inc(loaded[u].sem, 16)

        @block.tensor
        def _(pe):
            with pe.Fori(0, H // 2) as it:
                def mix_queries(u):
                    h = it * 2 + u
                    pe.wait_ge(added.sem, added.at(it * 8 + 4 * u - 4))
                    for n in range(2):
                        last = nc.tensor.matmul(k.ps[:, 4 * u + n, :], mix[:], qg[:, bass.ds(h * T + n * BANK, BANK)],
                                                start=True, stop=True)
                    last.then_inc(mixed_made.sem, 1)

                def make_values(u):
                    pe.wait_ge(loaded[u].sem, loaded[u].at(it * 32 + 32))
                    for i in range(NT):
                        for c in range(C):
                            last = nc.tensor.matmul(k.ps[:, 4 * u + 2 + i // 4, (i % 4) * P:(i % 4 + 1) * P],
                                                    k.xt[:, c, i * P:(i + 1) * P], wv[:, u, c * P:(c + 1) * P],
                                                    start=c == 0, stop=c == C - 1)
                    last.then_inc(v_made.sem, 1)

                def score(n):
                    u, i = n // NT, n % NT
                    if i == 0:
                        pe.wait_ge(mixed.sem, mixed.at(it * 2 + u + 1))
                        pe.wait_ge(keys_ready.sem, keys_ready.at(it * 2 + u + 1))
                    if n == 2:
                        pe.wait_ge(v_copied.sem, v_copied.at(it * 2 + 1))
                    nc.tensor.matmul(k.ps[:, n % 4, 0:BAND], qm[:, u, i * P:(i + 1) * P], kb[:, u, i * P:i * P + BAND],
                                     start=True, stop=False)
                    nc.tensor.matmul(k.ps[:, n % 4, 0:BAND], k.ident_bf[:], k.mask_band[:], start=False, stop=True)\
                        .then_inc(scored.sem, 1)

                def turn(n):
                    if n == 0:
                        pe.wait_ge(mixed.sem, mixed.at(it * 2 + 2))
                    pe.wait_ge(probs.sem, probs.at(it * N + n + 1))
                    pe.wait_ge(turned_copied.sem, turned_copied.at(it * N + n + 1 - 2))
                    for b in range(3):
                        rows = min(P, BAND - b * P)
                        last = nc.tensor.transpose(k.ps[0:rows, 4 + n % 2, b * P:(b + 1) * P], pr[:, n % 4, b * P:b * P + rows],
                                                   k.ident[:])
                    last.then_inc(turned.sem, 1)

                def value(n):
                    u, i = n // NT, n % NT
                    if n == 0:
                        pe.wait_ge(v_copied.sem, v_copied.at(it * 2 + 2))
                    pe.wait_ge(turned_copied.sem, turned_copied.at(it * N + n + 1))
                    pe.wait_ge(copied.sem, copied.at(it * N + n + 1 - 2))
                    for b in range(3):
                        rows, j = min(P, BAND - b * P), (i - 1 + b) % NT
                        last = nc.tensor.matmul(k.ps[:, 6 + n % 2, 0:P], vh[0:rows, u, j * P:(j + 1) * P],
                                                pt[0:rows, n % 2, b * P:(b + 1) * P], start=b == 0, stop=b == 2)
                    last.then_inc(summed.sem, 1)

                def project(u, n):
                    for i in (2 * n, 2 * n + 1):
                        last = nc.tensor.matmul(k.ps[:, 4 * u + n, (i % 2) * D:(i % 2 + 1) * D], ot[:, u, i * P:(i + 1) * P],
                                                wo[:, u, :], start=True, stop=True)
                    if n == NT // 2 - 1:
                        last.then_inc(projected.sem, 1)

                mix_queries(0)
                make_values(0)
                mix_queries(1)
                score(0)
                make_values(1)
                for n in range(1, N + 3):
                    if n < N:
                        score(n)
                    if 2 <= n < N + 2:
                        turn(n - 2)
                    if n == N:
                        pe.wait_ge(exped.sem, exped.at(it * N + N))
                        pe.wait_ge(copied.sem, copied.at(it * N + NT))
                    if N <= n < N + 2:
                        project(0, n - N)
                    if n >= 3:
                        value(n - 3)
                project(0, 2)
                project(0, 3)
                pe.wait_ge(copied.sem, copied.at(it * N + N))
                for n in range(NT // 2):
                    project(1, n)

        @block.scalar
        def _(act):
            with act.Fori(0, H // 2) as it:
                def copy_queries(u):
                    act.wait_ge(mixed_made.sem, mixed_made.at(it * 2 + u + 1))
                    nc.scalar.copy(qm[:, u, :], ps[:, 4 * u * BANK:(4 * u + 2) * BANK]).then_inc(mixed.sem, 1)

                def copy_values(u):
                    act.wait_ge(v_made.sem, v_made.at(it * 2 + u + 1))
                    nc.scalar.copy(vh[:, u, :], ps[:, (4 * u + 2) * BANK:(4 * u + 4) * BANK]).then_inc(v_copied.sem, 1)

                copy_queries(0)
                copy_values(0)
                copy_queries(1)
                for n in range(N + 2):
                    if n < N:
                        act.wait_ge(shifted.sem, shifted.at(it * N + n + 1))
                        nc.scalar.activation(pr[:, n % 4, :], k.ps[:, n % 4, 0:BAND], ACT.Exp, bias=stat[:, 1, n:n + 1],
                                             scale=rq[:, n % NT:n % NT + 1], accum_out=stat[:, 2, n:n + 1]).then_inc(exped.sem, 1)
                    if n == 0:
                        copy_values(1)
                    if n >= 2:
                        m = n - 2
                        act.wait_ge(turned.sem, turned.at(it * N + m + 1))
                        act.wait_ge(summed.sem, summed.at(it * N + m + 1 - 2))
                        nc.scalar.copy(pt[:, m % 2, 0:2 * P], k.ps[:, 4 + m % 2, 0:2 * P])
                        nc.scalar.copy(pt[0:PAD_R, m % 2, 2 * P:3 * P], k.ps[0:PAD_R, 4 + m % 2, 2 * P:3 * P])\
                            .then_inc(turned_copied.sem, 1)

        @block.vector
        def _(dve):
            s = Steps(dve, steps)
            dve.wait_ge(params.sem, params.at(32))
            s.mark(nc.vector.tensor_scalar(nrq[:], rq[:], -1.0, None, ALU.mult))
            s.link(nc.vector.tensor_tensor(k.x[:], k.x[:], bc(bo[:].unsqueeze(1), [P, NT, D]), ALU.add))
            steps.base += s.n
            before = 0
            with dve.Fori(0, H // 2) as it:
                s = Steps(dve, steps, it * (2 * N))
                for u in range(2):
                    h = it * 2 + u
                    nc.vector.tensor_tensor(kb[:, u, PAD_L:PAD_L + T], kg[:, bass.ds(h * T, T)], rk[:], ALU.mult)
                    nc.vector.tensor_tensor(kb[:, u, 0:PAD_L], kg[:, bass.ds(h * T + T - PAD_L, PAD_L)], rk[:, T - PAD_L:T], ALU.mult)
                    nc.vector.tensor_tensor(kb[:, u, PAD_L + T:W], kg[:, bass.ds(h * T, PAD_R)], rk[:, 0:PAD_R], ALU.mult)\
                        .then_inc(keys_ready.sem, 1)
                for n in range(N + 4):
                    if n < N:
                        dve.wait_ge(scored.sem, scored.at(it * N + n + 1))
                        s.link(nc.vector.reduce_max(stat[:, 0, n:n + 1], k.ps[:, n % 4, 0:BAND], X_AXIS))
                        nc.vector.tensor_tensor(stat[:, 1, n:n + 1], stat[:, 0, n:n + 1], nrq[:, n % NT:n % NT + 1], ALU.mult)\
                            .then_inc(shifted.sem, 1)
                    if 1 <= n <= N:
                        m = n - 1
                        dve.wait_ge(exped.sem, exped.at(it * N + m + 1))
                        s.link(nc.vector.reciprocal(stat[:, 3, m:m + 1], stat[:, 2, m:m + 1]))
                        nc.vector.tensor_scalar(pr[:, m % 4, :], pr[:, m % 4, :], stat[:, 3, m:m + 1], None, ALU.mult)\
                            .then_inc(probs.sem, 1)
                    if n >= 4:
                        m = n - 4
                        u, i = m // NT, m % NT
                        dve.wait_ge(summed.sem, summed.at(it * N + m + 1))
                        nc.vector.tensor_scalar(ot[:, u, i * P:(i + 1) * P], k.ps[:, 6 + m % 2, 0:P], bv[:, bass.ds(it * 2 + u, 1)],
                                                None, ALU.add).then_inc(copied.sem, 1)
                assert s.n == 2 * N
                for u in range(2):
                    dve.wait_ge(projected.sem, projected.at(it * 2 + u + 1))
                    for n in range(NT // 2):
                        pair = k.x[:, 2 * n:2 * n + 2, :].rearrange("p i n -> p (i n)")
                        dve.wait_ge(added.sem, added.at(it * 8 + 4 * u + n + 1 - 4))
                        nc.vector.tensor_tensor(pair, pair, k.ps[:, 4 * u + n, :], ALU.add).then_inc(added.sem, 1)
            steps.base += H // 2 * 2 * N

        params.base += 32
        for u in range(2):
            loaded[u].base += 16 * H
        for n in (keys_ready, mixed_made, mixed, v_made, v_copied, projected):
            n.base += H
        for n in (scored, shifted, exped, probs, turned, turned_copied, summed, copied):
            n.base += H * NT
        added.base += 4 * H


def layer_shifted(k):
    with Stage(k) as st:
        qg, kg = st.sb("qg", [P, H * T]), st.sb("kg", [P, H * T])
        mix, rk, rq = st.sb("mix", [P, P]), st.sb("rk", [P, T]), st.sb("rq", [P, NT])
        with Stage(k) as inner:
            w = inner.sb("w", [P, 2, 2 * C * P])

            def load_head(sp, h, u):
                sp.dma_start(w[:, u, :], k.dram["shifted_w_qk"][bass.ds(h * P, P), :]).then_inc(k.count(f"qk_loaded_{u}").sem, 16)

            def load_first(sp):
                for u in range(2):
                    load_head(sp, u, u)

            norm_stage(k, k.x, k.xn, preload=load_first)
            shifted_project_stage(k, w, load_head, qg, kg, mix, rk, rq)
        shifted_attention_stage(k, qg, kg, mix, rk, rq)


def differential_stage(k, w, bv, load_group):
    nc, d = k.nc, k.dram
    params, lam_dot, lam_exp = k.count("diff_params"), k.count("diff_dots"), k.count("diff_dot_exps")
    w_loaded, wo_loaded = k.count("diff_w_loaded"), k.count("diff_wo_loaded")
    made, by_act, by_dve = k.freed("diff_made"), k.freed("diff_copied_act"), k.freed("diff_copied_dve")
    scored, shifted, exped, probs = (k.count(n) for n in ("diff_scored", "diff_shift", "diff_exps", "diff_probs"))
    turned, turned_copied = k.count("diff_turned"), k.freed("diff_turned_copied")
    summed, taken = k.freed("diff_summed"), k.freed("diff_taken")
    rows = k.count("diff_rows")
    projected, added = k.freed("diff_projected"), k.freed("diff_added")
    steps, pool_steps = k.count("dve_steps"), k.count("pool_steps")
    G, Q = 4, 6
    N = 2 * NT
    V = 2 * D2
    scale = D2 ** -0.5
    HEAD_BANK = [2, 6, 0, 4, 2, 0]
    OUT_BANK = [0, 1, 4, 5]
    BEHIND = 3
    R = N + BEHIND
    DV = 2 * N + 2 * N
    with Stage(k) as st:
        wo = st.sb("wo", [P, 4 * D])
        bo = st.sb("bo", [P, D])
        sub = st.sb("sub", [P, C])
        lam_in = st.sb("lam_in", [P, 4, D2])
        lam = st.sb("lam", [P, 4])
        qt = st.sb("qt", [P, 4, T])
        kt = st.sb("kt", [P, 2, T])
        v = st.sb("v", [P, NT, V])
        e = st.sb("e", [P, 2, 2, T])
        pt = st.sb("pt", [P, 2, T])
        o = st.sb("o", [P, N, V])
        square = st.sb("square", [P, 2, V])
        stat = st.sb("stat", [P, 4, 2, N])
        ss = st.sb("ss", [P, 3, N])
        eps = st.sb("eps", [P, 1])
        block = st.block()
        ps = k.ps_flat
        weights = w[:, 0:C * (Q * P + V)].rearrange("p (c n) -> p c n", c=C)
        bias = w[:, C * (Q * P + V):]

        @block.sync
        def _(sp):
            sp.dma_start(bo[:], bc(d["diff_bo"], [P, D])).then_inc(params.sem, 16)
            sp.dma_start(sub[:], d["diff_sub"]).then_inc(params.sem, 16)
            sp.dma_start(lam_in[:], bc(d["diff_lambda"].unsqueeze(0), [P, 4, D2])).then_inc(params.sem, 16)
            sp.dma_start(wo[:], d["diff_wo"][0:P, :]).then_inc(wo_loaded.sem, 16)
            with sp.Fori(0, G - 1) as it:
                sp.wait_ge(made.sem, made.at((it + 1) * (Q + 2)))
                sp.wait_ge(by_act.sem, by_act.at((it + 1) * 3))
                sp.wait_ge(by_dve.sem, by_dve.at((it + 1) * 5))
                load_group(sp, it + 1)
                sp.wait_ge(projected.sem, projected.at((it + 1) * 4))
                sp.dma_start(wo[:], d["diff_wo"][bass.ds((it + 1) * P, P), :]).then_inc(wo_loaded.sem, 16)

        @block.tensor
        def _(pe):
            with pe.Fori(0, G) as it:
                pe.wait_ge(w_loaded.sem, w_loaded.at(it * 32 + 32))
                for h in range(Q):
                    if h in (2, 3):
                        pe.wait_ge(added.sem, added.at(it * 4 + 2 * (h - 1) - 4))
                    if h == 4:
                        pe.wait_ge(by_act.sem, by_act.at(it * 3 + 1))
                    if h == 5:
                        pe.wait_ge(by_act.sem, by_act.at(it * 3 + 2))
                    for n in range(2):
                        for c in range(C):
                            last = nc.tensor.matmul(k.ps[:, HEAD_BANK[h] + n, :], weights[:, c, h * P:(h + 1) * P],
                                                    k.xt[:, c, n * BANK:(n + 1) * BANK], start=c == 0, stop=c == C - 1)
                    last.then_inc(made.sem, 1)
                def make_values(tiles):
                    for i in tiles:
                        for c in range(C):
                            last = nc.tensor.matmul(k.ps[:, 4 + i // 2, (i % 2) * V:(i % 2 + 1) * V], k.xt[:, c, i * P:(i + 1) * P],
                                                    weights[:, c, Q * P:Q * P + V], start=c == 0, stop=c == C - 1)
                    return last

                def score(n):
                    u, i = n // NT, n % NT
                    for m in range(2):
                        if n:
                            pe.wait_ge(exped.sem, exped.at(it * (2 * N) + 2 * n - 1 + m))
                        width = (i + 1) * P
                        for col in range(0, width, BANK):
                            x = min(BANK, width - col)
                            nc.tensor.matmul(ps[:, m * T + col:m * T + col + x], qt[:, 2 * u + m, i * P:(i + 1) * P],
                                             kt[:, m, col:col + x], start=True, stop=col + x < width)
                        nc.tensor.matmul(ps[:, m * T + i * P:m * T + (i + 1) * P], k.ident_bf[:], k.mask_q[:],
                                         start=False, stop=True).then_inc(scored.sem, 1)

                def turn(n):
                    i = n % NT
                    if n == 0:
                        pe.wait_ge(by_dve.sem, by_dve.at(it * 5 + 4))
                    pe.wait_ge(probs.sem, probs.at(it * N + n + 1))
                    pe.wait_ge(turned_copied.sem, turned_copied.at(it * N + n))
                    for j in range(i + 1):
                        last = nc.tensor.transpose(ps[:, 4 * BANK + j * P:4 * BANK + (j + 1) * P], e[:, n % 2, 0, j * P:(j + 1) * P],
                                                   k.ident[:])
                    last.then_inc(turned.sem, 1)

                def value(n):
                    i = n % NT
                    pe.wait_ge(taken.sem, taken.at(it * R + n + 1 - 2))
                    if n >= BEHIND:
                        pe.wait_ge(rows.sem, rows.at(it * N + n - BEHIND + 1))
                        for c in range(2):
                            last = nc.tensor.transpose(k.ps[:, 6 + n % 2, V + c * P:V + (c + 1) * P],
                                                       o[:, n - BEHIND, c * P:(c + 1) * P], k.ident[:])
                    if n == 0:
                        pe.wait_ge(by_dve.sem, by_dve.at(it * 5 + 5))
                    if n < N:
                        pe.wait_ge(turned_copied.sem, turned_copied.at(it * N + n + 1))
                        for j in range(i + 1):
                            last = nc.tensor.matmul(k.ps[:, 6 + n % 2, 0:V], pt[:, n % 2, j * P:(j + 1) * P], v[:, j, :],
                                                    start=j == 0, stop=j == i)
                    last.then_inc(summed.sem, 1)

                def project(i):
                    if i == 0:
                        pe.wait_ge(wo_loaded.sem, wo_loaded.at(it * 16 + 16))
                    pe.wait_ge(taken.sem, taken.at(it * R + N - NT + i + BEHIND + 1))
                    for ch in range(4):
                        last = nc.tensor.matmul(k.ps[:, OUT_BANK[i // 2], (i % 2) * D:(i % 2 + 1) * D], qt[:, ch, i * P:(i + 1) * P],
                                                wo[:, ch * D:(ch + 1) * D], start=ch == 0, stop=ch == 3)
                    if i % 2:
                        last.then_inc(projected.sem, 1)

                pe.wait_ge(by_dve.sem, by_dve.at(it * 5 + 2))
                make_values(range(0, NT // 2)).then_inc(made.sem, 1)
                pe.wait_ge(by_act.sem, by_act.at(it * 3 + 3))
                pe.wait_ge(by_dve.sem, by_dve.at(it * 5 + 3))
                score(0)
                make_values(range(NT // 2, NT)).then_inc(made.sem, 1)
                for n in range(1, N):
                    score(n)
                    if n >= 2:
                        value(n - 2)
                    turn(n - 1)
                value(N - 2)
                pe.wait_ge(exped.sem, exped.at((it + 1) * (2 * N)))
                project(0)
                turn(N - 1)
                project(1)
                value(N - 1)
                project(2)
                value(N)
                project(3)
                value(N + 1)
                project(4)
                value(N + 2)
                for i in range(5, NT):
                    project(i)

        @block.scalar
        def _(act):
            act.wait_ge(lam_dot.sem, lam_dot.at(1))
            nc.scalar.activation(lam[:, 0:2], lam[:, 0:2], ACT.Exp).then_inc(lam_exp.sem, 1)
            act.wait_ge(lam_dot.sem, lam_dot.at(2))
            with act.Fori(0, G) as it:
                for h in (0, 2, 4):
                    act.wait_ge(made.sem, made.at(it * (Q + 2) + h + 1))
                    dst = qt[:, h, :] if h < 4 else kt[:, h - 4, :]
                    bank = HEAD_BANK[h] * BANK
                    nc.scalar.activation(dst, ps[:, bank:bank + T], ACT.Identity, bias=bias[:, h:h + 1]).then_inc(by_act.sem, 1)
                for n in range(R + 2):
                    i = n % NT
                    if n < N:
                        for m in range(2):
                            act.wait_ge(shifted.sem, shifted.at(it * (2 * N) + 2 * n + m + 1))
                            if m == 0 and n >= 2:
                                act.wait_ge(turned.sem, turned.at(it * N + n - 1))
                            width = (i + 1) * P
                            nc.scalar.activation(e[:, n % 2, m, 0:width], ps[:, m * T:m * T + width], ACT.Exp,
                                                 bias=stat[:, 1, m, n:n + 1], scale=scale, accum_out=stat[:, 2, m, n:n + 1])\
                                .then_inc(exped.sem, 1)
                    if n >= 2:
                        m = n - 2
                        act.wait_ge(summed.sem, summed.at(it * R + m + 1))
                        if m >= BEHIND:
                            u, tile = divmod(m - BEHIND, NT)
                            for c in range(2):
                                last = nc.scalar.activation(qt[:, 2 * u + c, tile * P:(tile + 1) * P],
                                                            k.ps[:, 6 + m % 2, V + c * P:V + (c + 1) * P], ACT.Copy,
                                                            scale=sub[:, c:c + 1])
                        if m < N:
                            if m >= 2:
                                act.wait_ge(taken.sem, taken.at(it * R + m + 1 - 2))
                            nc.scalar.activation(o[:, m, :], k.ps[:, 6 + m % 2, 0:V], ACT.Copy, scale=stat[:, 3, 0, m:m + 1])
                            last = nc.scalar.activation(square[:, m % 2, :], k.ps[:, 6 + m % 2, 0:V], ACT.Square,
                                                        scale=stat[:, 3, 0, m:m + 1], accum_out=ss[:, 0, m:m + 1])
                        last.then_inc(taken.sem, 1)
                    if 1 <= n <= N:
                        m = n - 1
                        width = (m % NT + 1) * P
                        act.wait_ge(turned.sem, turned.at(it * N + m + 1))
                        if m >= 2:
                            act.wait_ge(summed.sem, summed.at(it * R + m + 1 - 2))
                        nc.scalar.copy(pt[:, m % 2, 0:width], ps[:, 4 * BANK:4 * BANK + width]).then_inc(turned_copied.sem, 1)

        @block.vector
        def _(dve):
            s = Steps(dve, steps)
            dve.wait_ge(params.sem, params.at(48))
            for n in range(2):
                s.link(nc.vector.tensor_tensor(lam_in[:, 2 * n, :], lam_in[:, 2 * n, :], lam_in[:, 2 * n + 1, :], ALU.mult))
            s.mark(nc.vector.reduce_sum(lam[:, 0:1], lam_in[:, 0, :], X_AXIS))
            nc.vector.reduce_sum(lam[:, 1:2], lam_in[:, 2, :], X_AXIS).then_inc(lam_dot.sem, 1)
            dve.wait_ge(lam_exp.sem, lam_exp.at(1))
            s.link(nc.vector.tensor_tensor(lam[:, 2:3], lam[:, 1:2], lam[:, 0:1], ALU.subtract))
            s.link(nc.vector.tensor_scalar(lam[:, 3:4], lam[:, 2:3], -LAMBDA_INIT, None, ALU.add))
            nc.vector.tensor_scalar(sub[:], sub[:], (1.0 - LAMBDA_INIT) * V ** 0.5, None, ALU.mult).then_inc(lam_dot.sem, 1)
            s.link(nc.vector.tensor_tensor(k.x[:], k.x[:], bc(bo[:].unsqueeze(1), [P, NT, D]), ALU.add))
            steps.base += s.n
            with dve.Fori(0, G) as it:
                s = Steps(dve, steps, it * DV)
                dve.wait_ge(w_loaded.sem, w_loaded.at(it * 32 + 32))
                for h in (1, 3, 5):
                    dve.wait_ge(made.sem, made.at(it * (Q + 2) + h + 1))
                    dst = qt[:, h, :] if h < 4 else kt[:, h - 4, :]
                    bank = HEAD_BANK[h] * BANK
                    nc.vector.tensor_scalar(dst, ps[:, bank:bank + T], bias[:, h:h + 1], None, ALU.add).then_inc(by_dve.sem, 1)

                def copy_values(half):
                    tiles = slice(half * NT // 2, (half + 1) * NT // 2)
                    dve.wait_ge(made.sem, made.at(it * (Q + 2) + Q + 1 + half))
                    bank = (4 + 2 * half) * BANK
                    nc.vector.tensor_tensor(v[:, tiles, :], ps[:, bank:bank + T].rearrange("p (i n) -> p i n", n=V),
                                            bc(bv[:].unsqueeze(1), [P, NT // 2, V]), ALU.add).then_inc(by_dve.sem, 1)

                copy_values(0)
                for n in range(N + 1):
                    if n >= 1:
                        m = n - 1
                        width = (m % NT + 1) * P
                        first, second = e[:, m % 2, 0, 0:width], e[:, m % 2, 1, 0:width]
                        dve.wait_ge(exped.sem, exped.at(it * (2 * N) + 2 * m + 2))
                        s.link(nc.vector.reciprocal(stat[:, 3, :, m], stat[:, 2, :, m]))
                        s.link(nc.vector.scalar_tensor_tensor(stat[:, 3, 1, m:m + 1], stat[:, 3, 1, m:m + 1], lam[:, 3:4],
                                                              stat[:, 2, 0, m:m + 1], ALU.mult, ALU.mult))
                        nc.vector.scalar_tensor_tensor(first, second, stat[:, 3, 1, m:m + 1], first, ALU.mult, ALU.add)\
                            .then_inc(probs.sem, 1)
                    if n < N:
                        width = (n % NT + 1) * P
                        for m in range(2):
                            dve.wait_ge(scored.sem, scored.at(it * (2 * N) + 2 * n + m + 1))
                            s.link(nc.vector.reduce_max(stat[:, 0, m, n:n + 1], ps[:, m * T:m * T + width], X_AXIS))
                            nc.vector.tensor_scalar(stat[:, 1, m, n:n + 1], stat[:, 0, m, n:n + 1], -scale, None, ALU.mult)\
                                .then_inc(shifted.sem, 1)
                    if n == 0:
                        copy_values(1)
                assert s.n == DV, s.n
                for n in range(NT // 2):
                    dve.wait_ge(projected.sem, projected.at(it * 4 + n + 1))
                    pair = k.x[:, 2 * n:2 * n + 2, :].rearrange("p i n -> p (i n)")
                    dve.wait_ge(added.sem, added.at(it * 4 + n + 1 - 4))
                    nc.vector.tensor_tensor(pair, pair, k.ps[:, OUT_BANK[n], :], ALU.add).then_inc(added.sem, 1)
            steps.base += G * DV

        @block.gpsimd
        def _(pool):
            s = Steps(pool, pool_steps)
            s.link(nc.gpsimd.memset(eps[:], V * EPS))
            pool_steps.base += s.n
            with pool.Fori(0, G) as it:
                s = Steps(pool, pool_steps, it * (2 * N))
                for n in range(N):
                    pool.wait_ge(taken.sem, taken.at(it * R + n + 1))
                    s.link(nc.gpsimd.tensor_tensor(ss[:, 1, n:n + 1], ss[:, 0, n:n + 1], eps[:], ALU.add))
                    s.link(nc.gpsimd.tensor_tensor(ss[:, 2, n:n + 1], ss[:, 1, n:n + 1], k.minus_half[:, 0:1], ALU.pow))
                    nc.gpsimd.tensor_tensor(o[:, n, :], o[:, n, :], bc(ss[:, 2, n:n + 1], [P, V]), ALU.mult)\
                        .then_inc(rows.sem, 1)
            pool_steps.base += G * 2 * N

        params.base += 48
        lam_dot.base += 2
        lam_exp.base += 1
        w_loaded.base += 32 * G
        wo_loaded.base += 16 * G
        made.base += (Q + 2) * G
        by_act.base += 3 * G
        by_dve.base += 5 * G
        for n in (scored, shifted, exped):
            n.base += 2 * N * G
        for n in (probs, turned, turned_copied, rows):
            n.base += N * G
        for n in (summed, taken):
            n.base += R * G
        projected.base += 4 * G
        added.base += 4 * G


def layer_differential(k):
    with Stage(k) as st:
        w = st.sb("w", [P, C * (6 * P + 2 * D2) + 6])
        bv = st.sb("bv", [P, 2 * D2])

        def load_group(sp, group):
            sp.dma_start(w[:], k.dram["diff_w"][bass.ds(group * P, P), :]).then_inc(k.count("diff_w_loaded").sem, 16)
            sp.dma_start(bv[:], bc(k.dram["diff_bv"][bass.ds(group, 1), :], [P, 2 * D2])).then_inc(k.count("diff_w_loaded").sem, 16)

        norm_stage(k, k.x, k.xn, preload=lambda sp: load_group(sp, 0))
        differential_stage(k, w, bv, load_group)


def program(nc, dram, out, layers):
    with ExitStack() as ctx:
        k = Kernel(nc, ctx, dram)
        sb = lambda name, shape, dt=F32: ctx.enter_context(nc.sbuf_tensor(name, shape, dt))
        k.ps = ctx.enter_context(nc.psum_tensor("ps", [P, 8, BANK], F32))
        k.ps_flat = k.ps[:].rearrange("p b n -> p (b n)")
        k.x, k.xn, k.xt = sb("x", [P, NT, D]), sb("xn", [P, NT, D]), sb("xt", [P, C, T])
        k.bn = sb("bn", [P, NT, 6])
        k.ident, k.ones = sb("ident", [P, P]), sb("ones", [P, P])
        k.ident_bf, k.ones_bf, k.before_bf = (sb(n, [P, P], BF16) for n in ("ident_bf", "ones_bf", "before_bf"))
        k.mask_q, k.mask_k, k.mask_band = sb("mask_q", [P, P], BF16), sb("mask_k", [P, P], BF16), sb("mask_band", [P, BAND], BF16)
        k.iota, k.sel, k.minus_half = sb("iota", [P, 2, E0]), sb("sel", [P, NT, C, P]), sb("minus_half", [P, 2 * NT])
        for name in FREED:
            k.freed(name)
        constants_stage(k)
        for layer in layers:
            LAYERS[layer](k)
        stored = k.count("output_stored")
        with Stage(k) as st:
            block = st.block()

            @block.sync
            def _(sp):
                sp.dma_start(out.rearrange("(i p) n -> p i n", p=P), k.x[:]).then_inc(stored.sem, 16)
                sp.wait_ge(stored.sem, 16)


def layer_mha(k):
    small_attention(k, "mha")


def layer_mqa(k):
    small_attention(k, "mqa")


FREED = ["max_scores_freed", "value_products", "head_copied", "expert_turned", "expert_rows", "expert_products", "expert_hidden", "expert_hidden_copied", "expert_down", "expert_copied", "expert_shared_copied",
         "row_added", "dense_hidden", "dense_down", "dense_added", "qk_products", "qk_squared", "qk_scaled",
         "band_turned_copied", "band_summed", "band_copied", "band_projected", "band_added",
         "diff_made", "diff_copied_act", "diff_copied_dve", "diff_turned_copied", "diff_summed", "diff_taken",
         "diff_projected", "diff_added", "head_stored_0", "head_stored_1", "expert_stored_0", "expert_stored_1",
         "qk_summed"]
LAYERS = {"mha": layer_mha, "mqa": layer_mqa, "moe": layer_moe, "mla": layer_mla,
          "shifted": layer_shifted, "differential": layer_differential}


def constant_arrays():
    f = np.float32
    r = np.arange(P)
    square = np.concatenate([np.eye(P), np.where(r[None, :] > r[:, None], MASKED, 0.0),
                             np.where(r[None, :] < r[:, None], MASKED, 0.0), np.ones((P, P)),
                             (r[:, None] < r[None, :]) * 1.0], axis=1).astype(f)
    away = r[:, None] + PAD_L - np.arange(BAND)[None, :]
    band = np.where(np.isin(away, SHIFTS), 0.0, MASKED).astype(f)
    iota = np.stack([np.broadcast_to(np.arange(E0), (P, E0)), np.broadcast_to(np.arange(E0) * CAP, (P, E0))], axis=1).astype(f)
    of_head = (np.arange(D)[None, :] // HD == np.arange(H)[:, None]).astype(f)
    sel = (np.eye(NT, dtype=f)[None, :, :, None] * of_head[:, None, None, :]).reshape(P, NT, C, P)
    rd = HD // 2
    perm = np.zeros((P, P), f)
    for h in range(H):
        for j in range(rd // 2):
            perm[h * rd + rd // 2 + j, h * rd + j] = -1.0
            perm[h * rd + j, h * rd + rd // 2 + j] = 1.0
    inv = (1.0 / f(10000.0) ** (np.arange(0, rd, 2, dtype=f) / f(rd))).astype(f)
    ang = np.outer(np.arange(T, dtype=f), inv).astype(f)
    row = np.arange(P) % (rd // 2)
    roll = np.stack([np.roll(np.eye(P), s, axis=1) for s in ROLLS], axis=1).astype(f)
    return {"c_square": square, "c_band": band, "c_iota": np.ascontiguousarray(iota), "c_sel": sel, "c_perm": perm,
            "c_cos": np.cos(ang).T[row].astype(f), "c_sin": np.sin(ang).T[row].astype(f), "c_roll": roll}


def lay_out(a):
    g = {n: np.asarray(v) for n, v in a.items()}
    cut = lambda w: w.reshape(-1, P, w.shape[-1]).transpose(1, 0, 2)
    col = lambda b: b.reshape(-1, P).T
    o = {"x": g["L0_attn_a_x"].reshape(T, D)}
    p = "L0_attn_a_"
    o["mha_w"] = cut(np.concatenate([g[p + n].transpose(1, 0, 2).reshape(D, D) for n in ("Wq", "Wk", "Wv")], axis=1))
    o["mha_bqk"] = np.concatenate([col(g[p + "bq"].reshape(-1)), col(g[p + "bk"].reshape(-1))], axis=1)
    o["mha_bv"] = g[p + "bv"].reshape(1, D)
    o["mha_wo"], o["mha_bo"] = cut(g[p + "Wo"]), g[p + "bo"].reshape(1, D)
    p = "L1_attn_a_"
    b = g[p + "b_qkv"]
    o["mqa_w"] = cut(g[p + "w_qkv"])
    bk = np.zeros((P, 2), np.float32)
    bk[0:HD, 0] = b[D:D + HD]
    o["mqa_bqk"] = np.concatenate([col(b[0:D]), bk], axis=1)
    o["mqa_bv"] = b[D + HD:].reshape(1, HD)
    o["mqa_wo"], o["mqa_bo"] = cut(g[p + "w_fc"]), g[p + "b_fc"].reshape(1, D)
    p = "L1_ffn_"
    o["mla_down"] = cut(np.concatenate([g[p + "kv_d_w"], g[p + "q_d_w"]], axis=1))
    o["mla_rk"] = cut(g[p + "rope_k_w"])
    o["mla_lat"] = np.concatenate([g[p + n] for n in ("k_u_w", "q_u_w", "rope_q_w", "v_u_w")], axis=1)
    o["mla_wo"] = cut(g[p + "o_w"])
    o["ln1"], o["ln2"] = col(g[p + "ln1_w"]), col(g[p + "ln2_w"])
    lay_out_more(g, o, cut, col)
    return {n: np.ascontiguousarray(v) for n, v in o.items()}


def lay_out_more(g, o, cut, col):
    p = "L0_ffn_"
    o["moe_router"] = cut(g[p + "wg_router"].T)
    gu = np.stack([g[p + "w_gate"], g[p + "w_up"]], axis=1)
    o["expert_w_in"] = gu.reshape(E0, 2, C, P, F0).transpose(0, 3, 1, 2, 4).reshape(E0 * P, 2 * C * F0)
    o["expert_w_out"] = g[p + "w_down"].reshape(E0, 2, FH, D).transpose(0, 2, 1, 3).reshape(E0 * FH, 2 * D)
    gu = np.stack([g[p + "ws_gate"], g[p + "ws_up"]])
    o["shared_in"] = gu.reshape(2, C, P, FS).transpose(2, 0, 1, 3)
    o["shared_out"] = g[p + "ws_down"].reshape(NS, FH, D).transpose(1, 0, 2)
    p = "L0_attn_b_"
    head = lambda w: w.reshape(H, D2, C, P).transpose(0, 3, 2, 1)
    o["shifted_w_qk"] = np.stack([head(g[p + "wq"]), head(g[p + "wk"])], axis=2).reshape(H * P, 2 * C * P)
    o["shifted_bg"] = np.stack([np.stack([col(g[p + b]), col(g[p + n])], axis=1) for b, n in (("bq", "gq"), ("bk", "gk"))], axis=1)
    o["shifted_mix"] = g[p + "w_mix"]
    o["shifted_w_v"] = head(g[p + "wv"]).reshape(H * P, C * P)
    o["shifted_wo"] = g[p + "wo"].T
    o["shifted_bv"], o["shifted_bo"] = col(g[p + "bv"]), g[p + "bo"].reshape(1, D)
    p = "L1_attn_b_"
    w, b = g[p + "Wqkv_w"], g[p + "Wqkv_b"]
    qw, kw, vw = (x.reshape(4, -1, D) for x in (w[0:2048], w[2048:3072], w[3072:4096]))
    qb, kb, vb = (x.reshape(4, -1) for x in (b[0:2048], b[2048:3072], b[3072:4096]))
    ww = np.concatenate([qw, kw, vw], axis=1).reshape(4, -1, C, P).transpose(0, 3, 2, 1).reshape(4, P, -1)
    bb = np.concatenate([qb, kb], axis=1).reshape(4, -1, P).transpose(0, 2, 1)
    o["diff_w"] = np.concatenate([ww, bb], axis=2).reshape(4 * P, -1)
    o["diff_bv"] = vb
    o["diff_wo"] = g[p + "out_w"].T.reshape(4, 4, P, D).transpose(0, 2, 1, 3).reshape(4 * P, 4 * D)
    o["diff_bo"], o["diff_sub"] = g[p + "out_b"].reshape(1, D), col(g[p + "subln_w"])
    o["diff_lambda"] = np.stack([g[p + n] for n in ("lambda_q1", "lambda_k1", "lambda_q2", "lambda_k2")])
    p = "L1_ffn_"
    o["gate_router"], o["gate_bias"] = cut(g[p + "router_w"]), g[p + "router_b"].reshape(1, E1 - 1)
    gate = np.concatenate([g[p + "sh_gate"][None], g[p + "r_gate"]])
    up = np.concatenate([g[p + "sh_up"][None], g[p + "r_up"]])
    down = np.concatenate([g[p + "sh_down"][None], g[p + "r_down"]])
    o["dense_w_in"] = np.stack([gate, up], axis=1).reshape(E1, 2, C, P, I1).transpose(0, 3, 1, 2, 4).reshape(E1 * P, 2 * C * I1)
    o["dense_w_out"] = down.reshape(E1 * I1, D)


SCRATCH = {"q_parts": ([3, HD, H, T], BF16), "k_parts": ([3, HD, H, T], BF16), "head_out": ([D, T], F32), "head_sum": ([H, T], F32),
           "expert_in": ([SLOTS, D], F32), "expert_out": ([SLOTS, D], F32)}


def kernel(**inputs):
    import concourse.bacc as bacc
    from concourse.bass_utils import run_bass_kernel_spmd

    nc = bacc.Bacc("TRN2", target_bir_lowering=False, num_devices=1)
    arrays = {**lay_out(inputs), **constant_arrays()}
    dram = {n: nc.dram_tensor(f"in_{n}", a.shape, mybir.dt.from_np(a.dtype), kind="ExternalInput").ap() for n, a in arrays.items()}
    for name, (shape, dt) in SCRATCH.items():
        dram[name] = nc.dram_tensor(f"scratch_{name}", shape, dt, kind="Internal").ap()
    out = nc.dram_tensor("out_x", [T, D], F32, kind="ExternalOutput").ap()
    program(nc, dram, out, SEQUENCE)
    r = run_bass_kernel_spmd(nc, [{f"in_{n}": a for n, a in arrays.items()}], core_ids=[0])
    return r.results[0]["out_x"].reshape(1, T, D)


SEQUENCE = ["mha", "moe", "shifted", "moe", "mqa", "mla", "differential", "mla"]
```
